# Optimizing a Trainium2 kernel written in Bass

```python
import numpy as np
import jax
import jax.numpy as jnp

def _softmax(x, axis=-1):
    return jax.nn.softmax(x, axis=axis)

def _gelu(x):
    return jax.nn.gelu(x, approximate=True)

def _silu(x):
    return jax.nn.silu(x)

def _sigmoid(x):
    return jax.nn.sigmoid(x)

def _layernorm(x, axis=-1, eps=1e-05):
    m = jnp.mean(x, axis=axis, keepdims=True)
    v = jnp.var(x, axis=axis, keepdims=True)
    return (x - m) / jnp.sqrt(v + eps)

def _scatter_add(tgt, idx, src, axis=0):
    return tgt.at[idx].add(src)

def _segment_sum(src, seg, n):
    return jax.ops.segment_sum(src, seg, n)
kernel_name = 'mk_gnn_resnorm_d4_gnn_r64_e3e996'

def setup_inputs(seed: int=0):
    np.random.seed(seed)
    _w = jnp.asarray

    def _rec_inputs():
        import jax
        import jax.numpy as jnp
        _gk = jax.random.key(seed)
        x = -0.0004402 + 1 * jax.random.normal(jax.random.fold_in(_gk, 1), (100000, 16), jnp.float32)
        src = jax.random.randint(jax.random.fold_in(_gk, 2), (50000,), 0, 100000, jnp.int32)
        dst = jnp.minimum((100000 * jax.random.uniform(jax.random.fold_in(_gk, 3), (50000,)) ** 2.0).astype(jnp.int32), 99999)
        _o = jnp.argsort(dst, stable=True)
        src = src[_o]
        dst = dst[_o]
        edge_attr_16 = -3.57403e-05 + 0.999761 * jax.random.normal(jax.random.fold_in(_gk, 12), (50000, 16), jnp.float32)
        edge_type_8 = jax.random.randint(jax.random.fold_in(_gk, 14), (50000,), 0, 8, jnp.int32)
        return (x, src, dst, edge_attr_16, edge_type_8)
    x, src, dst, edge_attr_16, edge_type_8 = _rec_inputs()

    def _L0_gnn_setup():
        import jax, jax.numpy as jnp
        import numpy as np
        N_NODES = 30000
        N_EDGES = 300000
        IN_FEATS = 16
        OUT_FEATS = 16
        EDGE_DIM = 16
        key = jax.random.key(seed)
        ks = jax.random.split(key, 8)
        feat = jax.random.normal(ks[0], (N_NODES, IN_FEATS), dtype=jnp.float32)
        efeat = jax.random.normal(ks[1], (N_EDGES, EDGE_DIM), dtype=jnp.float32)
        W_msg = jax.random.normal(ks[2], (EDGE_DIM, IN_FEATS * OUT_FEATS), dtype=jnp.float32) * 0.1
        b_msg = jnp.zeros((IN_FEATS * OUT_FEATS,), dtype=jnp.float32)
        W_attn = jax.random.normal(ks[3], (EDGE_DIM, IN_FEATS * OUT_FEATS), dtype=jnp.float32) * 0.1
        b_attn = jnp.zeros((IN_FEATS * OUT_FEATS,), dtype=jnp.float32)
        src = jax.random.randint(ks[4], (N_EDGES,), 0, N_NODES, dtype=jnp.int32)
        dst = jax.random.randint(ks[5], (N_EDGES,), 0, N_NODES, dtype=jnp.int32)
        return {'feat': feat, 'efeat': efeat, 'W_msg': W_msg, 'b_msg': b_msg, 'W_attn': W_attn, 'b_attn': b_attn, 'src': src, 'dst': dst}
    _L0_gnn_all = _L0_gnn_setup()
    _L0_gnn_in = {k: v for k, v in _L0_gnn_all.items() if k in ('W_msg', 'b_msg', 'W_attn', 'b_attn')}
    del _L0_gnn_all

    def _L1_gnn_setup():
        import jax, jax.numpy as jnp
        import numpy as np
        N_NODES = 50000
        N_EDGES = 12500
        D = 16
        key = jax.random.key(seed)
        k1, k2, k3, k4 = jax.random.split(key, 4)
        x = jax.random.normal(k1, (N_NODES, D), dtype=jnp.float32)
        edge_index = jax.random.randint(k2, (2, N_EDGES), 0, N_NODES, dtype=jnp.int64)
        W_tp = jax.random.normal(k3, (D, D, D), dtype=jnp.float32) * (1.0 / D)
        weight = jax.random.normal(k4, (D, D), dtype=jnp.float32) * 0.01
        bias = jnp.zeros((D,), dtype=jnp.float32)
        return {'x': x, 'edge_index': edge_index, 'W_tp': W_tp, 'weight': weight, 'bias': bias}
    _L1_gnn_all = _L1_gnn_setup()
    _L1_gnn_in = {k: v for k, v in _L1_gnn_all.items() if k in ('W_tp', 'weight', 'bias')}
    del _L1_gnn_all

    def _L2_gnn_setup():
        import jax, jax.numpy as jnp
        import numpy as np
        N_NODES = 3125
        N_EDGES = 50000
        F_IN = 16
        N_CLASSES = 16

        def _gin_conv(x, src, dst, eps, wa, ba, wb, bb, n_nodes):
            agg = jax.ops.segment_sum(x[src], dst, num_segments=n_nodes)
            h = (1.0 + eps) * x + agg
            h = jax.nn.relu(h @ wa + ba) @ wb + bb
            return h
        key = jax.random.key(seed)
        ks = jax.random.split(key, 8)
        s = 1.0 / np.sqrt(F_IN)
        return {'x': jax.random.normal(ks[0], (N_NODES, F_IN), dtype=jnp.float32), 'edge_index': jax.random.randint(ks[1], (2, N_EDGES), 0, N_NODES, dtype=jnp.int32), 'eps1': jnp.zeros((), dtype=jnp.float32), 'w1a': jax.random.normal(ks[2], (F_IN, 16), dtype=jnp.float32) * s, 'b1a': jnp.zeros((16,), dtype=jnp.float32), 'w1b': jax.random.normal(ks[3], (16, 16), dtype=jnp.float32) * 0.25, 'b1b': jnp.zeros((16,), dtype=jnp.float32), 'eps2': jnp.zeros((), dtype=jnp.float32), 'w2a': jax.random.normal(ks[4], (16, N_CLASSES), dtype=jnp.float32) * 0.25, 'b2a': jnp.zeros((N_CLASSES,), dtype=jnp.float32), 'w2b': jax.random.normal(ks[5], (N_CLASSES, N_CLASSES), dtype=jnp.float32) * 0.25, 'b2b': jnp.zeros((N_CLASSES,), dtype=jnp.float32)}
    _L2_gnn_all = _L2_gnn_setup()
    _L2_gnn_in = {k: v for k, v in _L2_gnn_all.items() if k in ('eps1', 'w1a', 'b1a', 'w1b', 'b1b', 'eps2', 'w2a', 'b2a', 'w2b', 'b2b')}
    del _L2_gnn_all

    def _L3_gnn_setup():
        import jax, jax.numpy as jnp
        import numpy as np
        N_NODES = 100000
        N_EDGES = 15625
        MSG_DIM = 16
        HID_DIM = 16
        N_EDGE_TYPE = 8
        key = jax.random.key(seed)
        ks = jax.random.split(key, 9)
        features = jax.random.normal(ks[0], (N_NODES, HID_DIM), dtype=jnp.float32)
        edge_src = jax.random.randint(ks[1], (N_EDGES,), 0, N_NODES, dtype=jnp.int32)
        edge_dst = jax.random.randint(ks[2], (N_EDGES,), 0, N_NODES, dtype=jnp.int32)
        edge_type = jax.random.randint(ks[3], (N_EDGES,), 0, N_EDGE_TYPE, dtype=jnp.int32)
        edge_emb = jax.random.normal(ks[4], (N_EDGE_TYPE, MSG_DIM * HID_DIM), dtype=jnp.float32) * 0.1
        s = 1.0 / np.sqrt(HID_DIM)
        w_ih = jax.random.uniform(ks[5], (3 * HID_DIM, MSG_DIM), minval=-s, maxval=s, dtype=jnp.float32)
        w_hh = jax.random.uniform(ks[6], (3 * HID_DIM, HID_DIM), minval=-s, maxval=s, dtype=jnp.float32)
        b_ih = jax.random.uniform(ks[7], (3 * HID_DIM,), minval=-s, maxval=s, dtype=jnp.float32)
        b_hh = jax.random.uniform(ks[8], (3 * HID_DIM,), minval=-s, maxval=s, dtype=jnp.float32)
        return {'features': features, 'edge_src': edge_src, 'edge_dst': edge_dst, 'edge_type': edge_type, 'edge_emb': edge_emb, 'w_ih': w_ih, 'w_hh': w_hh, 'b_ih': b_ih, 'b_hh': b_hh}
    _L3_gnn_all = _L3_gnn_setup()
    _L3_gnn_in = {k: v for k, v in _L3_gnn_all.items() if k in ('edge_emb', 'w_ih', 'w_hh', 'b_ih', 'b_hh')}
    del _L3_gnn_all
    return {'x': x, 'src': src, 'dst': dst, 'edge_attr_16': edge_attr_16, 'edge_type_8': edge_type_8, 'L0_gnn_W_msg': _L0_gnn_in['W_msg'], 'L0_gnn_b_msg': _L0_gnn_in['b_msg'], 'L0_gnn_W_attn': _L0_gnn_in['W_attn'], 'L0_gnn_b_attn': _L0_gnn_in['b_attn'], 'L1_gnn_W_tp': _L1_gnn_in['W_tp'], 'L1_gnn_weight': _L1_gnn_in['weight'], 'L1_gnn_bias': _L1_gnn_in['bias'], 'L2_gnn_eps1': _L2_gnn_in['eps1'], 'L2_gnn_w1a': _L2_gnn_in['w1a'], 'L2_gnn_b1a': _L2_gnn_in['b1a'], 'L2_gnn_w1b': _L2_gnn_in['w1b'], 'L2_gnn_b1b': _L2_gnn_in['b1b'], 'L2_gnn_eps2': _L2_gnn_in['eps2'], 'L2_gnn_w2a': _L2_gnn_in['w2a'], 'L2_gnn_b2a': _L2_gnn_in['b2a'], 'L2_gnn_w2b': _L2_gnn_in['w2b'], 'L2_gnn_b2b': _L2_gnn_in['b2b'], 'L3_gnn_edge_emb': _L3_gnn_in['edge_emb'], 'L3_gnn_w_ih': _L3_gnn_in['w_ih'], 'L3_gnn_w_hh': _L3_gnn_in['w_hh'], 'L3_gnn_b_ih': _L3_gnn_in['b_ih'], 'L3_gnn_b_hh': _L3_gnn_in['b_hh']}

def reference(x, src, dst, edge_attr_16, edge_type_8, L0_gnn_W_msg, L0_gnn_b_msg, L0_gnn_W_attn, L0_gnn_b_attn, L1_gnn_W_tp, L1_gnn_weight, L1_gnn_bias, L2_gnn_eps1, L2_gnn_w1a, L2_gnn_b1a, L2_gnn_w1b, L2_gnn_b1b, L2_gnn_eps2, L2_gnn_w2a, L2_gnn_b2a, L2_gnn_w2b, L2_gnn_b2b, L3_gnn_edge_emb, L3_gnn_w_ih, L3_gnn_w_hh, L3_gnn_b_ih, L3_gnn_b_hh):
    import jax
    import jax.numpy as jnp

    def _L0_gnn_ref(feat, efeat, W_msg, b_msg, W_attn, b_attn, src, dst):
        import jax, jax.numpy as jnp
        import numpy as np
        N_NODES = 30000
        N_EDGES = 300000
        IN_FEATS = 16
        OUT_FEATS = 16
        EDGE_DIM = 16
        N, in_f = feat.shape
        E = efeat.shape[0]
        w_m = (efeat @ W_msg + b_msg).reshape(E, in_f, -1)
        w_a = (efeat @ W_attn + b_attn).reshape(E, in_f, -1)
        h_src = feat[src][:, :, None]
        e1 = w_m * h_src
        e2 = w_a * h_src
        seg_max = jax.ops.segment_max(e2, dst, num_segments=N)
        ex = jnp.exp(e2 - seg_max[dst])
        denom = jax.ops.segment_sum(ex, dst, num_segments=N)
        attn = ex / denom[dst]
        ft = jax.ops.segment_sum(e1 * attn, dst, num_segments=N)
        return ft.sum(axis=1)

    def _L1_gnn_ref(x, edge_index, W_tp, weight, bias):
        import jax, jax.numpy as jnp
        import numpy as np
        N_NODES = 50000
        N_EDGES = 12500
        D = 16
        row, col = (edge_index[0], edge_index[1])
        xr = x[row]
        xc = x[col]
        messages = jnp.einsum('eu,ev,uvw->ew', xr, xc, W_tp)
        out = jnp.zeros((x.shape[0], D), dtype=x.dtype).at[row].add(messages)
        return out @ weight.T + bias

    def _L2_gnn_ref(x, edge_index, eps1, w1a, b1a, w1b, b1b, eps2, w2a, b2a, w2b, b2b):
        import jax, jax.numpy as jnp
        import numpy as np
        N_NODES = 3125
        N_EDGES = 50000
        F_IN = 16
        N_CLASSES = 16

        def _gin_conv(x, src, dst, eps, wa, ba, wb, bb, n_nodes):
            agg = jax.ops.segment_sum(x[src], dst, num_segments=n_nodes)
            h = (1.0 + eps) * x + agg
            h = jax.nn.relu(h @ wa + ba) @ wb + bb
            return h
        src, dst = (edge_index[0], edge_index[1])
        n = x.shape[0]
        h = jax.nn.relu(_gin_conv(x, src, dst, eps1, w1a, b1a, w1b, b1b, n))
        h = _gin_conv(h, src, dst, eps2, w2a, b2a, w2b, b2b, n)
        return jax.nn.log_softmax(h, axis=1)

    def _L3_gnn_ref(features, edge_src, edge_dst, edge_type, edge_emb, w_ih, w_hh, b_ih, b_hh):
        import jax, jax.numpy as jnp
        import numpy as np
        N_NODES = 100000
        N_EDGES = 15625
        MSG_DIM = 16
        HID_DIM = 16
        N_EDGE_TYPE = 8
        n_nodes = features.shape[0]
        A = edge_emb[edge_type].reshape(-1, MSG_DIM, HID_DIM)
        h_src = features[edge_src]
        msg = jnp.einsum('emh,eh->em', A, h_src)
        m = jax.ops.segment_sum(msg, edge_dst, num_segments=n_nodes)
        gi = m @ w_ih.T + b_ih
        gh = features @ w_hh.T + b_hh
        i_r, i_z, i_n = jnp.split(gi, 3, axis=-1)
        h_r, h_z, h_n = jnp.split(gh, 3, axis=-1)
        r = jax.nn.sigmoid(i_r + h_r)
        z = jax.nn.sigmoid(i_z + h_z)
        n = jnp.tanh(i_n + r * h_n)
        h_new = (1.0 - z) * n + z * features
        return h_new
    edge_index = jnp.stack([src, dst])
    x = _layernorm(x + _L0_gnn_ref(x, edge_attr_16, L0_gnn_W_msg, L0_gnn_b_msg, L0_gnn_W_attn, L0_gnn_b_attn, src, dst), axis=-1)
    x = _layernorm(x + _L1_gnn_ref(x, edge_index, L1_gnn_W_tp, L1_gnn_weight, L1_gnn_bias), axis=-1)
    x = _layernorm(x + _L2_gnn_ref(x, edge_index, L2_gnn_eps1, L2_gnn_w1a, L2_gnn_b1a, L2_gnn_w1b, L2_gnn_b1b, L2_gnn_eps2, L2_gnn_w2a, L2_gnn_b2a, L2_gnn_w2b, L2_gnn_b2b), axis=-1)
    x = _layernorm(x + _L3_gnn_ref(x, src, dst, edge_type_8, L3_gnn_edge_emb, L3_gnn_w_ih, L3_gnn_w_hh, L3_gnn_b_ih, L3_gnn_b_hh), axis=-1)
    return x

_drawn_inputs = setup_inputs


def setup_inputs(seed=0):
    import zlib

    import numpy as np

    out = dict(_drawn_inputs(seed))
    spreads = {'L0_gnn_b_msg': (0.0, 0.1),
     'L0_gnn_b_attn': (0.0, 0.547),
     'L1_gnn_bias': (0.0, 0.1),
     'L2_gnn_b1a': (0.0, 0.277),
     'L2_gnn_b1b': (0.0, 0.1),
     'L2_gnn_b2a': (0.0, 0.1),
     'L2_gnn_b2b': (0.0, 0.1)}
    factors = {}
    for name, (base, spread) in spreads.items():
        noise = np.random.default_rng([zlib.crc32(name.encode()), seed]).standard_normal(out[name].shape)
        drawn = base * np.exp(spread * noise) if base else spread * noise
        out[name] = jnp.asarray(drawn.astype(out[name].dtype))
    for name, factor in factors.items():
        out[name] = (out[name] * factor).astype(out[name].dtype)
    return out
```

```python
from contextlib import ExitStack

import concourse.bass as bass
from concourse import mybir

FP32 = mybir.dt.float32
I32 = mybir.dt.int32
U32 = mybir.dt.uint32
ALU = mybir.AluOpType
ACT = mybir.ActivationFunctionType
AX = mybir.AxisListType.X

P = 128
F = 16
N_NODES = 100000
N_EDGES = 50000
TYPES = 8

SLOTS = 56
NODE_TILE = P * SLOTS
NODE_TILES = -(-N_NODES // NODE_TILE)
NP = NODE_TILES * NODE_TILE
PACK = P // F
PACKS = SLOTS // PACK
W = SLOTS * F

ET = 512
TILES = -(-N_EDGES // ET)
EP = TILES * ET
SUB = ET // P
CH = 2

GJ = 7
G = GJ * P
GROUPS = EP // G
PASSES = 4
COLS = EP // P

LOOP_FROM, LOOP_TO, DEPTH = 6, TILES - 2, 5
CLEARS = (LOOP_TO - LOOP_FROM) // 2
CLEAR_SLOTS = -(-PASSES * (NP + G) // (CLEARS * P))
CLEAR_ROWS = CLEAR_SLOTS * P

EPS = 1e-5
FAR = -1e30

C_ID, C_TRI, C_BLK, C_TRASH, C_IOTA, C_SELO = 0, 128, 128 + G, 136 + G, 136 + G + GJ, 144 + G + GJ
C_N = C_SELO + F
A_BTP, A_B1B, A_B2B, A_BIH, A_BHH = 0, 16, 32, 48, 96
A_B1A, A_B2A, A_EPS1, A_EPS2 = 144, 145, 146, 147
A_W1A, A_W1B, A_W2A, A_W2B, A_WIH, A_WHH, A_EMB = 148, 164, 180, 196, 212, 260, 308
A_N = 324


def build_program(nc, x, ef, wlog, src_t, dst_t, next_t, type_t, src_row, dst_row, prev_row,
                  const, par, par16, out):
    assert EP % G == 0 and GROUPS % 2 == 0 and TILES % 2 == 0 and NODE_TILES % 2 == 0
    ctx = ExitStack()
    with ctx:
        def sb(name, shape, dt=FP32):
            return ctx.enter_context(nc.sbuf_tensor(name, shape, dt))

        def sem(name):
            return ctx.enter_context(nc.semaphore(name))

        def pair(name):
            return [sem(name + "0"), sem(name + "1")]

        def dram(name, shape, dt=FP32):
            return nc.dram_tensor(name, shape, dt).ap()

        x1_t, x2_t, h_t, x3_t = (dram(n, [NP, F]) for n in ("x1_t", "x2_t", "h_t", "x3_t"))
        ft_t = dram("ft_t", [NP + EP, F])
        sums_all = dram("sums_all", [CLEARS * CLEAR_ROWS, F])
        sums_t = [sums_all[k * (NP + G):(k + 1) * (NP + G), :] for k in range(PASSES)]
        far_row = dram("far_row", [EP])
        ftidx_t = dram("ftidx_t", [P, COLS], I32)

        cst = sb("cst", [P, C_N])
        prm = sb("prm", [P, A_N])
        prm16 = sb("prm16", [F, F + F * P + CH * P])
        ident = cst[:, C_ID:C_ID + P]
        selo = cst[:, C_SELO:C_SELO + F]
        repsel = prm16[:, F + F * P:F + F * P + CH * P]
        zero = sb("zero", [P, CLEAR_SLOTS * F])
        wl = sb("wl", [F + 1, 2 * CH * P])

        ka = sb("ka", [P, COLS], I32)
        kb = sb("kb", [P, COLS], I32)
        kt = sb("kt", [P, COLS])
        kt2 = sb("kt2", [P, COLS])
        kspare = sb("kspare", [P, COLS], I32)
        kd = sb("kd", [P, COLS])
        ko = sb("ko", [P, COLS], I32)

        eft = [sb(f"eft{b}", [F + 1, ET]) for b in range(2)]
        far = [sb(f"far{b}", [P, ET]) for b in range(2)]
        xidx = [sb(f"xidx{b}", [P, SUB], I32) for b in range(2)]
        fidx = [sb(f"fidx{b}", [P, SUB], I32) for b in range(2)]
        xg = [sb(f"xg{b}", [P, SUB, F]) for b in range(2)]
        xT = sb("xT", [F, ET])
        hS = sb("hS", [P, CH, ET])
        e2 = sb("e2", [P, CH, ET])
        e1 = [sb(f"e1_{b}", [P, CH, ET]) for b in range(2)]
        mx = [sb(f"mx{b}", [P, CH, ET + 1]) for b in range(2)]
        mfar = sb("mfar", [P, CH, ET])
        uu = [sb(f"uu{b}", [P, CH, ET]) for b in range(2)]
        dd = [sb(f"dd{b}", [P, CH, ET]) for b in range(2)]
        qq = sb("qq", [P, CH, ET])
        den = [sb(f"den{b}", [P, CH, ET]) for b in range(2)]
        num = [sb(f"num{b}", [P, CH, ET]) for b in range(2)]
        lnd = sb("lnd", [P, CH, ET])
        inv = sb("inv", [P, CH, ET])
        rat = [sb(f"rat{b}", [P, CH, ET]) for b in range(2)]
        fts = [sb(f"fts{b}", [P, SUB * F]) for b in range(2)]

        gidx = [sb(f"gidx{b}", [P, GJ], I32) for b in range(2)]
        krow = [sb(f"krow{b}", [P, G], I32) for b in range(2)]
        kcol = [sb(f"kcol{b}", [P, GJ], I32) for b in range(2)]
        tcol = [sb(f"tcol{b}", [P, GJ], I32) for b in range(2)]
        kcf = [sb(f"kcf{b}", [P, GJ]) for b in range(2)]
        tcf = [sb(f"tcf{b}", [P, GJ]) for b in range(2)]
        EQ0 = [P * (J * (J + 1) // 2) for J in range(GJ + 1)]
        eqm = [sb(f"eqm{b}", [P, EQ0[GJ]]) for b in range(2)]
        cnt = [sb(f"cnt{b}", [P, GJ]) for b in range(2)]
        kdf = sb("kdf", [P, GJ])
        kmd = sb("kmd", [P, GJ])
        sidx = [sb(f"sidx{b}", [P, GJ], I32) for b in range(2)]
        yg = [sb(f"yg{b}", [P, GJ, F]) for b in range(2)]
        cmb = [sb(f"cmb{b}", [P, GJ, F]) for b in range(2)]

        xin = [sb(f"xin{b}", [P, W]) for b in range(2)]
        ain = [sb(f"ain{b}", [P, W]) for b in range(2)]
        yout = [sb(f"yout{b}", [P, W]) for b in range(2)]
        vv = sb("vv", [P, W])
        xm = sb("xm", [P, W])
        st = sb("st", [P, 6, SLOTS])

        wbk = [sb(f"wb{k}", [P, 4 * F * F]) for k in range(2)]
        bd = [sb(f"bd{k}", [P, P]) for k in range(4)]
        bdg = [sb(f"bdg{k}", [P, 4 * P]) for k in range(2)]
        bgate = sb("bgate", [P, 4, F])
        flat = lambda t: t[:, :, :].rearrange("p a b -> p (a b)")
        e2f = flat(e2)
        rin = [e2f[:, 0:W], flat(mx[0])[:, 0:W]]
        sq = flat(mx[1])[:, 0:W]
        sT = [flat(qq)[:, 0:P], flat(qq)[:, P:2 * P]]
        prod = [flat(lnd)[:, 0:512], flat(lnd)[:, 512:1024]]
        zz = flat(inv)[:, 0:W]
        yy = flat(hS)[:, 0:W]
        yT = flat(mfar)[:, 0:W]
        hT = flat(rat[0])[:, 0:W]
        mT = flat(rat[1])[:, 0:W]
        gates = [flat(t)[:, 0:W] for t in (dd[0], dd[1], uu[1], den[0])]
        rh = flat(den[1])[:, 0:W]
        nn = flat(num[0])[:, 0:W]
        zx = flat(num[1])[:, 0:W]
        ex = flat(e1[0])[:, 0:W]
        zc = flat(e1[1])[:, 0:W]
        zt = [flat(qq)[:, 0:W], flat(lnd)[:, 0:W]]
        ztT = [flat(inv)[:, 0:W], flat(hS)[:, 0:W]]
        ym = [flat(mfar)[:, 0:GJ * F], flat(mfar)[:, 512:512 + GJ * F]]

        ps = [ctx.enter_context(nc.psum_tensor(f"ps{k}", [P, 1024], FP32)) for k in range(4)]

        block = ctx.enter_context(nc.Block())

        cst_in, keys_in, zero_made, first_made, spare_made = (
            sem(n) for n in ("cst_in", "keys_in", "zero_made", "first_made", "spare_made"))
        ft_zero, sums_zero = sem("ft_zero"), sem("sums_zero")
        k_same, k_far, k_d, k_m, k_idx = (sem(n) for n in ("k_same", "k_far", "k_d", "k_m", "k_idx"))
        far_out, ftidx_out, next_in = sem("far_out"), sem("ftidx_out"), sem("next_in")
        w_tp, w_made, w_bias = sem("w_tp"), sem("w_made"), sem("w_bias")

        main_in, xidx_in, fidx_in, x_gathered = pair("main_in"), pair("xidx_in"), pair("fidx_in"), pair("x_gathered")
        xT_ps, xT_sb, h_ps, h_sb, wa_ps, wm_ps = (sem(n) for n in ("xT_ps", "xT_sb", "h_ps", "h_sb", "wa_ps", "wm_ps"))
        e2_done, m_first, m_done, e1_done, u_done, mfar_done, d_done = (
            sem(n) for n in ("e2_done", "m_first", "m_done", "e1_done", "u_done", "mfar_done", "d_done"))
        p_done, c_done, q_done, den_done, num_done, ln_done, inv_done, rat_done = (
            sem(n) for n in ("p_done", "c_done", "q_done", "den_done", "num_done", "ln_done", "inv_done", "rat_done"))
        ft_ps, ft_sb = sem("ft_ps"), sem("ft_sb")
        ft_scattered = pair("ft_scattered")

        sum_in, type_in, y_gathered = pair("sum_in"), pair("type_in"), pair("y_gathered")
        kcf_done, eq_done, kdf_done, kmd_done, sidx_done, comb_ps, comb_sb, added = (
            sem(n) for n in ("kcf_done", "eq_done", "kdf_done", "kmd_done", "sidx_done", "comb_ps", "comb_sb", "added"))
        tcf_done, zt_done, ztT_ps, ztT_sb, ym_ps, ym_sb = (
            sem(n) for n in ("tcf_done", "zt_done", "ztT_ps", "ztT_sb", "ym_ps", "ym_sb"))

        node_in, stored = pair("node_in"), pair("stored")
        v_done, s_sum, s_xm, s_sq, s_vs, s_ve, s_sd, s_rs, y_done = (
            sem(n) for n in ("v_done", "s_sum", "s_xm", "s_sq", "s_vs", "s_ve", "s_sd", "s_rs", "y_done"))
        b_tps, b_tsb, b_ps, b_prod, b_z, b_zb = (sem(n) for n in ("b_tps", "b_tsb", "b_ps", "b_prod", "b_z", "b_zb"))
        g_y, g_tps, g_tsb, g_hps, g_hsb, g_ops, g_o = (
            sem(n) for n in ("g_y", "g_tps", "g_tsb", "g_hps", "g_hsb", "g_ops", "g_o"))
        l_max, l_zc, l_ex, l_se, l_ln, l_t = (sem(n) for n in ("l_max", "l_zc", "l_ex", "l_se", "l_ln", "l_t"))
        u_tps, u_tsb, u_ps, u_g, u_sig, u_rh, u_in, u_n, u_zx, u_zd = (
            sem(n) for n in ("u_tps", "u_tsb", "u_ps", "u_g", "u_sig", "u_rh", "u_in", "u_n", "u_zx", "u_zd"))

        def static(i):
            return isinstance(i, int)

        def inside(i, c, n):
            return not static(i) or 0 <= 2 * i + c < n

        def later(i, c, least=0):
            return not static(i) or 2 * i + c >= least

        def nth(i, c):
            return i + c // 2

        def steps(eng, step, first, loop_from, loop_to, last):
            for t in range(first, loop_from):
                step(0, t)
            with eng.Fori(loop_from // 2, loop_to // 2) as i:
                step(i, 0)
                step(i, 1)
            for t in range(loop_to, last):
                step(0, t)

        NODE_HALF = NODE_TILES // 2

        def softmax_steps(eng, step):
            steps(eng, step, 0, LOOP_FROM, LOOP_TO, TILES + DEPTH)

        def group_steps(eng, step):
            steps(eng, step, 0, 2, GROUPS - 2, GROUPS)

        def ntile(t):
            return bass.ds(t * NODE_TILE, NODE_TILE)

        def rows(table, i, c):
            return table[ntile(2 * i + c), :].rearrange("(p k) f -> p (k f)", p=P)

        def n_par(c, g):
            return (c * PACKS + g) % 2

        NODE_PHASES = 5
        node_loads = [[x, ft_t], [x1_t, sums_t[0]], [x2_t, sums_t[1]], [h_t, sums_t[2], x2_t], [x3_t, sums_t[3]]]
        node_store = [x1_t, x2_t, h_t, x3_t, out]
        loads_before = [sum(len(n) for n in node_loads[:k]) * NODE_HALF for k in range(NODE_PHASES + 1)]

        def node_count(ph, i, c):
            return NODE_TILES * ph + 2 * i + c

        def wait_loaded(eng, ph, i, c):
            eng.wait_ge(node_in[c], 16 * loads_before[ph] + 16 * len(node_loads[ph]) * (i + 1))

        @block.sync
        def _(sp):
            def wait(sem_, value):
                sp.wait_ge(sem_, value)
                if not static(value):
                    sp.nop(nofuse=True)

            sp.dma_start(cst[:, :], const).then_inc(cst_in, 16)
            sp.dma_start(prm[:, :], par).then_inc(cst_in, 16)
            sp.dma_start(prm16[:, :], par16).then_inc(cst_in, 16)
            sp.dma_start(wl[:, :], wlog).then_inc(cst_in, 16)
            sp.dma_start(ka[:, :], dst_row.rearrange("(p c) -> p c", p=P)).then_inc(keys_in, 16)
            sp.dma_start(kb[:, :], prev_row.rearrange("(p c) -> p c", p=P)).then_inc(keys_in, 16)
            wait(zero_made, 1)
            for t in range(NODE_TILES):
                sp.dma_start(rows(ft_t, 0, t), zero[:, 0:W]).then_inc(ft_zero, 16)
            wait(k_far, 1)
            sp.dma_start(far_row.rearrange("(p c) -> p c", p=P), kt[:, :]).then_inc(far_out, 16)
            wait(far_out, 16)
            sp.dma_start(ka[:, :], dst_t).then_inc(next_in, 16)
            sp.dma_start(kb[:, :], next_t).then_inc(next_in, 16)
            wait(k_idx, 1)
            sp.dma_start(ftidx_t, ko[:, :]).then_inc(ftidx_out, 16)
            wait(ftidx_out, 16)

            def load_xidx(i, c):
                if not inside(i, c, TILES):
                    return
                b = c % 2
                if later(i, c, 2):
                    wait(x_gathered[b], 16 * SUB * nth(i, c))
                sp.dma_start(xidx[b][:, :], src_t[:, bass.ds((2 * i + c) * SUB, SUB)]).then_inc(xidx_in[b], 16)

            def load_step(i, c):
                if inside(i, c, TILES):
                    b = c % 2
                    if later(i, c, 2):
                        wait(wm_ps, 2 * i + c - 1)
                        wait(mfar_done, 2 * i + c - 1)
                        wait(m_done, 2 * i + c - 1)
                    sp.dma_start(eft[b][:, :], ef[:, bass.ds((2 * i + c) * ET, ET)]).then_inc(main_in[b], 16)
                    sp.dma_start(far[b][:, :], far_row[bass.ds((2 * i + c) * ET, ET)].rearrange("(a n) -> a n", a=1)
                                 .broadcast_to((P, ET))).then_inc(main_in[b], 16)
                load_xidx(i, c + 2)
                if inside(i, c - 4, TILES):
                    b = c % 2
                    if later(i, c - 4, 2):
                        wait(ft_scattered[b], 16 * SUB * nth(i, c - 4))
                    sp.dma_start(fidx[b][:, :], ftidx_t[:, bass.ds((2 * i + c - 4) * SUB, SUB)]).then_inc(fidx_in[b], 16)
                if not static(i) and c == 0:
                    sp.dma_start(sums_all[bass.ds((i - LOOP_FROM // 2) * CLEAR_ROWS, CLEAR_ROWS), :]
                                 .rearrange("(p k) f -> p (k f)", p=P), zero[:, :]).then_inc(sums_zero, 16)

            load_xidx(0, 0)
            load_xidx(0, 1)
            softmax_steps(sp, load_step)

            def node_stage(ph):
                def load(i, c):
                    for buf, table in zip((xin, ain, rin), node_loads[ph]):
                        sp.dma_start(buf[c][:, :], rows(table, i, c)).then_inc(node_in[c], 16)

                def store(i, c):
                    wait(y_done, node_count(ph, i, c) + 1)
                    sp.dma_start(rows(node_store[ph], i, c), yout[c][:, :]).then_inc(stored[c], 16)

                load(0, 0)
                load(0, 1)
                with sp.Fori(0, NODE_HALF - 1) as i:
                    for c in range(2):
                        store(i, c)
                        wait(stored[c], i * 16 + 16 * (NODE_HALF * ph + 1))
                        load(i + 1, c)
                for c in range(2):
                    store(NODE_HALF - 1, c)
                for c in range(2):
                    wait(stored[c], 16 * NODE_HALF * (ph + 1))

            def sum_pass(k, gather_row, key_t, key_row, with_types):
                base = GROUPS * k

                def step(i, c):
                    b = c % 2
                    if later(i, c, 2) or k:
                        wait(y_gathered[b], 2 * i * 8 * GJ + 16 * GJ * (base // 2 + c // 2))
                        wait(sidx_done, base + 2 * i + c - 1)
                    cols = bass.ds((2 * i + c) * GJ, GJ)
                    sp.dma_start(gidx[b][:, :], gather_row[:, cols]).then_inc(sum_in[b], 16)
                    sp.dma_start(kcol[b][:, :], key_t[:, cols]).then_inc(sum_in[b], 16)
                    sp.dma_start(krow[b][:, :], key_row[bass.ds((2 * i + c) * G, G)].rearrange("(a n) -> a n", a=1)
                                 .broadcast_to((P, G))).then_inc(sum_in[b], 16)
                    if with_types:
                        if later(i, c, 2):
                            wait(zt_done, 2 * i + c - 1)
                        sp.dma_start(tcol[b][:, :], type_t[:, cols]).then_inc(type_in[b], 16)
                group_steps(sp, step)

            for b in range(2):
                wait(ft_scattered[b], 16 * SUB * TILES // 2)
            node_stage(0)
            sum_pass(0, dst_t, src_t, src_row, False)
            wait(added, 16 * GJ * GROUPS)
            node_stage(1)
            sum_pass(1, src_t, dst_t, dst_row, False)
            wait(added, 16 * GJ * GROUPS * 2)
            node_stage(2)
            sum_pass(2, src_t, dst_t, dst_row, False)
            wait(added, 16 * GJ * GROUPS * 3)
            node_stage(3)
            sum_pass(3, src_t, dst_t, dst_row, True)
            wait(added, 16 * GJ * GROUPS * 4)
            node_stage(4)

        @block.gpsimd
        def _(pool):
            pool.iota(kspare[:, :], pattern=[[P, COLS]], base=NP, channel_multiplier=1).then_inc(spare_made, 1)

            def step(i, c):
                if inside(i, c, TILES):
                    pool.wait_ge(m_done, 2 * i + c + 1)
                    pool.wait_ge(main_in[c % 2], 32 * (nth(i, c) + 1))
                    if later(i, c, 1):
                        pool.wait_ge(d_done, 2 * i + c)
                    pool.tensor_tensor(mfar[:, :, :], mx[c % 2][:, :, 0:ET],
                                       far[c % 2][:, :].unsqueeze(1).broadcast_to((P, CH, ET)),
                                       ALU.add).then_inc(mfar_done, 1)
                gather(i, c + 2)
                if inside(i, c - 5, TILES):
                    b = (c - 5) % 2
                    pool.wait_ge(ft_sb, 2 * i + c - 5 + 1)
                    pool.wait_ge(fidx_in[b], 16 * (nth(i, c - 5) + 1))
                    pool.nop(nofuse=True)
                    for k in range(SUB):
                        pool.indirect_dma_start(ft_t, bass.IndirectOffsetOnAxis(ap=fidx[b][:, k:k + 1], axis=0),
                                                fts[b][:, k * F:(k + 1) * F], None).then_inc(ft_scattered[b], 16)

            def gather(i, c):
                if not inside(i, c, TILES):
                    return
                b = c % 2
                pool.wait_ge(xidx_in[b], 16 * (nth(i, c) + 1))
                if later(i, c, 2):
                    pool.wait_ge(xT_ps, 2 * i + c - 1)
                pool.nop(nofuse=True)
                for k in range(SUB):
                    pool.indirect_dma_start(xg[b][:, k, :], None, x,
                                            bass.IndirectOffsetOnAxis(ap=xidx[b][:, k:k + 1], axis=0)
                                            ).then_inc(x_gathered[b], 16)

            gather(0, 0)
            gather(0, 1)
            pool.wait_ge(ft_zero, 16 * NODE_TILES)
            softmax_steps(pool, step)

            def sum_pass(k, table, stage_before):
                base = GROUPS * k
                for b in range(2):
                    pool.wait_ge(stored[b], 16 * NODE_HALF * (stage_before + 1))

                def gather(i, c):
                    if not inside(i, c, GROUPS):
                        return
                    b = c % 2
                    pool.wait_ge(sum_in[b], 48 * i + 48 * (base // 2 + c // 2 + 1))
                    if later(i, c, 2) or k:
                        pool.wait_ge(comb_ps, base + 2 * i + c - 1)
                    if k == 3 and later(i, c, 2):
                        pool.wait_ge(zt_done, 2 * i + c - 1)
                    pool.nop(nofuse=True)
                    for j in range(GJ):
                        pool.indirect_dma_start(yg[b][:, j, :], None, table,
                                                bass.IndirectOffsetOnAxis(ap=gidx[b][:, j:j + 1], axis=0)
                                                ).then_inc(y_gathered[b], 16)

                def step(i, c):
                    gather(i, c + 1)
                    b = c % 2
                    pool.wait_ge(comb_sb, base + 2 * i + c + 1)
                    pool.wait_ge(sidx_done, base + 2 * i + c + 1)
                    if later(i, c, 1) or k:
                        pool.wait_ge(added, 32 * GJ * i + 16 * GJ * (base + c))
                    pool.nop(nofuse=True)
                    for j in range(GJ):
                        pool.indirect_dma_start(sums_all, bass.IndirectOffsetOnAxis(ap=sidx[b][:, j:j + 1], axis=0),
                                                cmb[b][:, j, :], None, compute_op=ALU.add).then_inc(added, 16)

                gather(0, 0)
                if k == 0:
                    pool.wait_ge(sums_zero, 16 * CLEARS)
                group_steps(pool, step)

            sum_pass(0, x1_t, 0)
            sum_pass(1, x2_t, 1)
            sum_pass(2, h_t, 2)
            sum_pass(3, x3_t, 3)

        @block.scalar
        def _(act):
            def step(i, c):
                b = c % 2
                if inside(i, c, TILES):
                    act.wait_ge(xT_ps, 2 * i + c + 1)
                    if later(i, c, 1):
                        act.wait_ge(h_ps, 2 * i + c)
                    act.activation(xT[:, :], ps[3][0:F, 0:ET], ACT.Copy).then_inc(xT_sb, 1)
                    act.wait_ge(h_ps, 2 * i + c + 1)
                    if later(i, c, 1):
                        act.wait_ge(e1_done, 2 * i + c)
                    act.activation(flat(hS), ps[2][:, :], ACT.Copy).then_inc(h_sb, 1)
                if inside(i, c - 4, TILES):
                    act.wait_ge(ft_ps, 2 * i + c - 4 + 1)
                    if later(i, c - 4, 2):
                        act.wait_ge(ft_scattered[b], 16 * SUB * nth(i, c - 4))
                    act.activation(fts[b][:, :], ps[3][:, 512:512 + SUB * F], ACT.Copy).then_inc(ft_sb, 1)
                if inside(i, c - 2, TILES):
                    act.wait_ge(den_done, 2 * i + c - 2 + 1)
                    if later(i, c - 2, 1):
                        act.wait_ge(inv_done, 2 * i + c - 2)
                    act.activation(lnd[:, :, :], den[b][:, :, :], ACT.Ln).then_inc(ln_done, 1)
                    act.wait_ge(ln_done, 2 * i + c - 2 + 1)
                    if later(i, c - 2, 1):
                        act.wait_ge(rat_done, 2 * i + c - 2)
                    act.activation(inv[:, :, :], lnd[:, :, :], ACT.Exp, scale=-1.0).then_inc(inv_done, 1)
                if inside(i, c, TILES):
                    act.wait_ge(u_done, 2 * i + c + 1)
                    act.activation(uu[b][:, :, :], uu[b][:, :, :], ACT.Exp).then_inc(p_done, 1)
                    act.wait_ge(d_done, 2 * i + c + 1)
                    act.activation(dd[b][:, :, :], dd[b][:, :, :], ACT.Exp).then_inc(c_done, 1)

            softmax_steps(act, step)

            def norm(ph, i, c):
                n = node_count(ph, i, c)
                act.wait_ge(s_xm, n + 1)
                act.activation(sq[:, :], xm[:, :], ACT.Square).then_inc(s_sq, 1)
                act.wait_ge(s_ve, n + 1)
                act.activation(st[:, 3, :], st[:, 2, :], ACT.Sqrt).then_inc(s_sd, 1)

            def both(eng, body):
                with eng.Fori(0, NODE_HALF) as i:
                    body(i, 0)
                    body(i, 1)

            def sum_pass(k):
                base = GROUPS * k

                def step(i, c):
                    b = c % 2
                    n = 2 * i + c
                    if k == 3:
                        act.wait_ge(ztT_ps, n + 1)
                        if later(i, c, 2):
                            act.wait_ge(ym_ps, n - 1)
                        act.activation(ztT[b], ps[0][:, 0:W], ACT.Copy).then_inc(ztT_sb, 1)
                        act.wait_ge(ym_ps, n + 1)
                        if later(i, c, 2):
                            act.wait_ge(comb_ps, base + n - 1)
                        act.activation(ym[b], ps[1][:, 0:GJ * F], ACT.Copy).then_inc(ym_sb, 1)
                    act.wait_ge(comb_ps, base + n + 1)
                    if later(i, c, 2) or k:
                        act.wait_ge(added, 32 * GJ * i + 16 * GJ * (base + c - 1))
                    act.activation(cmb[b][:, :, :].rearrange("p a b -> p (a b)"),
                                   ps[3][:, 512 * b:512 * b + GJ * F], ACT.Copy).then_inc(comb_sb, 1)
                group_steps(act, step)

            both(act, lambda i, c: norm(0, i, c))
            sum_pass(0)

            def bilinear(i, c):
                for g in range(PACKS):
                    n = (2 * i + c) * PACKS + g
                    act.wait_ge(b_tps, n + 1)
                    act.wait_ge(b_ps, 8 + 4 * (n - 1))
                    act.activation(sT[n_par(c, g)], ps[0][:, 512 * n_par(c, g):512 * n_par(c, g) + P],
                                   ACT.Copy).then_inc(b_tsb, 1)
                norm(1, i, c)

            both(act, bilinear)
            sum_pass(1)

            def gin(q, i, c):
                n = NODE_TILES * q + 2 * i + c
                act.wait_ge(g_tps, n + 1)
                act.activation(yT, ps[0][:, 0:W], ACT.Copy).then_inc(g_tsb, 1)
                act.wait_ge(g_hps, n + 1)
                act.activation(hT, ps[1][:, 0:W], ACT.Relu, bias=prm[:, A_B1A + q:A_B1A + q + 1]).then_inc(g_hsb, 1)

            both(act, lambda i, c: gin(0, i, c))
            sum_pass(2)

            def gin_out(i, c):
                gin(1, i, c)
                n = 2 * i + c
                act.wait_ge(l_zc, n + 1)
                act.activation(ex, zc, ACT.Exp).then_inc(l_ex, 1)
                act.wait_ge(l_se, n + 1)
                act.activation(st[:, 5, :], st[:, 4, :], ACT.Ln).then_inc(l_ln, 1)
                norm(3 - 1, i, c)

            both(act, gin_out)
            sum_pass(3)

            def gru(i, c):
                n = 2 * i + c
                act.wait_ge(u_tps, n + 1)
                act.activation(mT, ps[0][:, 0:W], ACT.Copy).then_inc(u_tsb, 1)
                act.activation(yT, ps[1][:, 0:W], ACT.Copy).then_inc(u_tsb, 1)
                act.wait_ge(u_g, PACKS * (n + 1))
                act.activation(gates[0], gates[0], ACT.Sigmoid).then_inc(u_sig, 1)
                act.activation(gates[1], gates[1], ACT.Sigmoid).then_inc(u_sig, 1)
                act.wait_ge(u_in, n + 1)
                act.activation(nn, gates[2], ACT.Tanh).then_inc(u_n, 1)
                norm(4 - 1, i, c)

            both(act, gru)

        @block.tensor
        def _(pe):
            pe.wait_ge(cst_in, 64)
            for u in range(F):
                last = pe.matmul(ps[0][:, u * F:(u + 1) * F], prm16[:, F + u * P:F + (u + 1) * P], prm16[:, 0:F],
                                 start=True, stop=True)
            last.then_inc(w_tp, 1)

            def step(i, c):
                b = c % 2
                n = 2 * i + c
                if inside(i, c, TILES):
                    pe.wait_ge(x_gathered[b], 16 * SUB * (nth(i, c) + 1))
                    if later(i, c, 1):
                        pe.wait_ge(xT_sb, n)
                    for k in range(SUB):
                        last = pe.matmul(ps[3][0:F, k * P:(k + 1) * P], xg[b][:, k, :], ident, start=True, stop=True)
                    last.then_inc(xT_ps, 1)
                if inside(i, c - 4, TILES):
                    pe.wait_ge(rat_done, n - 3)
                    if later(i, c - 4, 1):
                        pe.wait_ge(ft_sb, n - 4)
                    for k in range(SUB):
                        for h in range(CH):
                            last = pe.matmul(ps[3][:, 512 + k * F:512 + (k + 1) * F],
                                             rat[b][:, h, k * P:(k + 1) * P], selo, start=h == 0, stop=h == CH - 1)
                    last.then_inc(ft_ps, 1)
                if inside(i, c, TILES):
                    pe.wait_ge(xT_sb, n + 1)
                    if later(i, c, 1):
                        pe.wait_ge(h_sb, n)
                    for h in range(CH):
                        last = pe.matmul(ps[2][:, h * ET:(h + 1) * ET], repsel[:, h * P:(h + 1) * P], xT[:, :],
                                         start=True, stop=True)
                    last.then_inc(h_ps, 1)
                    pe.wait_ge(main_in[b], 32 * (nth(i, c) + 1))
                    for k, used, made in ((0, e2_done, wa_ps), (1, e1_done, wm_ps)):
                        if later(i, c, 1):
                            pe.wait_ge(used, n)
                        elif k == 0:
                            pe.wait_ge(w_made, TYPES)
                        for h in range(CH):
                            last = pe.matmul(ps[k][:, h * ET:(h + 1) * ET],
                                             wl[:, (k * CH + h) * P:(k * CH + h + 1) * P], eft[b][:, :],
                                             start=True, stop=True)
                        last.then_inc(made, 1)

            softmax_steps(pe, step)

            def both(body):
                with pe.Fori(0, NODE_HALF) as i:
                    body(i, 0)
                    body(i, 1)

            def sum_pass(k):
                base = GROUPS * k

                def step(i, c):
                    b = c % 2
                    n = 2 * i + c
                    rows_of = yg[b]
                    if k == 3:
                        pe.wait_ge(zt_done, n + 1)
                        if later(i, c, 1):
                            pe.wait_ge(ztT_sb, n)
                        for j in range(GJ):
                            last = pe.matmul(ps[0][:, j * P:(j + 1) * P], zt[b][:, j * P:(j + 1) * P], ident,
                                             start=True, stop=True)
                        last.then_inc(ztT_ps, 1)
                        pe.wait_ge(ztT_sb, n + 1)
                        if later(i, c, 1):
                            pe.wait_ge(ym_sb, n)
                        for j in range(GJ):
                            last = pe.matmul(ps[1][:, j * F:(j + 1) * F], ztT[b][:, j * P:(j + 1) * P],
                                             prm[:, A_EMB:A_EMB + F], start=True, stop=True)
                        last.then_inc(ym_ps, 1)
                        pe.wait_ge(ym_sb, n + 1)
                        row = lambda j: ym[b][:, j * F:(j + 1) * F]
                    else:
                        pe.wait_ge(y_gathered[b], 16 * GJ * i + 16 * GJ * (base // 2 + c // 2 + 1))
                        row = lambda j: yg[b][:, j, :]
                    pe.wait_ge(eq_done, base + n + 1)
                    if later(i, c, 2) or k:
                        pe.wait_ge(comb_sb, base + n - 1)
                    for t in range(GJ):
                        for j in range(t, GJ):
                            last = pe.matmul(ps[3][:, 512 * b + t * F:512 * b + (t + 1) * F],
                                             eqm[b][:, EQ0[j] + t * P:EQ0[j] + (t + 1) * P], row(j),
                                             start=j == t, stop=j == GJ - 1)
                    last.then_inc(comb_ps, 1)
                group_steps(pe, step)

            sum_pass(0)

            def bilinear(i, c):
                wait_loaded(pe, 1, i, c)
                for g in range(PACKS):
                    n = (2 * i + c) * PACKS + g
                    par_ = n_par(c, g)
                    pe.wait_ge(b_tsb, 2 + n - 1)
                    pe.matmul(ps[0][:, 512 * par_:512 * par_ + P], ain[c][:, g * P:(g + 1) * P], ident,
                              start=True, stop=True).then_inc(b_tps, 1)
                    pe.wait_ge(b_tsb, 2 + n + 1)
                    for k in range(PACK // 2):
                        pe.wait_ge(b_prod, 4 * n + k + 1)
                        for s in range(2):
                            j = 2 * k + s
                            bank = ps[1 + k // 2][:, 512 * (k % 2) + 256 * s:512 * (k % 2) + 256 * (s + 1)]
                            wj = wbk[j // 4]
                            last = pe.matmul(bank, sT[par_], wj[:, (j % 4) * 256:(j % 4 + 1) * 256],
                                             start=True, stop=True)
                        last.then_inc(b_ps, 1)

            both(bilinear)
            sum_pass(1)

            def gin(q, i, c):
                n = NODE_TILES * q + 2 * i + c
                pe.wait_ge(g_y, n + 1)
                for g in range(PACKS):
                    last = pe.matmul(ps[0][:, g * P:(g + 1) * P], yy[:, g * P:(g + 1) * P], ident,
                                     start=True, stop=True)
                last.then_inc(g_tps, 1)
                pe.wait_ge(g_tsb, n + 1)
                pe.matmul(ps[1][:, 0:512], bd[2 * q][:, :], yT[:, 0:512], start=True, stop=True)
                pe.matmul(ps[1][:, 512:W], bd[2 * q][:, :], yT[:, 512:W], start=True, stop=True).then_inc(g_hps, 1)
                pe.wait_ge(g_hsb, n + 1)
                for g in range(PACKS):
                    last = pe.matmul(ps[2][:, g * P:(g + 1) * P], hT[:, g * P:(g + 1) * P], bd[2 * q + 1][:, :],
                                     start=True, stop=True)
                last.then_inc(g_ops, 1)

            both(lambda i, c: gin(0, i, c))
            sum_pass(2)
            both(lambda i, c: gin(1, i, c))
            sum_pass(3)

            def gru(i, c):
                n = 2 * i + c
                wait_loaded(pe, 4, i, c)
                for k, t in ((0, ain), (1, xin)):
                    for g in range(PACKS):
                        last = pe.matmul(ps[k][:, g * P:(g + 1) * P], t[c][:, g * P:(g + 1) * P], ident,
                                         start=True, stop=True)
                last.then_inc(u_tps, 1)
                pe.wait_ge(u_tsb, 2 * (n + 1))
                for g in range(PACKS):
                    bank = ps[2 + g // 2 % 2][:, 512 * (g % 2):512 * (g % 2 + 1)]
                    if g >= 4:
                        pe.wait_ge(u_g, PACKS * n + g - 3)
                    pe.matmul(bank, mT[:, g * P:(g + 1) * P], bdg[0][:, :], start=True, stop=False)
                    pe.matmul(bank, yT[:, g * P:(g + 1) * P], bdg[1][:, :], start=False, stop=True).then_inc(u_ps, 1)

            both(gru)

        @block.vector
        def _(dve):
            dve.memset(zero[:, :], 0.0).then_inc(zero_made, 1)
            for b in range(2):
                dve.memset(mx[b][:, :, :], FAR).then_inc(first_made, 1)
            dve.memset(den[1][:, :, :], 0.0).then_inc(first_made, 1)
            dve.memset(num[1][:, :, :], 0.0).then_inc(first_made, 1)
            dve.wait_ge(first_made, 4)
            dve.wait_ge(keys_in, 32)
            dve.tensor_tensor(kd[:, :], ka[:, :], kb[:, :], ALU.is_equal).then_inc(k_same, 1)
            dve.wait_ge(k_same, 1)
            dve.tensor_scalar(kt[:, :], kd[:, :], -1.0, -FAR, ALU.add, ALU.mult).then_inc(k_far, 1)
            dve.wait_ge(next_in, 32)
            dve.wait_ge(spare_made, 1)
            dve.tensor_tensor(kd[:, :], ka[:, :], kb[:, :], ALU.is_equal).then_inc(k_same, 1)
            dve.tensor_tensor(kt2[:, :], kspare[:, :], ka[:, :], ALU.subtract).then_inc(k_d, 1)
            dve.wait_ge(k_same, 2)
            dve.wait_ge(k_d, 1)
            dve.tensor_tensor(kt2[:, :], kt2[:, :], kd[:, :], ALU.mult).then_inc(k_m, 1)
            dve.wait_ge(k_m, 1)
            dve.tensor_tensor(ko[:, :], kt2[:, :], ka[:, :], ALU.add).then_inc(k_idx, 1)
            dve.wait_ge(cst_in, 64)
            blk = cst[:, C_BLK:C_BLK + PACK]
            bmask = blk.unsqueeze(2).broadcast_to((P, PACK, F))
            for k, a in enumerate((A_W1A, A_W1B, A_W2A, A_W2B)):
                dve.tensor_tensor(bd[k][:, :].rearrange("p (j f) -> p j f", f=F),
                                  prm[:, a:a + F].unsqueeze(1).broadcast_to((P, PACK, F)), bmask,
                                  ALU.mult).then_inc(w_bias, 1)
            for k, a, cols in ((0, A_WIH, (0, 1, 2, None)), (1, A_WHH, (0, 1, None, 2))):
                for q, g in enumerate(cols):
                    o = bdg[k][:, q * P:(q + 1) * P]
                    if g is None:
                        dve.memset(o, 0.0).then_inc(w_bias, 1)
                    else:
                        dve.tensor_tensor(o.rearrange("p (j f) -> p j f", f=F),
                                          prm[:, a + g * F:a + (g + 1) * F].unsqueeze(1).broadcast_to((P, PACK, F)),
                                          bmask, ALU.mult).then_inc(w_bias, 1)
            WEIGHTS_MADE = 16
            flatg = bgate[:, :, :].rearrange("p a b -> p (a b)")
            dve.tensor_tensor(flatg[:, 0:32], prm[:, A_BIH:A_BIH + 32], prm[:, A_BHH:A_BHH + 32],
                              ALU.add).then_inc(w_bias, 1)
            dve.tensor_copy(flatg[:, 32:48], prm[:, A_BIH + 32:A_BIH + 48]).then_inc(w_bias, 1)
            dve.tensor_copy(flatg[:, 48:64], prm[:, A_BHH + 32:A_BHH + 48]).then_inc(w_bias, 1)
            dve.tensor_scalar(prm[:, A_EPS1:A_EPS1 + 2], prm[:, A_EPS1:A_EPS1 + 2], 1.0, None,
                              ALU.add).then_inc(w_bias, 1)
            dve.wait_ge(w_tp, 1)
            for j in range(PACK):
                o = wbk[j // 4][:, (j % 4) * 256:(j % 4 + 1) * 256]
                dve.tensor_scalar(o, ps[0][:, 0:256], blk[:, j:j + 1], None, ALU.mult).then_inc(w_made, 1)
            dve.wait_ge(w_bias, WEIGHTS_MADE)

            def step(i, c):
                n = 2 * i + c
                b = c % 2
                if inside(i, c, TILES):
                    dve.wait_ge(h_sb, n + 1)
                    dve.wait_ge(wa_ps, n + 1)
                    dve.tensor_tensor(e2f, ps[0][:, :], flat(hS), ALU.mult).then_inc(e2_done, 1)
                    dve.wait_ge(main_in[b], 32 * (nth(i, c) + 1))
                    if later(i, c, 1):
                        dve.tensor_copy(mx[b][:, :, 0:1], mx[1 - b][:, :, ET:ET + 1]).then_inc(m_first, 1)
                        dve.wait_ge(m_first, n)
                    dve.wait_ge(e2_done, n + 1)
                    for h in range(CH):
                        last = dve.tensor_tensor_scan(mx[b][:, h, 1:ET + 1], far[b][:, :], e2f[:, h * ET:(h + 1) * ET],
                                                      mx[b][:, h, 0:1], ALU.add, ALU.max)
                    last.then_inc(m_done, 1)
                    dve.wait_ge(wm_ps, n + 1)
                    dve.tensor_tensor(flat(e1[b]), ps[1][:, :], flat(hS), ALU.mult).then_inc(e1_done, 1)
                    dve.wait_ge(m_done, n + 1)
                    dve.tensor_tensor(uu[b][:, :, :], e2f.rearrange("p (h e) -> p h e", h=CH),
                                      mx[b][:, :, 1:ET + 1], ALU.subtract).then_inc(u_done, 1)
                    dve.wait_ge(mfar_done, n + 1)
                    dve.tensor_tensor(dd[b][:, :, :], mfar[:, :, :], mx[b][:, :, 1:ET + 1],
                                      ALU.subtract).then_inc(d_done, 1)
                if inside(i, c - 1, TILES):
                    m = n - 1
                    o = 1 - b
                    dve.wait_ge(p_done, m + 1)
                    if later(i, c - 1, 1):
                        dve.wait_ge(num_done, m)
                    dve.tensor_tensor(qq[:, :, :], uu[o][:, :, :], e1[o][:, :, :], ALU.mult).then_inc(q_done, 1)
                    dve.wait_ge(c_done, m + 1)
                    for h in range(CH):
                        last = dve.tensor_tensor_scan(den[o][:, h, :], dd[o][:, h, :], uu[o][:, h, :],
                                                      den[1 - o][:, h, ET - 1:ET], ALU.mult, ALU.add)
                    last.then_inc(den_done, 1)
                    dve.wait_ge(q_done, m + 1)
                    for h in range(CH):
                        last = dve.tensor_tensor_scan(num[o][:, h, :], dd[o][:, h, :], qq[:, h, :],
                                                      num[1 - o][:, h, ET - 1:ET], ALU.mult, ALU.add)
                    last.then_inc(num_done, 1)
                if inside(i, c - 2, TILES):
                    m = n - 2
                    dve.wait_ge(inv_done, m + 1)
                    if later(i, c - 2, 2):
                        dve.wait_ge(ft_ps, m - 1)
                    dve.wait_ge(num_done, m + 1)
                    dve.tensor_tensor(rat[b][:, :, :], num[b][:, :, :], inv[:, :, :], ALU.mult).then_inc(rat_done, 1)

            softmax_steps(dve, step)

            def both(body):
                with dve.Fori(0, NODE_HALF) as i:
                    body(i, 0)
                    body(i, 1)

            slots = lambda t: t.rearrange("p (k f) -> p k f", f=F)
            over = lambda t: t.unsqueeze(2).broadcast_to((P, SLOTS, F))

            def norm(ph, n_norm, i, c, v):
                n = NODE_TILES * n_norm + 2 * i + c
                dve.wait_ge(v_done, n + 1)
                dve.tensor_reduce(st[:, 0, :], slots(v), AX, ALU.add).then_inc(s_sum, 1)
                dve.wait_ge(s_sum, n + 1)
                dve.scalar_tensor_tensor(slots(xm[:, :]), over(st[:, 0, :]), -1.0 / F, slots(v),
                                         ALU.mult, ALU.add).then_inc(s_xm, 1)
                dve.wait_ge(s_sq, n + 1)
                dve.tensor_reduce(st[:, 1, :], slots(sq[:, :]), AX, ALU.add).then_inc(s_vs, 1)
                dve.wait_ge(s_vs, n + 1)
                dve.tensor_scalar(st[:, 2, :], st[:, 1, :], 1.0 / F, EPS, ALU.mult, ALU.add).then_inc(s_ve, 1)
                dve.wait_ge(s_sd, n + 1)
                dve.reciprocal(st[:, 3, :], st[:, 3, :]).then_inc(s_rs, 1)
                dve.wait_ge(s_rs, n + 1)
                dve.tensor_tensor(slots(yout[c][:, :]), slots(xm[:, :]), over(st[:, 3, :]),
                                  ALU.mult).then_inc(y_done, 1)

            def sum_pass(k):
                base = GROUPS * k
                tri = cst[:, C_TRI:C_TRI + G]

                def step(i, c):
                    b = c % 2
                    n = 2 * i + c
                    dve.wait_ge(sum_in[b], 48 * i + 48 * (base // 2 + c // 2 + 1))
                    dve.tensor_copy(kcf[b][:, :], kcol[b][:, :]).then_inc(kcf_done, 1)
                    dve.wait_ge(kcf_done, base + n + 1)
                    if later(i, c, 2) or k:
                        dve.wait_ge(comb_ps, base + n - 1)
                    for j in range(GJ):
                        w = P * (j + 1)
                        last = dve.scalar_tensor_tensor(eqm[b][:, EQ0[j]:EQ0[j] + w], krow[b][:, 0:w],
                                                        kcf[b][:, j:j + 1], tri[:, G - w:G], ALU.is_equal, ALU.mult,
                                                        accum_out=cnt[b][:, j:j + 1])
                    last.then_inc(eq_done, 1)
                    dve.tensor_tensor(kdf[:, :], cst[:, C_TRASH:C_TRASH + GJ], kcf[b][:, :],
                                      ALU.subtract).then_inc(kdf_done, 1)
                    dve.wait_ge(eq_done, base + n + 1)
                    dve.wait_ge(kdf_done, base + n + 1)
                    dve.scalar_tensor_tensor(kmd[:, :], cnt[b][:, :], 1.5, kdf[:, :], ALU.is_gt,
                                             ALU.mult).then_inc(kmd_done, 1)
                    dve.wait_ge(kmd_done, base + n + 1)
                    if later(i, c, 2) or k:
                        dve.wait_ge(added, 32 * GJ * i + 16 * GJ * (base + c - 1))
                    dve.scalar_tensor_tensor(sidx[b][:, :], kmd[:, :], float(k * (NP + G)), kcf[b][:, :],
                                             ALU.add, ALU.add).then_inc(sidx_done, 1)
                    if k == 3:
                        dve.wait_ge(type_in[b], 16 * (nth(i, c) + 1))
                        dve.tensor_copy(tcf[b][:, :], tcol[b][:, :]).then_inc(tcf_done, 1)
                        dve.wait_ge(tcf_done, n + 1)
                        dve.wait_ge(y_gathered[b], 16 * GJ * i + 16 * GJ * (base // 2 + c // 2 + 1))
                        if later(i, c, 2):
                            dve.wait_ge(ztT_ps, n - 1)
                        iota = cst[:, C_IOTA:C_IOTA + TYPES].unsqueeze(2).broadcast_to((P, TYPES, F))
                        for j in range(GJ):
                            last = dve.scalar_tensor_tensor(
                                zt[b][:, j * P:(j + 1) * P].rearrange("p (k f) -> p k f", f=F), iota,
                                tcf[b][:, j:j + 1], yg[b][:, j, :].unsqueeze(1).broadcast_to((P, TYPES, F)),
                                ALU.is_equal, ALU.mult)
                        last.then_inc(zt_done, 1)
                group_steps(dve, step)

            def first(i, c):
                wait_loaded(dve, 0, i, c)
                dve.tensor_tensor(vv[:, :], xin[c][:, :], ain[c][:, :], ALU.add).then_inc(v_done, 1)
                norm(0, 0, i, c, vv[:, :])
            both(first)
            sum_pass(0)

            dve.memset(zz, 0.0).then_inc(b_prod, 4)
            dve.memset(vv[:, :], 0.0).then_inc(b_ps, 8)
            dve.memset(xm[:, :], 0.0).then_inc(b_tsb, 2)

            def bilinear(i, c):
                wait_loaded(dve, 1, i, c)
                x_s = slots(xin[c][:, :])
                for g in range(PACKS):
                    for k in range(PACK // 2):
                        n = ((2 * i + c) * PACKS + g) * 4 + k
                        bank = ps[1 + k // 2][:, 512 * (k % 2):512 * (k % 2 + 1)]
                        s0 = g * PACK + 2 * k
                        dve.wait_ge(b_ps, 8 + n + 1)
                        dve.tensor_tensor(prod[k % 2].rearrange("p (s u w) -> p s u w", s=2, u=F),
                                          bank.rearrange("p (s u w) -> p s u w", s=2, u=F),
                                          x_s[:, s0:s0 + 2, :].unsqueeze(3).broadcast_to((P, 2, F, F)),
                                          ALU.mult).then_inc(b_prod, 1)
                        dve.wait_ge(b_prod, n + 5)
                        dve.tensor_reduce(slots(zz)[:, s0:s0 + 2, :],
                                          prod[k % 2].rearrange("p (s u w) -> p s w u", s=2, u=F),
                                          AX, ALU.add).then_inc(b_z, 1)
                m = 2 * i + c
                dve.wait_ge(b_z, 4 * PACKS * (m + 1))
                dve.tensor_tensor(slots(zz), slots(zz),
                                  prm[:, A_BTP:A_BTP + F].unsqueeze(1).broadcast_to((P, SLOTS, F)),
                                  ALU.add).then_inc(b_zb, 1)
                dve.wait_ge(b_zb, m + 1)
                dve.tensor_tensor(vv[:, :], zz, xin[c][:, :], ALU.add).then_inc(v_done, 1)
                norm(1, 1, i, c, vv[:, :])
            both(bilinear)
            sum_pass(1)

            def gin(q, ph, i, c, dst):
                n = NODE_TILES * q + 2 * i + c
                wait_loaded(dve, ph, i, c)
                dve.scalar_tensor_tensor(yy, xin[c][:, :], prm[:, A_EPS1 + q:A_EPS1 + q + 1], ain[c][:, :],
                                         ALU.mult, ALU.add).then_inc(g_y, 1)
                dve.wait_ge(g_ops, n + 1)
                a = A_B1B + F * q
                dve.tensor_tensor(slots(dst), slots(ps[2][:, 0:W]),
                                  prm[:, a:a + F].unsqueeze(1).broadcast_to((P, SLOTS, F)),
                                  ALU.add).then_inc(g_o, 1)
                dve.wait_ge(g_o, n + 1)

            def gin_first(i, c):
                gin(0, 2, i, c, zz)
                dve.tensor_scalar(yout[c][:, :], zz, 0.0, None, ALU.max).then_inc(y_done, 1)
            both(gin_first)
            sum_pass(2)

            def gin_second(i, c):
                gin(1, 3, i, c, zz)
                n = 2 * i + c
                dve.tensor_reduce(st[:, 4, :], slots(zz), AX, ALU.max).then_inc(l_max, 1)
                dve.wait_ge(l_max, n + 1)
                dve.tensor_tensor(slots(zc), slots(zz), over(st[:, 4, :]), ALU.subtract).then_inc(l_zc, 1)
                dve.wait_ge(l_ex, n + 1)
                dve.tensor_reduce(st[:, 4, :], slots(ex), AX, ALU.add).then_inc(l_se, 1)
                dve.wait_ge(l_zc, n + 1)
                dve.tensor_tensor(vv[:, :], zc, rin[c][:, :], ALU.add).then_inc(l_t, 1)
                dve.wait_ge(l_ln, n + 1)
                dve.wait_ge(l_t, n + 1)
                dve.tensor_tensor(slots(vv[:, :]), slots(vv[:, :]), over(st[:, 5, :]),
                                  ALU.subtract).then_inc(v_done, 1)
                norm(3, 2, i, c, vv[:, :])
            both(gin_second)
            sum_pass(3)

            def gru(i, c):
                n = 2 * i + c
                wait_loaded(dve, 4, i, c)
                for g in range(PACKS):
                    bank = ps[2 + g // 2 % 2][:, 512 * (g % 2):512 * (g % 2 + 1)].rearrange("p (a j f) -> p a j f", a=4, f=F)
                    dve.wait_ge(u_ps, PACKS * n + g + 1)
                    for a in range(4):
                        last = dve.tensor_tensor(gates[a][:, g * P:(g + 1) * P].rearrange("p (j f) -> p j f", f=F),
                                                 bank[:, a], bgate[:, a, :].unsqueeze(1).broadcast_to((P, PACK, F)),
                                                 ALU.add)
                    last.then_inc(u_g, 1)
                dve.wait_ge(u_sig, 2 * (n + 1))
                dve.wait_ge(u_g, PACKS * (n + 1))
                dve.tensor_tensor(rh, gates[0], gates[3], ALU.mult).then_inc(u_rh, 1)
                dve.wait_ge(u_rh, n + 1)
                dve.tensor_tensor(gates[2], rh, gates[2], ALU.add).then_inc(u_in, 1)
                dve.wait_ge(u_n, n + 1)
                dve.tensor_tensor(zx, xin[c][:, :], nn, ALU.subtract).then_inc(u_zx, 1)
                dve.wait_ge(u_zx, n + 1)
                dve.tensor_tensor(rh, zx, gates[1], ALU.mult).then_inc(u_zd, 1)
                dve.tensor_tensor(vv[:, :], nn, xin[c][:, :], ALU.add).then_inc(l_t, 1)
                dve.wait_ge(u_zd, n + 1)
                dve.wait_ge(l_t, NODE_TILES + n + 1)
                dve.tensor_tensor(vv[:, :], vv[:, :], rh, ALU.add).then_inc(v_done, 1)
                norm(4, 3, i, c, vv[:, :])
            both(gru)


def kernel(**inputs):
    import numpy as np
    import concourse.bacc as bacc
    from concourse.bass_utils import run_bass_kernel_spmd

    a = {k: np.asarray(v) for k, v in inputs.items()}

    def padded(v, n, fill):
        return np.concatenate([v, np.full((n - len(v),) + v.shape[1:], fill, v.dtype)])

    def edge_tiles(v):
        return np.ascontiguousarray(v.reshape(COLS, P).T)

    tiled = lambda w: np.tile(w, (PACK, 1))
    on_all = lambda v: np.tile(v.reshape(1, -1), (P, 1))
    src, dst = padded(a["src"], EP, N_NODES), padded(a["dst"], EP, N_NODES)
    none = np.full((1,), NP, dst.dtype)
    p = np.arange(P)
    const = np.zeros((P, C_N), np.float32)
    const[:, C_ID:C_ID + P] = np.eye(P)
    const[:, C_TRI:C_TRI + G] = np.arange(G)[None] - (G - P) <= p[:, None]
    const[:, C_BLK:C_BLK + PACK] = p[:, None] // F == np.arange(PACK)[None]
    const[:, C_TRASH:C_TRASH + GJ] = NP + np.arange(GJ)[None] * P + p[:, None]
    const[:, C_IOTA:C_IOTA + TYPES] = np.arange(TYPES)[None]
    const[:, C_SELO:C_SELO + F] = p[:, None] % F == np.arange(F)[None]
    rep = np.zeros((F, CH, P), np.float32)
    for h in range(CH):
        rep[PACK * h + p // F, h, p] = 1.0
    par = np.concatenate([
        on_all(a["L1_gnn_bias"]), on_all(a["L2_gnn_b1b"]), on_all(a["L2_gnn_b2b"]),
        on_all(a["L3_gnn_b_ih"]), on_all(a["L3_gnn_b_hh"]),
        np.tile(a["L2_gnn_b1a"], PACK)[:, None], np.tile(a["L2_gnn_b2a"], PACK)[:, None],
        on_all(a["L2_gnn_eps1"]), on_all(a["L2_gnn_eps2"]),
        tiled(a["L2_gnn_w1a"]), tiled(a["L2_gnn_w1b"]), tiled(a["L2_gnn_w2a"]), tiled(a["L2_gnn_w2b"]),
        tiled(a["L3_gnn_w_ih"].T), tiled(a["L3_gnn_w_hh"].T),
        a["L3_gnn_edge_emb"].reshape(TYPES, F, F).transpose(0, 2, 1).reshape(P, F),
    ], axis=1)
    wtp = np.tile(a["L1_gnn_W_tp"].transpose(2, 0, 1)[:, :, None, :], (1, 1, PACK, 1)).reshape(F, F * P)
    par16 = np.concatenate([a["L1_gnn_weight"].T, wtp, rep.reshape(F, CH * P)], axis=1)
    arrays = {
        "x": padded(a["x"], NP, 0),
        "ef": np.concatenate([padded(a["edge_attr_16"], EP, 0).T, np.ones((1, EP), np.float32)]),
        "wlog": np.concatenate([np.concatenate([a["L0_gnn_W_attn"], a["L0_gnn_W_msg"]], axis=1),
                                np.concatenate([a["L0_gnn_b_attn"], a["L0_gnn_b_msg"]])[None]]),
        "src_t": edge_tiles(src), "dst_t": edge_tiles(dst),
        "next_t": edge_tiles(np.concatenate([dst[1:], none])),
        "type_t": edge_tiles(padded(a["edge_type_8"], EP, 0)),
        "src_row": src, "dst_row": dst, "prev_row": np.concatenate([none, dst[:-1]]),
        "const": const, "par": par, "par16": par16,
    }
    arrays = {k: np.ascontiguousarray(v) for k, v in arrays.items()}
    nc = bacc.Bacc("TRN2", target_bir_lowering=False, num_devices=1)
    args = [nc.dram_tensor(f"in_{k}", v.shape, mybir.dt.from_np(v.dtype), kind="ExternalInput").ap()
            for k, v in arrays.items()]
    out = nc.dram_tensor("out_x", (NP, F), FP32, kind="ExternalOutput").ap()
    build_program(nc, *args, out)
    r = run_bass_kernel_spmd(nc, [{f"in_{k}": v for k, v in arrays.items()}], core_ids=[0])
    return r.results[0]["out_x"][:N_NODES]
```

```python
from contextlib import ExitStack

import concourse.bass as bass
from concourse import mybir

FP32 = mybir.dt.float32
BF16 = mybir.dt.bfloat16
I32 = mybir.dt.int32
FP16 = mybir.dt.float16
ALU = mybir.AluOpType
ACT = mybir.ActivationFunctionType
AX = mybir.AxisListType.X

P = 128
F = 16
N_NODES = 100000
N_EDGES = 50000
TYPES = 8

SLOTS = 56
NODE_TILE = P * SLOTS
NODE_TILES = -(-N_NODES // NODE_TILE)
NP = NODE_TILES * NODE_TILE
PACK = P // F
PACKS = SLOTS // PACK
W = SLOTS * F

ET = 512
TILES = -(-N_EDGES // ET)
EP = TILES * ET
SUB = ET // P
CH = 2
PARTS = 3

GJ = 7
G = GJ * P
GROUPS = EP // G
COLS = EP // P

BLOCK = P * PACK
BLOCKS = NP // BLOCK
SG = 8
SLOT_GROUPS = -(-(COLS + BLOCKS - 1) // (2 * SG)) * 2
SQ = -(-SLOT_GROUPS * SG // P)
SN = SQ * P
DST_PASSES = 3

LOOP_FROM, LOOP_TO, DEPTH = 6, TILES - 2, 5
CLEARS = (LOOP_TO - LOOP_FROM) // 2
CLEAR_SLOTS = -(-(NP + G) // (CLEARS * P))
CLEAR_ROWS = CLEAR_SLOTS * P

EPS = 1e-5
FAR = -1e30

C_ID, C_TRI, C_BLK, C_TRASH, C_IOTA, C_SELO = 0, 128, 128 + G, 136 + G, 136 + G + GJ, 144 + G + GJ
C_N = C_SELO + F
A_BTP, A_B1B, A_B2B, A_BIH, A_BHH = 0, 16, 32, 48, 96
A_B1A, A_B2A, A_EPS1, A_EPS2 = 144, 145, 146, 147
A_W1A, A_W1B, A_W2A, A_W2B, A_WIH, A_WHH, A_EMB = 148, 164, 180, 196, 212, 260, 308
A_N = 324


def build_program(nc, x, ef, wlog, repcon, src_t, dst_t, next_t, src_row, dst_row, prev_row, type_row, first_row,
                  const, par, par16, block_node, out):
    assert EP % G == 0 and GROUPS % 2 == 0 and TILES % 2 == 0 and NODE_TILES % 2 == 0
    ctx = ExitStack()
    with ctx:
        def sb(name, shape, dt=FP32):
            return ctx.enter_context(nc.sbuf_tensor(name, shape, dt))

        def sem(name):
            return ctx.enter_context(nc.semaphore(name))

        def pair(name):
            return [sem(name + "0"), sem(name + "1")]

        def dram(name, shape, dt=FP32):
            return nc.dram_tensor(name, shape, dt).ap()

        x1_t, x2_t, h_t, x3_t = (dram(n, [NP, F]) for n in ("x1_t", "x2_t", "h_t", "x3_t"))
        ft_t = dram("ft_t", [NP + EP, F])
        sums_all = dram("sums_all", [CLEARS * CLEAR_ROWS, F])
        block_row = dram("block_row", [SQ, P], I32)
        slot_src = dram("slot_src", [P, SN], I32)
        far_row = dram("far_row", [EP])
        ftidx_t = dram("ftidx_t", [P, COLS], I32)

        cst = sb("cst", [P, C_N])
        prm = sb("prm", [P, A_N])
        repsel = sb("repsel", [PARTS * F, CH * P], BF16)
        identb = sb("identb", [P, P], BF16)
        ident = cst[:, C_ID:C_ID + P]
        selo = cst[:, C_SELO:C_SELO + F]
        zero = sb("zero", [P, W])
        wl = sb("wl", [F + 1, 2 * CH * P])

        UNIT, N_UNITS, N_ACC = 1024, 20, -(-(BLOCKS + 1) * P // 1024)
        arena = sb("arena", [P, N_UNITS * UNIT + 4])
        extra = sb("extra", [P, 8 * UNIT])
        acc = arena[:, 0:(BLOCKS + 1) * P]
        prm16 = arena[0:F, 0:F + F * P]
        repf = arena[0:PARTS * F, 3 * UNIT:3 * UNIT + CH * P]
        node_of = arena[:, 4 * UNIT:5 * UNIT]
        unit = [arena[:, k * UNIT:(k + 1) * UNIT] for k in range(N_UNITS - 2)]
        spare = [arena[:, k * UNIT:(k + 1) * UNIT] for k in range(N_ACC, N_UNITS)]
        spare += [extra[:, k * UNIT:(k + 1) * UNIT] for k in range(8)]

        prep = [extra[:, k * COLS:(k + 1) * COLS] for k in range(11)]
        ka, kb, ko, kspare, vrow, vcnt = (prep[k].bitcast(I32) for k in range(6))
        kt, kd, kt2, vsum, ones = prep[6:11]
        grow = [[extra[:, 11 * COLS + (a * SQ + q) * P:11 * COLS + (a * SQ + q + 1) * P] for q in range(SQ)]
                for a in range(3)]
        growf = [[extra[:, 11 * COLS + ((3 + a) * SQ + q) * P:11 * COLS + ((3 + a) * SQ + q + 1) * P]
                  for q in range(SQ)] for a in range(3)]
        kjunk = [extra[:, 11 * COLS + (12 + k) * P:11 * COLS + (12 + k) * P + COLS] for k in (0, 4, 8, 12)][:SQ]
        sl_i = sb("sl_i", [P, SQ], I32)
        sl_s = sb("sl_s", [P, SQ])
        sl_n = sb("sl_n", [P, SQ])
        sl_t = sb("sl_t", [P, SQ])
        sl_b = sb("sl_b", [P, SQ])
        sl_ti = sb("sl_ti", [P, SQ], I32)
        sl_base = sb("sl_base", [P, SQ])
        sl_off = sb("sl_off", [P, SQ])
        sl_row = sb("sl_row", [SQ, P], I32)
        offs = sb("offs", [1, SN], I32)
        rel = sb("rel", [P, SN])
        typ = sb("typ", [P, SN])
        srci = extra[:, 0:SN].bitcast(I32)

        eft = [sb(f"eft{b}", [F + 1, ET]) for b in range(2)]
        far = [sb(f"far{b}", [P, ET]) for b in range(2)]
        xidx = [sb(f"xidx{b}", [P, SUB], I32) for b in range(2)]
        fidx = [sb(f"fidx{b}", [P, SUB], I32) for b in range(2)]
        xg = [sb(f"xg{b}", [P, SUB, F]) for b in range(2)]
        xp = sb("xp", [P, SUB, PARTS, F], BF16)
        xr = [sb(f"xr{k}", [P, SUB, F]) for k in range(2)]
        xT = sb("xT", [PARTS * F, ET], BF16)
        halves = [u.rearrange("p (h e) -> p h e", h=CH) for u in unit]
        hS, e2, mfar, qq, lnd, inv = halves[0:6]
        e1, uu, dd, den, num, rat = (halves[6 + 2 * k:8 + 2 * k] for k in range(6))
        at_mx = (N_UNITS - 2) * UNIT
        mx = [arena[:, at_mx + b * (UNIT + 2):at_mx + (b + 1) * (UNIT + 2)].rearrange("p (h e) -> p h e", h=CH)
              for b in range(2)]
        fts = [sb(f"fts{b}", [P, SUB * F]) for b in range(2)]

        gidx = [sb(f"gidx{b}", [P, GJ], I32) for b in range(2)]
        krow = [unit[b][:, 0:G].bitcast(I32) for b in range(2)]
        kcol = [sb(f"kcol{b}", [P, GJ], I32) for b in range(2)]
        kcf = [sb(f"kcf{b}", [P, GJ]) for b in range(2)]
        EQ0 = [P * (J * (J + 1) // 2) for J in range(GJ + 1)]
        eqm = [extra[:, b * 4 * UNIT:b * 4 * UNIT + EQ0[GJ]] for b in range(2)]
        cnt = [sb(f"cnt{b}", [P, GJ]) for b in range(2)]
        kdf = sb("kdf", [P, GJ])
        kmd = sb("kmd", [P, GJ])
        sidx = [sb(f"sidx{b}", [P, GJ], I32) for b in range(2)]
        yg = [sb(f"yg{b}", [P, GJ, F]) for b in range(2)]
        cmb = [sb(f"cmb{b}", [P, GJ, F]) for b in range(2)]

        xin = [sb(f"xin{b}", [P, W]) for b in range(2)]
        ain = [sb(f"ain{b}", [P, W]) for b in range(2)]
        yout = [sb(f"yout{b}", [P, W]) for b in range(2)]
        vv = sb("vv", [P, W])
        xm = sb("xm", [P, W])
        st = sb("st", [P, 6, SLOTS])

        wbk = [sb(f"wb{k}", [P, 4 * F * F]) for k in range(2)]
        bd = [sb(f"bd{k}", [P, P]) for k in range(4)]
        bdg = [sb(f"bdg{k}", [P, 4 * P]) for k in range(2)]
        bgate = sb("bgate", [P, 4, F])
        flat = lambda t: t.rearrange("p a b -> p (a b)")
        e2f = flat(e2)
        tile_of = lambda k: spare[k][:, 0:W]

        io_f = sb("io_f", [P, BLOCK], FP16)
        dgidx = [sb(f"dgidx{b}", [P, SG], I32) for b in range(2)]
        dy = [sb(f"dy{b}", [P, SG, F]) for b in range(2)]
        dp = [sb(f"dp{b}", [P, PARTS, SG * F], BF16) for b in range(2)]
        dr = [sb(f"dr{k}", [P, SG * F]) for k in range(2)]
        oneh = [[extra[:, (b * SG + j) * UNIT // 2:(b * SG + j + 1) * UNIT // 2].bitcast(BF16) for j in range(SG)]
                for b in range(2)]
        zt, ztT = spare[0:2], spare[2]

        sq = tile_of(0)
        rin = [tile_of(1), tile_of(2)]
        zz, yy, yT, hT, ex, zc = (tile_of(k) for k in range(3, 9))
        gates, rh, nn, zx, mT = [tile_of(k) for k in (4, 7, 8, 9)], tile_of(10), tile_of(11), tile_of(12), tile_of(13)
        gates[0] = tile_of(3)
        sT = [spare[4][:, 0:P], spare[4][:, P:2 * P]]
        prod = [spare[5][:, 0:512], spare[5][:, 512:1024]]

        ps = [ctx.enter_context(nc.psum_tensor(f"ps{k}", [P, 1024], FP32)) for k in range(4)]

        block = ctx.enter_context(nc.Block())

        cst_in, keys_in, zero_made, first_made, spare_made = (
            sem(n) for n in ("cst_in", "keys_in", "zero_made", "first_made", "spare_made"))
        ft_zero, sums_zero = sem("ft_zero"), sem("sums_zero")
        k_same, k_far, k_d, k_m, k_idx = (sem(n) for n in ("k_same", "k_far", "k_d", "k_m", "k_idx"))
        far_out, ftidx_out, next_in = sem("far_out"), sem("ftidx_out"), sem("next_in")
        w_tp, w_made, w_bias = sem("w_tp"), sem("w_made"), sem("w_bias")

        main_in, xidx_in, fidx_in, x_gathered = pair("main_in"), pair("xidx_in"), pair("fidx_in"), pair("x_gathered")
        xT_ps, xT_sb, h_ps, h_sb, wa_ps, wm_ps = (sem(n) for n in ("xT_ps", "xT_sb", "h_ps", "h_sb", "wa_ps", "wm_ps"))
        e2_done, m_first, m_done, e1_done, u_done, mfar_done, d_done = (
            sem(n) for n in ("e2_done", "m_first", "m_done", "e1_done", "u_done", "mfar_done", "d_done"))
        p_done, c_done, q_done, den_done, num_done, ln_done, inv_done, rat_done = (
            sem(n) for n in ("p_done", "c_done", "q_done", "den_done", "num_done", "ln_done", "inv_done", "rat_done"))
        split_done, casts = sem("split_done"), sem("casts")
        ft_ps, ft_sb = sem("ft_ps"), sem("ft_sb")
        ft_scattered = pair("ft_scattered")

        sum_in, y_gathered = pair("sum_in"), pair("y_gathered")
        first_in, row_made, counted, v_shift, v_sum, v_ones, v_s, v_n, v_t, v_b, v_idx = (
            sem(n) for n in ("first_in", "row_made", "counted", "v_shift", "v_sum", "v_ones", "v_s", "v_n", "v_t", "v_b", "v_idx"))
        v_rows, v_cast, v_turned, v_off, slots_done, blk_out, offs_in, src_out = (
            sem(n) for n in ("v_rows", "v_cast", "v_turned", "v_off", "slots_done", "blk_out", "offs_in", "src_out"))
        didx_in, d_gathered = pair("didx_in"), pair("d_gathered")
        dsplit, oneh_done, slot_ps, acc_done = (sem(n) for n in ("dsplit", "oneh_done", "slot_ps", "acc_done"))
        kcf_done, eq_done, kdf_done, kmd_done, sidx_done, comb_ps, comb_sb, added = (
            sem(n) for n in ("kcf_done", "eq_done", "kdf_done", "kmd_done", "sidx_done", "comb_ps", "comb_sb", "added"))
        zt_done, ztT_ps, ztT_sb, ym_ps = (sem(n) for n in ("zt_done", "ztT_ps", "ztT_sb", "ym_ps"))
        ACC_ZEROS = 1

        node_in, stored = pair("node_in"), pair("stored")
        v_done, s_sum, s_xm, s_sq, s_vs, s_ve, s_sd, s_rs, y_done = (
            sem(n) for n in ("v_done", "s_sum", "s_xm", "s_sq", "s_vs", "s_ve", "s_sd", "s_rs", "y_done"))
        b_tps, b_tsb, b_ps, b_prod, b_z, b_zb = (sem(n) for n in ("b_tps", "b_tsb", "b_ps", "b_prod", "b_z", "b_zb"))
        g_y, g_tps, g_tsb, g_hps, g_hsb, g_ops, g_o = (
            sem(n) for n in ("g_y", "g_tps", "g_tsb", "g_hps", "g_hsb", "g_ops", "g_o"))
        l_max, l_zc, l_ex, l_se, l_ln, l_t = (sem(n) for n in ("l_max", "l_zc", "l_ex", "l_se", "l_ln", "l_t"))
        u_tps, u_tsb, u_ps, u_g, u_sig, u_rh, u_in, u_n, u_zx, u_zd = (
            sem(n) for n in ("u_tps", "u_tsb", "u_ps", "u_g", "u_sig", "u_rh", "u_in", "u_n", "u_zx", "u_zd"))

        def static(i):
            return isinstance(i, int)

        def inside(i, c, n):
            return not static(i) or 0 <= 2 * i + c < n

        def later(i, c, least=0):
            return not static(i) or 2 * i + c >= least

        def nth(i, c):
            return i + c // 2

        def steps(eng, step, first, loop_from, loop_to, last):
            for t in range(first, loop_from):
                step(0, t)
            with eng.Fori(loop_from // 2, loop_to // 2) as i:
                step(i, 0)
                step(i, 1)
            for t in range(loop_to, last):
                step(0, t)

        NODE_HALF = NODE_TILES // 2

        def softmax_steps(eng, step):
            steps(eng, step, 0, LOOP_FROM, LOOP_TO, TILES + DEPTH)

        def group_steps(eng, step):
            steps(eng, step, 0, 2, GROUPS - 2, GROUPS)

        def ntile(t):
            return bass.ds(t * NODE_TILE, NODE_TILE)

        def rows(table, i, c):
            return table[ntile(2 * i + c), :].rearrange("(g p j) f -> p g (j f)", g=PACKS, p=P)

        def tiled(buf):
            return buf.rearrange("p (g q) -> p g q", g=PACKS)

        def n_par(c, g):
            return (c * PACKS + g) % 2

        NODE_PHASES = 5
        node_loads = [[x, ft_t], [x1_t, sums_all], [x2_t, None], [h_t, None, x2_t], [x3_t, None]]
        node_store = [x1_t, x2_t, h_t, x3_t, out]
        loads_before = [sum(len(n) for n in node_loads[:k]) * NODE_HALF for k in range(NODE_PHASES + 1)]

        def node_count(ph, i, c):
            return NODE_TILES * ph + 2 * i + c

        def wait_loaded(eng, ph, i, c):
            eng.wait_ge(node_in[c], 16 * loads_before[ph] + 16 * len(node_loads[ph]) * (i + 1))

        @block.sync
        def _(sp):
            def wait(sem_, value):
                sp.wait_ge(sem_, value)
                if not static(value):
                    sp.nop(nofuse=True)

            sp.dma_start(cst[:, :], const).then_inc(cst_in, 16)
            sp.dma_start(prm[:, :], par).then_inc(cst_in, 16)
            sp.dma_start(prm16, par16).then_inc(cst_in, 16)
            sp.dma_start(wl[:, :], wlog).then_inc(cst_in, 16)
            sp.dma_start(repf, repcon).then_inc(cst_in, 16)
            sp.dma_start(node_of, block_node).then_inc(cst_in, 16)
            sp.dma_start(ka, dst_row.rearrange("(p c) -> p c", p=P)).then_inc(keys_in, 16)
            sp.dma_start(kb, prev_row.rearrange("(p c) -> p c", p=P)).then_inc(keys_in, 16)
            sp.dma_start(vrow, first_row.rearrange("(a n) -> a n", a=1).broadcast_to((P, COLS))).then_inc(first_in, 16)
            wait(zero_made, 1)
            for t in range(NODE_TILES):
                sp.dma_start(rows(ft_t, 0, t), tiled(zero[:, :])).then_inc(ft_zero, 16)
            wait(k_far, 1)
            sp.dma_start(far_row.rearrange("(p c) -> p c", p=P), kt).then_inc(far_out, 16)
            wait(far_out, 16)
            sp.dma_start(ka, dst_t).then_inc(next_in, 16)
            sp.dma_start(kb, next_t).then_inc(next_in, 16)
            wait(k_idx, 1)
            sp.dma_start(ftidx_t, ko).then_inc(ftidx_out, 16)
            wait(ftidx_out, 16)

            wait(row_made, 1)
            sp.dma_start(block_row, sl_row[:, :]).then_inc(blk_out, 16)
            wait(blk_out, 16)
            sp.dma_start(offs[:, :], block_row.rearrange("(a q) p -> a (q p)", a=1)).then_inc(offs_in, 16)
            wait(slots_done, 3)
            sp.dma_start(slot_src, srci).then_inc(src_out, 16)
            wait(src_out, 16)

            def load_xidx(i, c):
                if not inside(i, c, TILES):
                    return
                b = c % 2
                if later(i, c, 2):
                    wait(x_gathered[b], 16 * SUB * nth(i, c))
                sp.dma_start(xidx[b][:, :], src_t[:, bass.ds((2 * i + c) * SUB, SUB)]).then_inc(xidx_in[b], 16)

            def load_step(i, c):
                if inside(i, c, TILES):
                    b = c % 2
                    if later(i, c, 2):
                        wait(wm_ps, 2 * i + c - 1)
                        wait(mfar_done, 2 * i + c - 1)
                        wait(m_done, 2 * i + c - 1)
                    sp.dma_start(eft[b][:, :], ef[:, bass.ds((2 * i + c) * ET, ET)]).then_inc(main_in[b], 16)
                    sp.dma_start(far[b][:, :], far_row[bass.ds((2 * i + c) * ET, ET)].rearrange("(a n) -> a n", a=1)
                                 .broadcast_to((P, ET))).then_inc(main_in[b], 16)
                load_xidx(i, c + 2)
                if inside(i, c - 4, TILES):
                    b = c % 2
                    if later(i, c - 4, 2):
                        wait(ft_scattered[b], 16 * SUB * nth(i, c - 4))
                    sp.dma_start(fidx[b][:, :], ftidx_t[:, bass.ds((2 * i + c - 4) * SUB, SUB)]).then_inc(fidx_in[b], 16)
                if not static(i) and c == 0:
                    sp.dma_start(sums_all[bass.ds((i - LOOP_FROM // 2) * CLEAR_ROWS, CLEAR_ROWS), :]
                                 .rearrange("(p k) f -> p (k f)", p=P), zero[:, 0:CLEAR_SLOTS * F]).then_inc(sums_zero, 16)

            load_xidx(0, 0)
            load_xidx(0, 1)
            softmax_steps(sp, load_step)

            def node_stage(ph):
                def load(i, c):
                    for buf, table in zip((xin, ain, rin), node_loads[ph]):
                        if table is None:
                            sp.dma_start(buf[c][:, :], acc[:, bass.ds((2 * i + c) * W, W)]).then_inc(node_in[c], 16)
                        else:
                            sp.dma_start(tiled(buf[c][:, :]), rows(table, i, c)).then_inc(node_in[c], 16)

                def store(i, c):
                    wait(y_done, node_count(ph, i, c) + 1)
                    sp.dma_start(rows(node_store[ph], i, c), tiled(yout[c][:, :])).then_inc(stored[c], 16)

                load(0, 0)
                load(0, 1)
                with sp.Fori(0, NODE_HALF - 1) as i:
                    for c in range(2):
                        store(i, c)
                        wait(stored[c], i * 16 + 16 * (NODE_HALF * ph + 1))
                        load(i + 1, c)
                for c in range(2):
                    store(NODE_HALF - 1, c)
                for c in range(2):
                    wait(stored[c], 16 * NODE_HALF * (ph + 1))

            def sum_by_source(gather_row, key_t, key_row):
                def step(i, c):
                    b = c % 2
                    if later(i, c, 2):
                        wait(y_gathered[b], 16 * GJ * nth(i, c))
                        wait(sidx_done, 2 * i + c - 1)
                    cols = bass.ds((2 * i + c) * GJ, GJ)
                    sp.dma_start(gidx[b][:, :], gather_row[:, cols]).then_inc(sum_in[b], 16)
                    sp.dma_start(kcol[b][:, :], key_t[:, cols]).then_inc(sum_in[b], 16)
                    sp.dma_start(krow[b], key_row[bass.ds((2 * i + c) * G, G)].rearrange("(a n) -> a n", a=1)
                                 .broadcast_to((P, G))).then_inc(sum_in[b], 16)
                group_steps(sp, step)

            def sum_by_destination(k):
                base = SLOT_GROUPS * k

                def step(i, c):
                    b = c % 2
                    if later(i, c, 2) or k:
                        wait(d_gathered[b], 16 * SG * i + 16 * SG * (base // 2 + c // 2))
                    sp.dma_start(dgidx[b][:, :], slot_src[:, bass.ds((2 * i + c) * SG, SG)]).then_inc(didx_in[b], 16)
                steps(sp, step, 0, 2, SLOT_GROUPS, SLOT_GROUPS)
                wait(acc_done, ACC_ZEROS * (k + 1) + SG * SLOT_GROUPS * (k + 1))

            for b in range(2):
                wait(ft_scattered[b], 16 * SUB * TILES // 2)
            node_stage(0)
            sum_by_source(dst_t, src_t, src_row)
            wait(added, 16 * GJ * GROUPS)
            node_stage(1)
            for k in range(DST_PASSES):
                sum_by_destination(k)
                node_stage(k + 2)

        @block.gpsimd
        def _(pool):
            pool.iota(kspare, pattern=[[P, COLS]], base=NP, channel_multiplier=1).then_inc(spare_made, 1)
            pool.iota(vcnt, pattern=[[1, COLS]], base=0, channel_multiplier=0).then_inc(counted, 1)
            pool.iota(sl_i[:, :], pattern=[[P, SQ]], base=0, channel_multiplier=1).then_inc(counted, 1)
            pool.wait_ge(v_idx, 1)
            for a, table in enumerate((src_row, dst_row, type_row)):
                for q in range(SQ):
                    pool.indirect_dma_start(grow[a][q].bitcast(I32), None, table.rearrange("(t e) -> t e", e=P),
                                            bass.IndirectOffsetOnAxis(ap=sl_ti[:, q:q + 1], axis=0)
                                            ).then_inc(v_rows, 16)

            def step(i, c):
                if inside(i, c, TILES):
                    pool.wait_ge(m_done, 2 * i + c + 1)
                    pool.wait_ge(main_in[c % 2], 32 * (nth(i, c) + 1))
                    if later(i, c, 1):
                        pool.wait_ge(d_done, 2 * i + c)
                    pool.tensor_tensor(mfar[:, :, :], mx[c % 2][:, :, 0:ET],
                                       far[c % 2][:, :].unsqueeze(1).broadcast_to((P, CH, ET)),
                                       ALU.add).then_inc(mfar_done, 1)
                gather(i, c + 2)
                if inside(i, c - 5, TILES):
                    b = (c - 5) % 2
                    pool.wait_ge(ft_sb, 2 * i + c - 5 + 1)
                    pool.wait_ge(fidx_in[b], 16 * (nth(i, c - 5) + 1))
                    pool.nop(nofuse=True)
                    for k in range(SUB):
                        pool.indirect_dma_start(ft_t, bass.IndirectOffsetOnAxis(ap=fidx[b][:, k:k + 1], axis=0),
                                                fts[b][:, k * F:(k + 1) * F], None).then_inc(ft_scattered[b], 16)

            def gather(i, c):
                if not inside(i, c, TILES):
                    return
                b = c % 2
                pool.wait_ge(xidx_in[b], 16 * (nth(i, c) + 1))
                if later(i, c, 2):
                    pool.wait_ge(split_done, 5 * (2 * i + c - 1))
                pool.nop(nofuse=True)
                for k in range(SUB):
                    pool.indirect_dma_start(xg[b][:, k, :], None, x,
                                            bass.IndirectOffsetOnAxis(ap=xidx[b][:, k:k + 1], axis=0)
                                            ).then_inc(x_gathered[b], 16)

            gather(0, 0)
            gather(0, 1)
            pool.wait_ge(ft_zero, 16 * NODE_TILES)
            softmax_steps(pool, step)

            def sum_by_source(table):
                for b in range(2):
                    pool.wait_ge(stored[b], 16 * NODE_HALF)

                def gather(i, c):
                    if not inside(i, c, GROUPS):
                        return
                    b = c % 2
                    pool.wait_ge(sum_in[b], 48 * (nth(i, c) + 1))
                    if later(i, c, 2):
                        pool.wait_ge(comb_ps, 2 * i + c - 1)
                    pool.nop(nofuse=True)
                    for j in range(GJ):
                        pool.indirect_dma_start(yg[b][:, j, :], None, table,
                                                bass.IndirectOffsetOnAxis(ap=gidx[b][:, j:j + 1], axis=0)
                                                ).then_inc(y_gathered[b], 16)

                def step(i, c):
                    gather(i, c + 2)
                    b = c % 2
                    pool.wait_ge(comb_sb, 2 * i + c + 1)
                    pool.wait_ge(sidx_done, 2 * i + c + 1)
                    if later(i, c, 1):
                        pool.wait_ge(added, 16 * GJ * (2 * i + c))
                    pool.nop(nofuse=True)
                    for j in range(GJ):
                        pool.indirect_dma_start(sums_all, bass.IndirectOffsetOnAxis(ap=sidx[b][:, j:j + 1], axis=0),
                                                cmb[b][:, j, :], None, compute_op=ALU.add).then_inc(added, 16)

                gather(0, 0)
                gather(0, 1)
                pool.wait_ge(sums_zero, 16 * CLEARS)
                group_steps(pool, step)

            def sum_by_destination(k, table):
                base = SLOT_GROUPS * k
                for b in range(2):
                    pool.wait_ge(stored[b], 16 * NODE_HALF * (k + 2))

                def step(i, c):
                    b = c % 2
                    pool.wait_ge(didx_in[b], 16 * i + 16 * (base // 2 + c // 2 + 1))
                    if later(i, c, 2) or k:
                        if k == DST_PASSES - 1 and later(i, c, 2):
                            pool.wait_ge(zt_done, 2 * i + c - 1)
                        else:
                            pool.wait_ge(dsplit, 10 * i + 5 * (base + c - 1))
                    pool.nop(nofuse=True)
                    for j in range(SG):
                        pool.indirect_dma_start(dy[b][:, j, :], None, table,
                                                bass.IndirectOffsetOnAxis(ap=dgidx[b][:, j:j + 1], axis=0)
                                                ).then_inc(d_gathered[b], 16)
                steps(pool, step, 0, 2, SLOT_GROUPS, SLOT_GROUPS)

            sum_by_source(x1_t)
            for k, table in enumerate((x2_t, h_t, x3_t)):
                sum_by_destination(k, table)

        @block.scalar
        def _(act):
            def step(i, c):
                b = c % 2
                if inside(i, c, TILES):
                    act.wait_ge(h_ps, 2 * i + c + 1)
                    if later(i, c, 1):
                        act.wait_ge(e1_done, 2 * i + c)
                    act.activation(flat(hS), ps[2][:, :], ACT.Copy).then_inc(h_sb, 1)
                if inside(i, c - 4, TILES):
                    act.wait_ge(ft_ps, 2 * i + c - 4 + 1)
                    if later(i, c - 4, 2):
                        act.wait_ge(ft_scattered[b], 16 * SUB * nth(i, c - 4))
                    act.activation(fts[b][:, :], ps[3][:, 512:512 + SUB * F], ACT.Copy).then_inc(ft_sb, 1)
                if inside(i, c - 2, TILES):
                    act.wait_ge(den_done, 2 * i + c - 2 + 1)
                    if later(i, c - 2, 1):
                        act.wait_ge(inv_done, 2 * i + c - 2)
                    act.activation(lnd[:, :, :], den[b][:, :, :], ACT.Ln).then_inc(ln_done, 1)
                    act.wait_ge(ln_done, 2 * i + c - 2 + 1)
                    if later(i, c - 2, 1):
                        act.wait_ge(rat_done, 2 * i + c - 2)
                    act.activation(inv[:, :, :], lnd[:, :, :], ACT.Exp, scale=-1.0).then_inc(inv_done, 1)
                copy_xT(i, c + 1)
                if inside(i, c, TILES):
                    act.wait_ge(u_done, 2 * i + c + 1)
                    act.activation(uu[b][:, :, :], uu[b][:, :, :], ACT.Exp).then_inc(p_done, 1)
                    act.wait_ge(d_done, 2 * i + c + 1)
                    act.activation(dd[b][:, :, :], dd[b][:, :, :], ACT.Exp).then_inc(c_done, 1)

            def copy_xT(i, c):
                if not inside(i, c, TILES):
                    return
                act.wait_ge(xT_ps, 2 * i + c + 1)
                if later(i, c, 1):
                    act.wait_ge(h_ps, 2 * i + c)
                act.activation(xT[:, :], ps[3][0:PARTS * F, 0:ET], ACT.Copy).then_inc(xT_sb, 1)

            copy_xT(0, 0)
            softmax_steps(act, step)

            def norm(ph, i, c):
                n = node_count(ph, i, c)
                act.wait_ge(s_xm, n + 1)
                act.activation(sq[:, :], xm[:, :], ACT.Square).then_inc(s_sq, 1)
                act.wait_ge(s_ve, n + 1)
                act.activation(st[:, 3, :], st[:, 2, :], ACT.Sqrt).then_inc(s_sd, 1)

            def both(eng, body):
                with eng.Fori(0, NODE_HALF) as i:
                    body(i, 0)
                    body(i, 1)

            def sum_by_source():
                def step(i, c):
                    b = c % 2
                    n = 2 * i + c
                    act.wait_ge(comb_ps, n + 1)
                    if later(i, c, 2):
                        act.wait_ge(added, 16 * GJ * (n - 1))
                    act.activation(cmb[b][:, :, :].rearrange("p a b -> p (a b)"),
                                   ps[3][:, 512 * b:512 * b + GJ * F], ACT.Copy).then_inc(comb_sb, 1)
                group_steps(act, step)

            def turn_by_type():
                def step(i, c):
                    n = 2 * i + c
                    act.wait_ge(ztT_ps, n + 1)
                    if later(i, c, 1):
                        act.wait_ge(ym_ps, n)
                    act.activation(ztT, ps[0][:, :], ACT.Copy).then_inc(ztT_sb, 1)
                steps(act, step, 0, 2, SLOT_GROUPS, SLOT_GROUPS)

            both(act, lambda i, c: norm(0, i, c))
            sum_by_source()

            def bilinear(i, c):
                for g in range(PACKS):
                    n = (2 * i + c) * PACKS + g
                    act.wait_ge(b_tps, n + 1)
                    act.wait_ge(b_ps, 8 + 4 * (n - 1))
                    act.activation(sT[n_par(c, g)], ps[0][:, 512 * n_par(c, g):512 * n_par(c, g) + P],
                                   ACT.Copy).then_inc(b_tsb, 1)
                norm(1, i, c)

            both(act, bilinear)

            def gin(q, i, c):
                n = NODE_TILES * q + 2 * i + c
                act.wait_ge(g_tps, n + 1)
                act.activation(yT, ps[0][:, 0:W], ACT.Copy).then_inc(g_tsb, 1)
                act.wait_ge(g_hps, n + 1)
                act.activation(hT, ps[1][:, 0:W], ACT.Relu, bias=prm[:, A_B1A + q:A_B1A + q + 1]).then_inc(g_hsb, 1)

            both(act, lambda i, c: gin(0, i, c))

            def gin_out(i, c):
                gin(1, i, c)
                n = 2 * i + c
                act.wait_ge(l_zc, n + 1)
                act.activation(ex, zc, ACT.Exp).then_inc(l_ex, 1)
                act.wait_ge(l_se, n + 1)
                act.activation(st[:, 5, :], st[:, 4, :], ACT.Ln).then_inc(l_ln, 1)
                norm(3 - 1, i, c)

            both(act, gin_out)
            turn_by_type()

            def gru(i, c):
                n = 2 * i + c
                act.wait_ge(u_tps, n + 1)
                act.activation(mT, ps[0][:, 0:W], ACT.Copy).then_inc(u_tsb, 1)
                act.activation(yT, ps[1][:, 0:W], ACT.Copy).then_inc(u_tsb, 1)
                act.wait_ge(u_g, PACKS * (n + 1))
                act.activation(gates[0], gates[0], ACT.Sigmoid).then_inc(u_sig, 1)
                act.activation(gates[1], gates[1], ACT.Sigmoid).then_inc(u_sig, 1)
                act.wait_ge(u_in, n + 1)
                act.activation(nn, gates[2], ACT.Tanh).then_inc(u_n, 1)
                norm(4 - 1, i, c)

            both(act, gru)

        @block.tensor
        def _(pe):
            pe.wait_ge(cst_in, 96)
            pe.wait_ge(casts, 3)
            pe.wait_ge(v_off, 1)
            pe.matmul(ps[3][0:SQ, 0:P], sl_off[:, :], ident, start=True, stop=True).then_inc(v_turned, 1)
            pe.wait_ge(v_cast, 3 * SQ)
            for a, bank in enumerate((ps[1][:, 0:SN], ps[1][:, 512:512 + SN], ps[2][:, 0:SN])):
                for q in range(SQ):
                    last = pe.matmul(bank[:, q * P:(q + 1) * P], growf[a][q], ident, start=True, stop=True)
                last.then_inc(v_turned, 1)
            for u in range(F):
                last = pe.matmul(ps[0][:, u * F:(u + 1) * F], prm16[:, F + u * P:F + (u + 1) * P], prm16[:, 0:F],
                                 start=True, stop=True)
            last.then_inc(w_tp, 1)

            def step(i, c):
                b = c % 2
                n = 2 * i + c
                if inside(i, c - 4, TILES):
                    pe.wait_ge(rat_done, n - 3)
                    if later(i, c - 4, 1):
                        pe.wait_ge(ft_sb, n - 4)
                    for k in range(SUB):
                        for h in range(CH):
                            last = pe.matmul(ps[3][:, 512 + k * F:512 + (k + 1) * F],
                                             rat[b][:, h, k * P:(k + 1) * P], selo, start=h == 0, stop=h == CH - 1)
                    last.then_inc(ft_ps, 1)
                if inside(i, c, TILES):
                    pe.wait_ge(xT_sb, n + 1)
                    if later(i, c, 1):
                        pe.wait_ge(h_sb, n)
                    for h in range(CH):
                        last = pe.matmul(ps[2][:, h * ET:(h + 1) * ET], repsel[:, h * P:(h + 1) * P], xT[:, :],
                                         start=True, stop=True)
                    last.then_inc(h_ps, 1)
                    pe.wait_ge(main_in[b], 32 * (nth(i, c) + 1))
                    for k, used, made in ((0, e2_done, wa_ps), (1, e1_done, wm_ps)):
                        if later(i, c, 1):
                            pe.wait_ge(used, n)
                        elif k == 0:
                            pe.wait_ge(w_made, TYPES)
                        for h in range(CH):
                            last = pe.matmul(ps[k][:, h * ET:(h + 1) * ET],
                                             wl[:, (k * CH + h) * P:(k * CH + h + 1) * P], eft[b][:, :],
                                             start=True, stop=True)
                        last.then_inc(made, 1)
                transpose(i, c + 1)

            def transpose(i, c):
                if not inside(i, c, TILES):
                    return
                n = 2 * i + c
                pe.wait_ge(split_done, 5 * (n + 1))
                if later(i, c, 1):
                    pe.wait_ge(xT_sb, n)
                for k in range(SUB):
                    last = pe.matmul(ps[3][0:PARTS * F, k * P:(k + 1) * P],
                                     xp[:, k, :, :].rearrange("p a f -> p (a f)"), identb[:, :],
                                     start=True, stop=True)
                last.then_inc(xT_ps, 1)

            transpose(0, 0)
            softmax_steps(pe, step)

            def both(body):
                with pe.Fori(0, NODE_HALF) as i:
                    body(i, 0)
                    body(i, 1)

            def sum_by_source():
                def step(i, c):
                    b = c % 2
                    n = 2 * i + c
                    pe.wait_ge(y_gathered[b], 16 * GJ * (nth(i, c) + 1))
                    pe.wait_ge(eq_done, n + 1)
                    if later(i, c, 2):
                        pe.wait_ge(comb_sb, n - 1)
                    for t in range(GJ):
                        for j in range(t, GJ):
                            last = pe.matmul(ps[3][:, 512 * b + t * F:512 * b + (t + 1) * F],
                                             eqm[b][:, EQ0[j] + t * P:EQ0[j] + (t + 1) * P], yg[b][:, j, :],
                                             start=j == t, stop=j == GJ - 1)
                    last.then_inc(comb_ps, 1)
                group_steps(pe, step)

            def sum_by_destination(k):
                base = SLOT_GROUPS * k
                typed = k == DST_PASSES - 1

                def messages(i, c):
                    if not inside(i, c, SLOT_GROUPS):
                        return
                    n = 2 * i + c
                    pe.wait_ge(zt_done, n + 1)
                    if later(i, c, 1):
                        pe.wait_ge(ztT_sb, n)
                    for j in range(SG):
                        last = pe.matmul(ps[0][:, j * P:(j + 1) * P], zt[c % 2][:, j * P:(j + 1) * P], ident,
                                         start=True, stop=True)
                    last.then_inc(ztT_ps, 1)
                    pe.wait_ge(ztT_sb, n + 1)
                    if later(i, c, 1):
                        pe.wait_ge(dsplit, 10 * i + 5 * (base + c))
                    for j in range(SG):
                        last = pe.matmul(ps[1][:, j * F:(j + 1) * F], ztT[:, j * P:(j + 1) * P],
                                         prm[:, A_EMB:A_EMB + F], start=True, stop=True)
                    last.then_inc(ym_ps, 1)

                def step(i, c):
                    b = c % 2
                    n = 2 * i + c
                    if typed:
                        messages(i, c + 1)
                    pe.wait_ge(dsplit, 10 * i + 5 * (base + c + 1))
                    if later(i, c, 2) or k:
                        pe.wait_ge(acc_done, 2 * SG * i + SG * (base + c - 1) + ACC_ZEROS * (k + later(i, c, 2)))
                    for j in range(SG):
                        pe.wait_ge(oneh_done, 2 * SG * i + SG * (base + c) + j + 1)
                        for u in range(PACK):
                            for a in range(PARTS):
                                last = pe.matmul(ps[2 + b][:, j * P + u * F:j * P + (u + 1) * F],
                                                 oneh[b][j][:, u * P:(u + 1) * P], dp[b][:, a, j * F:(j + 1) * F],
                                                 start=a == 0, stop=a == PARTS - 1)
                        last.then_inc(slot_ps, 1)
                if typed:
                    messages(0, 0)
                steps(pe, step, 0, 2, SLOT_GROUPS - 2, SLOT_GROUPS)

            sum_by_source()

            def bilinear(i, c):
                wait_loaded(pe, 1, i, c)
                for g in range(PACKS):
                    n = (2 * i + c) * PACKS + g
                    par_ = n_par(c, g)
                    pe.wait_ge(b_tsb, 2 + n - 1)
                    pe.matmul(ps[0][:, 512 * par_:512 * par_ + P], ain[c][:, g * P:(g + 1) * P], ident,
                              start=True, stop=True).then_inc(b_tps, 1)
                    pe.wait_ge(b_tsb, 2 + n + 1)
                    for k in range(PACK // 2):
                        pe.wait_ge(b_prod, 4 * n + k + 1)
                        for s in range(2):
                            j = 2 * k + s
                            bank = ps[1 + k // 2][:, 512 * (k % 2) + 256 * s:512 * (k % 2) + 256 * (s + 1)]
                            wj = wbk[j // 4]
                            last = pe.matmul(bank, sT[par_], wj[:, (j % 4) * 256:(j % 4 + 1) * 256],
                                             start=True, stop=True)
                        last.then_inc(b_ps, 1)

            both(bilinear)
            sum_by_destination(0)

            def gin(q, i, c):
                n = NODE_TILES * q + 2 * i + c
                pe.wait_ge(g_y, n + 1)
                for g in range(PACKS):
                    last = pe.matmul(ps[0][:, g * P:(g + 1) * P], yy[:, g * P:(g + 1) * P], ident,
                                     start=True, stop=True)
                last.then_inc(g_tps, 1)
                pe.wait_ge(g_tsb, n + 1)
                pe.matmul(ps[1][:, 0:512], bd[2 * q][:, :], yT[:, 0:512], start=True, stop=True)
                pe.matmul(ps[1][:, 512:W], bd[2 * q][:, :], yT[:, 512:W], start=True, stop=True).then_inc(g_hps, 1)
                pe.wait_ge(g_hsb, n + 1)
                for g in range(PACKS):
                    last = pe.matmul(ps[2][:, g * P:(g + 1) * P], hT[:, g * P:(g + 1) * P], bd[2 * q + 1][:, :],
                                     start=True, stop=True)
                last.then_inc(g_ops, 1)

            both(lambda i, c: gin(0, i, c))
            sum_by_destination(1)
            both(lambda i, c: gin(1, i, c))
            sum_by_destination(2)

            def gru(i, c):
                n = 2 * i + c
                wait_loaded(pe, 4, i, c)
                for k, t in ((0, ain), (1, xin)):
                    for g in range(PACKS):
                        last = pe.matmul(ps[k][:, g * P:(g + 1) * P], t[c][:, g * P:(g + 1) * P], ident,
                                         start=True, stop=True)
                last.then_inc(u_tps, 1)
                pe.wait_ge(u_tsb, 2 * (n + 1))
                for g in range(PACKS):
                    bank = ps[2 + g // 2 % 2][:, 512 * (g % 2):512 * (g % 2 + 1)]
                    if g >= 4:
                        pe.wait_ge(u_g, PACKS * n + g - 3)
                    pe.matmul(bank, mT[:, g * P:(g + 1) * P], bdg[0][:, :], start=True, stop=False)
                    pe.matmul(bank, yT[:, g * P:(g + 1) * P], bdg[1][:, :], start=False, stop=True).then_inc(u_ps, 1)

            both(gru)

        @block.vector
        def _(dve):
            dve.memset(zero[:, :], 0.0).then_inc(zero_made, 1)
            for b in range(2):
                dve.memset(mx[b][:, :, :], FAR).then_inc(first_made, 1)
            dve.memset(den[1][:, :, :], 0.0).then_inc(first_made, 1)
            dve.memset(num[1][:, :, :], 0.0).then_inc(first_made, 1)
            dve.wait_ge(first_made, 4)
            dve.wait_ge(cst_in, 96)
            dve.tensor_copy(io_f[:, :], node_of).then_inc(casts, 1)
            dve.tensor_copy(repsel[:, :], repf).then_inc(casts, 1)
            dve.tensor_copy(identb[:, :], ident).then_inc(casts, 1)
            dve.wait_ge(keys_in, 32)
            dve.tensor_tensor(kd, ka, kb, ALU.is_equal).then_inc(k_same, 1)
            dve.wait_ge(k_same, 1)
            dve.tensor_scalar(kt, kd, -1.0, -FAR, ALU.add, ALU.mult).then_inc(k_far, 1)
            dve.wait_ge(next_in, 32)
            dve.wait_ge(spare_made, 1)
            dve.tensor_tensor(kd, ka, kb, ALU.is_equal).then_inc(k_same, 1)
            dve.tensor_tensor(kt2, kspare, ka, ALU.subtract).then_inc(k_d, 1)
            dve.wait_ge(k_same, 2)
            dve.wait_ge(k_d, 1)
            dve.tensor_tensor(kt2, kt2, kd, ALU.mult).then_inc(k_m, 1)
            dve.wait_ge(k_m, 1)
            dve.tensor_tensor(ko, kt2, ka, ALU.add).then_inc(k_idx, 1)
            dve.wait_ge(first_in, 16)
            dve.wait_ge(counted, 2)
            dve.memset(ones, 1.0).then_inc(v_ones, 1)
            dve.tensor_copy(sl_s[:, :], sl_i[:, :]).then_inc(v_s, 1)
            dve.tensor_scalar(vrow, vrow, BLOCK.bit_length() - 1, None, ALU.logical_shift_right).then_inc(v_shift, 1)
            dve.wait_ge(v_shift, 1)
            dve.tensor_tensor(vsum, vrow, vcnt, ALU.add).then_inc(v_sum, 1)
            dve.wait_ge(v_sum, 1)
            dve.wait_ge(v_ones, 1)
            dve.wait_ge(v_s, 1)
            for q in range(SQ):
                dve.scalar_tensor_tensor(kjunk[q], vsum, sl_s[:, q:q + 1], ones, ALU.is_le, ALU.mult,
                                         accum_out=sl_n[:, q:q + 1]).then_inc(v_n, 1)
            dve.wait_ge(v_n, SQ)
            dve.tensor_scalar(sl_t[:, :], sl_n[:, :], -1.0, 0.0, ALU.add, ALU.max).then_inc(v_t, 1)
            dve.wait_ge(v_t, 1)
            dve.tensor_copy(sl_ti[:, :], sl_t[:, :]).then_inc(v_idx, 1)
            dve.tensor_tensor(sl_b[:, :], sl_s[:, :], sl_t[:, :], ALU.subtract).then_inc(v_b, 1)
            dve.wait_ge(v_b, 1)
            dve.tensor_scalar(sl_base[:, :], sl_b[:, :], float(BLOCKS), float(BLOCK), ALU.min, ALU.mult).then_inc(v_b, 1)
            dve.tensor_scalar(sl_off[:, :], sl_b[:, :], float(BLOCKS), float(P), ALU.min, ALU.mult).then_inc(v_off, 1)
            dve.wait_ge(v_turned, 1)
            dve.tensor_copy(sl_row[:, :], ps[3][0:SQ, 0:P]).then_inc(row_made, 1)
            dve.wait_ge(v_b, 2)
            dve.wait_ge(v_rows, 16 * 3 * SQ)
            for q in range(SQ):
                dve.tensor_copy(growf[0][q], grow[0][q].bitcast(I32)).then_inc(v_cast, 1)
                dve.tensor_scalar(growf[1][q], grow[1][q].bitcast(I32), sl_base[:, q:q + 1], None,
                                  ALU.subtract).then_inc(v_cast, 1)
                dve.tensor_copy(growf[2][q], grow[2][q].bitcast(I32)).then_inc(v_cast, 1)
            dve.wait_ge(v_turned, 4)
            dve.tensor_copy(srci, ps[1][:, 0:SN]).then_inc(slots_done, 1)
            dve.tensor_copy(rel[:, :], ps[1][:, 512:512 + SN]).then_inc(slots_done, 1)
            dve.tensor_copy(typ[:, :], ps[2][:, 0:SN]).then_inc(slots_done, 1)
            blk = cst[:, C_BLK:C_BLK + PACK]
            bmask = blk.unsqueeze(2).broadcast_to((P, PACK, F))
            for k, a in enumerate((A_W1A, A_W1B, A_W2A, A_W2B)):
                dve.tensor_tensor(bd[k][:, :].rearrange("p (j f) -> p j f", f=F),
                                  prm[:, a:a + F].unsqueeze(1).broadcast_to((P, PACK, F)), bmask,
                                  ALU.mult).then_inc(w_bias, 1)
            for k, a, cols in ((0, A_WIH, (0, 1, 2, None)), (1, A_WHH, (0, 1, None, 2))):
                for q, g in enumerate(cols):
                    o = bdg[k][:, q * P:(q + 1) * P]
                    if g is None:
                        dve.memset(o, 0.0).then_inc(w_bias, 1)
                    else:
                        dve.tensor_tensor(o.rearrange("p (j f) -> p j f", f=F),
                                          prm[:, a + g * F:a + (g + 1) * F].unsqueeze(1).broadcast_to((P, PACK, F)),
                                          bmask, ALU.mult).then_inc(w_bias, 1)
            WEIGHTS_MADE = 16
            flatg = bgate[:, :, :].rearrange("p a b -> p (a b)")
            dve.tensor_tensor(flatg[:, 0:32], prm[:, A_BIH:A_BIH + 32], prm[:, A_BHH:A_BHH + 32],
                              ALU.add).then_inc(w_bias, 1)
            dve.tensor_copy(flatg[:, 32:48], prm[:, A_BIH + 32:A_BIH + 48]).then_inc(w_bias, 1)
            dve.tensor_copy(flatg[:, 48:64], prm[:, A_BHH + 32:A_BHH + 48]).then_inc(w_bias, 1)
            dve.tensor_scalar(prm[:, A_EPS1:A_EPS1 + 2], prm[:, A_EPS1:A_EPS1 + 2], 1.0, None,
                              ALU.add).then_inc(w_bias, 1)
            dve.wait_ge(w_tp, 1)
            for j in range(PACK):
                o = wbk[j // 4][:, (j % 4) * 256:(j % 4 + 1) * 256]
                dve.tensor_scalar(o, ps[0][:, 0:256], blk[:, j:j + 1], None, ALU.mult).then_inc(w_made, 1)
            dve.wait_ge(w_bias, WEIGHTS_MADE)

            def split(i, c):
                if not inside(i, c, TILES):
                    return
                n = 2 * i + c
                rows_, part = xg[c % 2], lambda a: xp[:, :, a, :]
                dve.wait_ge(x_gathered[c % 2], 16 * SUB * (nth(i, c) + 1))
                if later(i, c, 1):
                    dve.wait_ge(xT_ps, n)
                dve.tensor_copy(part(0), rows_[:, :, :]).then_inc(split_done, 1)
                dve.wait_ge(split_done, 5 * n + 1)
                dve.tensor_tensor(xr[0][:, :, :], rows_[:, :, :], part(0), ALU.subtract).then_inc(split_done, 1)
                dve.wait_ge(split_done, 5 * n + 2)
                dve.tensor_copy(part(1), xr[0][:, :, :]).then_inc(split_done, 1)
                dve.wait_ge(split_done, 5 * n + 3)
                dve.tensor_tensor(xr[1][:, :, :], xr[0][:, :, :], part(1), ALU.subtract).then_inc(split_done, 1)
                dve.wait_ge(split_done, 5 * n + 4)
                dve.tensor_copy(part(2), xr[1][:, :, :]).then_inc(split_done, 1)

            def step(i, c):
                n = 2 * i + c
                b = c % 2
                split(i, c + 1)
                if inside(i, c, TILES):
                    dve.wait_ge(h_sb, n + 1)
                    dve.wait_ge(wa_ps, n + 1)
                    dve.tensor_tensor(e2f, ps[0][:, :], flat(hS), ALU.mult).then_inc(e2_done, 1)
                    dve.wait_ge(main_in[b], 32 * (nth(i, c) + 1))
                    if later(i, c, 1):
                        dve.tensor_copy(mx[b][:, :, 0:1], mx[1 - b][:, :, ET:ET + 1]).then_inc(m_first, 1)
                        dve.wait_ge(m_first, n)
                    dve.wait_ge(e2_done, n + 1)
                    for h in range(CH):
                        last = dve.tensor_tensor_scan(mx[b][:, h, 1:ET + 1], far[b][:, :], e2f[:, h * ET:(h + 1) * ET],
                                                      mx[b][:, h, 0:1], ALU.add, ALU.max)
                    last.then_inc(m_done, 1)
                    dve.wait_ge(wm_ps, n + 1)
                    dve.tensor_tensor(flat(e1[b]), ps[1][:, :], flat(hS), ALU.mult).then_inc(e1_done, 1)
                    dve.wait_ge(m_done, n + 1)
                    dve.tensor_tensor(uu[b][:, :, :], e2f.rearrange("p (h e) -> p h e", h=CH),
                                      mx[b][:, :, 1:ET + 1], ALU.subtract).then_inc(u_done, 1)
                    dve.wait_ge(mfar_done, n + 1)
                    dve.tensor_tensor(dd[b][:, :, :], mfar[:, :, :], mx[b][:, :, 1:ET + 1],
                                      ALU.subtract).then_inc(d_done, 1)
                if inside(i, c - 1, TILES):
                    m = n - 1
                    o = 1 - b
                    dve.wait_ge(p_done, m + 1)
                    if later(i, c - 1, 1):
                        dve.wait_ge(num_done, m)
                    dve.tensor_tensor(qq[:, :, :], uu[o][:, :, :], e1[o][:, :, :], ALU.mult).then_inc(q_done, 1)
                    dve.wait_ge(c_done, m + 1)
                    for h in range(CH):
                        last = dve.tensor_tensor_scan(den[o][:, h, :], dd[o][:, h, :], uu[o][:, h, :],
                                                      den[1 - o][:, h, ET - 1:ET], ALU.mult, ALU.add)
                    last.then_inc(den_done, 1)
                    dve.wait_ge(q_done, m + 1)
                    for h in range(CH):
                        last = dve.tensor_tensor_scan(num[o][:, h, :], dd[o][:, h, :], qq[:, h, :],
                                                      num[1 - o][:, h, ET - 1:ET], ALU.mult, ALU.add)
                    last.then_inc(num_done, 1)
                if inside(i, c - 2, TILES):
                    m = n - 2
                    dve.wait_ge(inv_done, m + 1)
                    if later(i, c - 2, 2):
                        dve.wait_ge(ft_ps, m - 1)
                    dve.wait_ge(num_done, m + 1)
                    dve.tensor_tensor(rat[b][:, :, :], num[b][:, :, :], inv[:, :, :], ALU.mult).then_inc(rat_done, 1)

            split(0, 0)
            softmax_steps(dve, step)

            def both(body):
                with dve.Fori(0, NODE_HALF) as i:
                    body(i, 0)
                    body(i, 1)

            slots = lambda t: t.rearrange("p (k f) -> p k f", f=F)
            over = lambda t: t.unsqueeze(2).broadcast_to((P, SLOTS, F))

            def norm(ph, n_norm, i, c, v):
                n = NODE_TILES * n_norm + 2 * i + c
                dve.wait_ge(v_done, n + 1)
                dve.tensor_reduce(st[:, 0, :], slots(v), AX, ALU.add).then_inc(s_sum, 1)
                dve.wait_ge(s_sum, n + 1)
                dve.scalar_tensor_tensor(slots(xm[:, :]), over(st[:, 0, :]), -1.0 / F, slots(v),
                                         ALU.mult, ALU.add).then_inc(s_xm, 1)
                dve.wait_ge(s_sq, n + 1)
                dve.tensor_reduce(st[:, 1, :], slots(sq[:, :]), AX, ALU.add).then_inc(s_vs, 1)
                dve.wait_ge(s_vs, n + 1)
                dve.tensor_scalar(st[:, 2, :], st[:, 1, :], 1.0 / F, EPS, ALU.mult, ALU.add).then_inc(s_ve, 1)
                dve.wait_ge(s_sd, n + 1)
                dve.reciprocal(st[:, 3, :], st[:, 3, :]).then_inc(s_rs, 1)
                dve.wait_ge(s_rs, n + 1)
                dve.tensor_tensor(slots(yout[c][:, :]), slots(xm[:, :]), over(st[:, 3, :]),
                                  ALU.mult).then_inc(y_done, 1)

            def sum_by_source():
                tri = cst[:, C_TRI:C_TRI + G]

                def step(i, c):
                    b = c % 2
                    n = 2 * i + c
                    dve.wait_ge(sum_in[b], 48 * (nth(i, c) + 1))
                    dve.tensor_copy(kcf[b][:, :], kcol[b][:, :]).then_inc(kcf_done, 1)
                    dve.wait_ge(kcf_done, n + 1)
                    if later(i, c, 2):
                        dve.wait_ge(comb_ps, n - 1)
                    for j in range(GJ):
                        w = P * (j + 1)
                        last = dve.scalar_tensor_tensor(eqm[b][:, EQ0[j]:EQ0[j] + w], krow[b][:, 0:w],
                                                        kcf[b][:, j:j + 1], tri[:, G - w:G], ALU.is_equal, ALU.mult,
                                                        accum_out=cnt[b][:, j:j + 1])
                    last.then_inc(eq_done, 1)
                    dve.tensor_tensor(kdf[:, :], cst[:, C_TRASH:C_TRASH + GJ], kcf[b][:, :],
                                      ALU.subtract).then_inc(kdf_done, 1)
                    dve.wait_ge(eq_done, n + 1)
                    dve.wait_ge(kdf_done, n + 1)
                    dve.scalar_tensor_tensor(kmd[:, :], cnt[b][:, :], 1.5, kdf[:, :], ALU.is_gt,
                                             ALU.mult).then_inc(kmd_done, 1)
                    dve.wait_ge(kmd_done, n + 1)
                    if later(i, c, 2):
                        dve.wait_ge(added, 16 * GJ * (n - 1))
                    dve.tensor_tensor(sidx[b][:, :], kmd[:, :], kcf[b][:, :], ALU.add).then_inc(sidx_done, 1)
                group_steps(dve, step)

            def sum_by_destination(k):
                base = SLOT_GROUPS * k
                typed = k == DST_PASSES - 1
                iota = cst[:, C_IOTA:C_IOTA + TYPES].unsqueeze(2).broadcast_to((P, TYPES, F))
                dve.memset(acc, 0.0).then_inc(acc_done, ACC_ZEROS)

                def place(i, c):
                    if not inside(i, c, SLOT_GROUPS):
                        return
                    b = c % 2
                    n = 2 * i + c
                    dve.wait_ge(d_gathered[b], 16 * SG * i + 16 * SG * (base // 2 + c // 2 + 1))
                    if later(i, c, 2):
                        dve.wait_ge(ztT_ps, n - 1)
                    for j in range(SG):
                        last = dve.scalar_tensor_tensor(
                            zt[b][:, j * P:(j + 1) * P].rearrange("p (k f) -> p k f", f=F), iota,
                            typ[:, bass.ds(n * SG + j, 1)], dy[b][:, j, :].unsqueeze(1).broadcast_to((P, TYPES, F)),
                            ALU.is_equal, ALU.mult)
                    last.then_inc(zt_done, 1)

                def split(i, c):
                    b = c % 2
                    at = lambda d: 10 * i + 5 * (base + c) + d
                    if typed:
                        dve.wait_ge(ym_ps, 2 * i + c + 1)
                        rows_ = ps[1][:, 0:SG * F]
                    else:
                        dve.wait_ge(d_gathered[b], 16 * SG * i + 16 * SG * (base // 2 + c // 2 + 1))
                        rows_ = dy[b][:, :, :].rearrange("p j f -> p (j f)")
                    if later(i, c, 2) or k:
                        dve.wait_ge(slot_ps, 2 * SG * i + SG * (base + c - 1))
                    dve.tensor_copy(dp[b][:, 0, :], rows_).then_inc(dsplit, 1)
                    dve.wait_ge(dsplit, at(1))
                    dve.tensor_tensor(dr[0][:, :], rows_, dp[b][:, 0, :], ALU.subtract).then_inc(dsplit, 1)
                    dve.wait_ge(dsplit, at(2))
                    dve.tensor_copy(dp[b][:, 1, :], dr[0][:, :]).then_inc(dsplit, 1)
                    dve.wait_ge(dsplit, at(3))
                    dve.tensor_tensor(dr[1][:, :], dr[0][:, :], dp[b][:, 1, :], ALU.subtract).then_inc(dsplit, 1)
                    dve.wait_ge(dsplit, at(4))
                    dve.tensor_copy(dp[b][:, 2, :], dr[1][:, :]).then_inc(dsplit, 1)

                def collect(i, c):
                    if not inside(i, c, SLOT_GROUPS):
                        return
                    b = c % 2
                    n = 2 * i + c
                    _, at = nc.values_load_multi_w_load_instructions(
                        offs[0:1, bass.ds(n * SG, SG)], engines=[mybir.EngineType.DVE], min_val=0, max_val=BLOCKS * P,
                        skip_runtime_bounds_check_because="the offsets are clipped where they are made")
                    for j in range(SG):
                        s_ = 2 * SG * i + SG * (base + c) + j
                        if j % 4 == 0:
                            dve.wait_ge(slot_ps, s_ + 4)
                        dve.wait_ge(acc_done, s_ + ACC_ZEROS * (k + 1))
                        o = acc[:, bass.ds(at[j], P)]
                        dve.tensor_tensor(o, o, ps[2 + b][:, j * P:(j + 1) * P], ALU.add).then_inc(acc_done, 1)

                def step(i, c):
                    b = c % 2
                    n = 2 * i + c
                    if typed:
                        place(i, c + 1)
                    split(i, c)
                    for j in range(SG):
                        dve.tensor_scalar(oneh[b][j], io_f[:, :], rel[:, bass.ds(n * SG + j, 1)], None,
                                          ALU.is_equal).then_inc(oneh_done, 1)
                    collect(i, c - 1)

                if typed:
                    place(0, 0)
                if k == 0:
                    dve.wait_ge(offs_in, 16)
                steps(dve, step, 0, 2, SLOT_GROUPS - 2, SLOT_GROUPS)
                collect(0, SLOT_GROUPS - 1)

            def first(i, c):
                wait_loaded(dve, 0, i, c)
                dve.tensor_tensor(vv[:, :], xin[c][:, :], ain[c][:, :], ALU.add).then_inc(v_done, 1)
                norm(0, 0, i, c, vv[:, :])
            both(first)
            sum_by_source()

            dve.memset(zz, 0.0).then_inc(b_prod, 4)
            dve.memset(vv[:, :], 0.0).then_inc(b_ps, 8)
            dve.memset(xm[:, :], 0.0).then_inc(b_tsb, 2)

            def bilinear(i, c):
                wait_loaded(dve, 1, i, c)
                x_s = slots(xin[c][:, :])
                for g in range(PACKS):
                    for k in range(PACK // 2):
                        n = ((2 * i + c) * PACKS + g) * 4 + k
                        bank = ps[1 + k // 2][:, 512 * (k % 2):512 * (k % 2 + 1)]
                        s0 = g * PACK + 2 * k
                        dve.wait_ge(b_ps, 8 + n + 1)
                        dve.tensor_tensor(prod[k % 2].rearrange("p (s u w) -> p s u w", s=2, u=F),
                                          bank.rearrange("p (s u w) -> p s u w", s=2, u=F),
                                          x_s[:, s0:s0 + 2, :].unsqueeze(3).broadcast_to((P, 2, F, F)),
                                          ALU.mult).then_inc(b_prod, 1)
                        dve.wait_ge(b_prod, n + 5)
                        dve.tensor_reduce(slots(zz)[:, s0:s0 + 2, :],
                                          prod[k % 2].rearrange("p (s u w) -> p s w u", s=2, u=F),
                                          AX, ALU.add).then_inc(b_z, 1)
                m = 2 * i + c
                dve.wait_ge(b_z, 4 * PACKS * (m + 1))
                dve.tensor_tensor(slots(zz), slots(zz),
                                  prm[:, A_BTP:A_BTP + F].unsqueeze(1).broadcast_to((P, SLOTS, F)),
                                  ALU.add).then_inc(b_zb, 1)
                dve.wait_ge(b_zb, m + 1)
                dve.tensor_tensor(vv[:, :], zz, xin[c][:, :], ALU.add).then_inc(v_done, 1)
                norm(1, 1, i, c, vv[:, :])
            both(bilinear)
            sum_by_destination(0)

            def gin(q, ph, i, c, dst):
                n = NODE_TILES * q + 2 * i + c
                wait_loaded(dve, ph, i, c)
                dve.scalar_tensor_tensor(yy, xin[c][:, :], prm[:, A_EPS1 + q:A_EPS1 + q + 1], ain[c][:, :],
                                         ALU.mult, ALU.add).then_inc(g_y, 1)
                dve.wait_ge(g_ops, n + 1)
                a = A_B1B + F * q
                dve.tensor_tensor(slots(dst), slots(ps[2][:, 0:W]),
                                  prm[:, a:a + F].unsqueeze(1).broadcast_to((P, SLOTS, F)),
                                  ALU.add).then_inc(g_o, 1)
                dve.wait_ge(g_o, n + 1)

            def gin_first(i, c):
                gin(0, 2, i, c, zz)
                dve.tensor_scalar(yout[c][:, :], zz, 0.0, None, ALU.max).then_inc(y_done, 1)
            both(gin_first)
            sum_by_destination(1)

            def gin_second(i, c):
                gin(1, 3, i, c, zz)
                n = 2 * i + c
                dve.tensor_reduce(st[:, 4, :], slots(zz), AX, ALU.max).then_inc(l_max, 1)
                dve.wait_ge(l_max, n + 1)
                dve.tensor_tensor(slots(zc), slots(zz), over(st[:, 4, :]), ALU.subtract).then_inc(l_zc, 1)
                dve.wait_ge(l_ex, n + 1)
                dve.tensor_reduce(st[:, 4, :], slots(ex), AX, ALU.add).then_inc(l_se, 1)
                dve.wait_ge(l_zc, n + 1)
                dve.tensor_tensor(vv[:, :], zc, rin[c][:, :], ALU.add).then_inc(l_t, 1)
                dve.wait_ge(l_ln, n + 1)
                dve.wait_ge(l_t, n + 1)
                dve.tensor_tensor(slots(vv[:, :]), slots(vv[:, :]), over(st[:, 5, :]),
                                  ALU.subtract).then_inc(v_done, 1)
                norm(3, 2, i, c, vv[:, :])
            both(gin_second)
            sum_by_destination(2)

            def gru(i, c):
                n = 2 * i + c
                wait_loaded(dve, 4, i, c)
                for g in range(PACKS):
                    bank = ps[2 + g // 2 % 2][:, 512 * (g % 2):512 * (g % 2 + 1)].rearrange("p (a j f) -> p a j f", a=4, f=F)
                    dve.wait_ge(u_ps, PACKS * n + g + 1)
                    for a in range(4):
                        last = dve.tensor_tensor(gates[a][:, g * P:(g + 1) * P].rearrange("p (j f) -> p j f", f=F),
                                                 bank[:, a], bgate[:, a, :].unsqueeze(1).broadcast_to((P, PACK, F)),
                                                 ALU.add)
                    last.then_inc(u_g, 1)
                dve.wait_ge(u_sig, 2 * (n + 1))
                dve.wait_ge(u_g, PACKS * (n + 1))
                dve.tensor_tensor(rh, gates[0], gates[3], ALU.mult).then_inc(u_rh, 1)
                dve.wait_ge(u_rh, n + 1)
                dve.tensor_tensor(gates[2], rh, gates[2], ALU.add).then_inc(u_in, 1)
                dve.wait_ge(u_n, n + 1)
                dve.tensor_tensor(zx, xin[c][:, :], nn, ALU.subtract).then_inc(u_zx, 1)
                dve.wait_ge(u_zx, n + 1)
                dve.tensor_tensor(rh, zx, gates[1], ALU.mult).then_inc(u_zd, 1)
                dve.tensor_tensor(vv[:, :], nn, xin[c][:, :], ALU.add).then_inc(l_t, 1)
                dve.wait_ge(u_zd, n + 1)
                dve.wait_ge(l_t, NODE_TILES + n + 1)
                dve.tensor_tensor(vv[:, :], vv[:, :], rh, ALU.add).then_inc(v_done, 1)
                norm(4, 3, i, c, vv[:, :])
            both(gru)


def kernel(**inputs):
    import numpy as np
    import concourse.bacc as bacc
    from concourse.bass_utils import run_bass_kernel_spmd

    a = {k: np.asarray(v) for k, v in inputs.items()}

    def padded(v, n, fill):
        return np.concatenate([v, np.full((n - len(v),) + v.shape[1:], fill, v.dtype)])

    def edge_tiles(v):
        return np.ascontiguousarray(v.reshape(COLS, P).T)

    tiled = lambda w: np.tile(w, (PACK, 1))
    on_all = lambda v: np.tile(v.reshape(1, -1), (P, 1))
    src, dst = padded(a["src"], EP, N_NODES), padded(a["dst"], EP, N_NODES)
    none = np.full((1,), NP, dst.dtype)
    p = np.arange(P)
    const = np.zeros((P, C_N), np.float32)
    const[:, C_ID:C_ID + P] = np.eye(P)
    const[:, C_TRI:C_TRI + G] = np.arange(G)[None] - (G - P) <= p[:, None]
    const[:, C_BLK:C_BLK + PACK] = p[:, None] // F == np.arange(PACK)[None]
    const[:, C_TRASH:C_TRASH + GJ] = NP + np.arange(GJ)[None] * P + p[:, None]
    const[:, C_IOTA:C_IOTA + TYPES] = np.arange(TYPES)[None]
    const[:, C_SELO:C_SELO + F] = p[:, None] % F == np.arange(F)[None]
    block_node = np.tile((PACK * p[None, :] + np.arange(PACK, dtype=np.float32)[:, None]).reshape(1, -1), (P, 1))
    rep = np.zeros((F, CH, P), np.float32)
    for h in range(CH):
        rep[PACK * h + p // F, h, p] = 1.0
    par = np.concatenate([
        on_all(a["L1_gnn_bias"]), on_all(a["L2_gnn_b1b"]), on_all(a["L2_gnn_b2b"]),
        on_all(a["L3_gnn_b_ih"]), on_all(a["L3_gnn_b_hh"]),
        np.tile(a["L2_gnn_b1a"], PACK)[:, None], np.tile(a["L2_gnn_b2a"], PACK)[:, None],
        on_all(a["L2_gnn_eps1"]), on_all(a["L2_gnn_eps2"]),
        tiled(a["L2_gnn_w1a"]), tiled(a["L2_gnn_w1b"]), tiled(a["L2_gnn_w2a"]), tiled(a["L2_gnn_w2b"]),
        tiled(a["L3_gnn_w_ih"].T), tiled(a["L3_gnn_w_hh"].T),
        a["L3_gnn_edge_emb"].reshape(TYPES, F, F).transpose(0, 2, 1).reshape(P, F),
    ], axis=1)
    wtp = np.tile(a["L1_gnn_W_tp"].transpose(2, 0, 1)[:, :, None, :], (1, 1, PACK, 1)).reshape(F, F * P)
    par16 = np.concatenate([a["L1_gnn_weight"].T, wtp], axis=1)
    arrays = {
        "x": padded(a["x"], NP, 0),
        "ef": np.concatenate([padded(a["edge_attr_16"], EP, 0).T, np.ones((1, EP), np.float32)]),
        "wlog": np.concatenate([np.concatenate([a["L0_gnn_W_attn"], a["L0_gnn_W_msg"]], axis=1),
                                np.concatenate([a["L0_gnn_b_attn"], a["L0_gnn_b_msg"]])[None]]),
        "repcon": np.tile(rep.reshape(F, CH * P), (PARTS, 1)),
        "src_t": edge_tiles(src), "dst_t": edge_tiles(dst),
        "next_t": edge_tiles(np.concatenate([dst[1:], none])),
        "src_row": src, "dst_row": dst, "prev_row": np.concatenate([none, dst[:-1]]),
        "type_row": padded(a["edge_type_8"], EP, 0), "first_row": dst[::P],
        "const": const, "par": par, "par16": par16, "block_node": block_node.astype(np.float32),
    }
    arrays = {k: np.ascontiguousarray(v) for k, v in arrays.items()}
    nc = bacc.Bacc("TRN2", target_bir_lowering=False, num_devices=1)
    args = [nc.dram_tensor(f"in_{k}", v.shape, mybir.dt.from_np(v.dtype), kind="ExternalInput").ap()
            for k, v in arrays.items()]
    out = nc.dram_tensor("out_x", (NP, F), FP32, kind="ExternalOutput").ap()
    build_program(nc, *args, out)
    r = run_bass_kernel_spmd(nc, [{f"in_{k}": v for k, v in arrays.items()}], core_ids=[0])
    return r.results[0]["out_x"][:N_NODES]
```

```python
from contextlib import ExitStack

import concourse.bass as bass
from concourse import mybir

FP32 = mybir.dt.float32
BF16 = mybir.dt.bfloat16
I32 = mybir.dt.int32
FP16 = mybir.dt.float16
ALU = mybir.AluOpType
ACT = mybir.ActivationFunctionType
AX = mybir.AxisListType.X

P = 128
F = 16
N_NODES = 100000
N_EDGES = 50000
TYPES = 8

SLOTS = 56
NODE_TILE = P * SLOTS
NODE_TILES = -(-N_NODES // NODE_TILE)
NP = NODE_TILES * NODE_TILE
PACK = P // F
PACKS = SLOTS // PACK
W = SLOTS * F

ET = 512
TILES = -(-N_EDGES // ET)
EP = TILES * ET
SUB = ET // P
CH = 2
PARTS = 3

GJ = 7
G = GJ * P
GROUPS = EP // G
COLS = EP // P

BLOCK = P * PACK
BLOCKS = NP // BLOCK
SG = 8
SLOT_GROUPS = -(-(COLS + BLOCKS - 1) // (2 * SG)) * 2
SQ = -(-SLOT_GROUPS * SG // P)
SN = SQ * P
DST_PASSES = 3

LOOP_FROM, LOOP_TO, DEPTH = 6, TILES - 2, 5
CLEARS = (LOOP_TO - LOOP_FROM) // 2
CLEAR_SLOTS = -(-(NP + G) // (CLEARS * P))
CLEAR_ROWS = CLEAR_SLOTS * P

EPS = 1e-5
FAR = -1e30

C_ID, C_TRI, C_BLK, C_TRASH, C_IOTA, C_SELO = 0, 128, 128 + G, 136 + G, 136 + G + GJ, 144 + G + GJ
C_N = C_SELO + F
A_BTP, A_B1B, A_B2B, A_BIH, A_BHH = 0, 16, 32, 48, 96
A_B1A, A_B2A, A_EPS1, A_EPS2 = 144, 145, 146, 147
A_W1A, A_W1B, A_W2A, A_W2B, A_WIH, A_WHH, A_EMB = 148, 164, 180, 196, 212, 260, 308
A_N = 324


def build_program(nc, x, ef, wlog, repcon, src_t, dst_t, next_t, src_row, dst_row, prev_row, type_row, first_row,
                  const, par, par16, block_node, out):
    assert EP % G == 0 and GROUPS % 2 == 0 and TILES % 2 == 0 and NODE_TILES % 2 == 0
    ctx = ExitStack()
    with ctx:
        def sb(name, shape, dt=FP32):
            return ctx.enter_context(nc.sbuf_tensor(name, shape, dt))

        def sem(name):
            return ctx.enter_context(nc.semaphore(name))

        def pair(name):
            return [sem(name + "0"), sem(name + "1")]

        def dram(name, shape, dt=FP32):
            return nc.dram_tensor(name, shape, dt).ap()

        x1_t, x2_t, h_t, x3_t = (dram(n, [NP, F]) for n in ("x1_t", "x2_t", "h_t", "x3_t"))
        ft_t = dram("ft_t", [NP + EP, F])
        sums_all = dram("sums_all", [CLEARS * CLEAR_ROWS, F])
        block_row = dram("block_row", [SQ, P], I32)
        slot_src = dram("slot_src", [P, SN], I32)
        far_row = dram("far_row", [EP])
        ftidx_t = dram("ftidx_t", [P, COLS], I32)

        cst = sb("cst", [P, C_N])
        prm = sb("prm", [P, A_N])
        repsel = sb("repsel", [PARTS * F, CH * P], BF16)
        identb = sb("identb", [P, P], BF16)
        ident = cst[:, C_ID:C_ID + P]
        selo = cst[:, C_SELO:C_SELO + F]
        zero = sb("zero", [P, W])
        wl = sb("wl", [F + 1, 2 * CH * P])

        UNIT, N_UNITS, N_ACC = 1024, 20, -(-(BLOCKS + 1) * P // 1024)
        arena = sb("arena", [P, N_UNITS * UNIT + 4])
        extra = sb("extra", [P, 8 * UNIT])
        acc = arena[:, 0:(BLOCKS + 1) * P]
        prm16 = arena[0:F, 0:F + F * P]
        repf = arena[0:PARTS * F, 3 * UNIT:3 * UNIT + CH * P]
        node_of = arena[:, 4 * UNIT:5 * UNIT]
        unit = [arena[:, k * UNIT:(k + 1) * UNIT] for k in range(N_UNITS - 2)]
        spare = [arena[:, k * UNIT:(k + 1) * UNIT] for k in range(N_ACC, N_UNITS)]
        spare += [extra[:, k * UNIT:(k + 1) * UNIT] for k in range(8)]

        prep = [extra[:, k * COLS:(k + 1) * COLS] for k in range(11)]
        ka, kb, ko, kspare, vrow, vcnt = (prep[k].bitcast(I32) for k in range(6))
        kt, kd, kt2, vsum, ones = prep[6:11]
        grow = [[extra[:, 11 * COLS + (a * SQ + q) * P:11 * COLS + (a * SQ + q + 1) * P] for q in range(SQ)]
                for a in range(3)]
        growf = [[extra[:, 11 * COLS + ((3 + a) * SQ + q) * P:11 * COLS + ((3 + a) * SQ + q + 1) * P]
                  for q in range(SQ)] for a in range(3)]
        kjunk = [extra[:, 11 * COLS + (12 + k) * P:11 * COLS + (12 + k) * P + COLS] for k in (0, 4, 8, 12)][:SQ]
        sl_i = sb("sl_i", [P, SQ], I32)
        sl_s = sb("sl_s", [P, SQ])
        sl_n = sb("sl_n", [P, SQ])
        sl_t = sb("sl_t", [P, SQ])
        sl_b = sb("sl_b", [P, SQ])
        sl_ti = sb("sl_ti", [P, SQ], I32)
        sl_base = sb("sl_base", [P, SQ])
        sl_off = sb("sl_off", [P, SQ])
        sl_row = sb("sl_row", [SQ, P], I32)
        offs = sb("offs", [1, SN], I32)
        rel = sb("rel", [P, SN])
        typ = sb("typ", [P, SN])
        srci = extra[:, 0:SN].bitcast(I32)

        edge_in = sb("edge_in", [P, 4 * ET])
        eft = [edge_in[0:F + 1, b * ET:(b + 1) * ET] for b in range(2)]
        far = [edge_in[:, (2 + b) * ET:(3 + b) * ET] for b in range(2)]
        xidx = [sb(f"xidx{b}", [P, SUB], I32) for b in range(2)]
        fidx = [sb(f"fidx{b}", [P, SUB], I32) for b in range(2)]
        xg = [sb(f"xg{b}", [P, SUB, F]) for b in range(2)]
        xp = sb("xp", [P, SUB, PARTS, F], BF16)
        xr = [sb(f"xr{k}", [P, SUB, F]) for k in range(2)]
        xT = sb("xT", [PARTS * F, ET], BF16)
        halves = [u.rearrange("p (h e) -> p h e", h=CH) for u in unit]
        hS, e2, mfar, qq, lnd, inv = halves[0:6]
        e1, uu, dd, den, num, rat = (halves[6 + 2 * k:8 + 2 * k] for k in range(6))
        at_mx = (N_UNITS - 2) * UNIT
        mx = [arena[:, at_mx + b * (UNIT + 2):at_mx + (b + 1) * (UNIT + 2)].rearrange("p (h e) -> p h e", h=CH)
              for b in range(2)]
        fts = [sb(f"fts{b}", [P, SUB * F]) for b in range(2)]

        gidx = [sb(f"gidx{b}", [P, GJ], I32) for b in range(2)]
        krow = [unit[b][:, 0:G].bitcast(I32) for b in range(2)]
        kcol = [sb(f"kcol{b}", [P, GJ], I32) for b in range(2)]
        kcf = [sb(f"kcf{b}", [P, GJ]) for b in range(2)]
        EQ0 = [P * (J * (J + 1) // 2) for J in range(GJ + 1)]
        eqm = [extra[:, b * 4 * UNIT:b * 4 * UNIT + EQ0[GJ]] for b in range(2)]
        cnt = [sb(f"cnt{b}", [P, GJ]) for b in range(2)]
        kdf = sb("kdf", [P, GJ])
        kmd = sb("kmd", [P, GJ])
        sidx = [sb(f"sidx{b}", [P, GJ], I32) for b in range(2)]
        yg = [sb(f"yg{b}", [P, GJ, F]) for b in range(2)]
        cmb = [sb(f"cmb{b}", [P, GJ, F]) for b in range(2)]

        xin = [sb(f"xin{b}", [P, W]) for b in range(2)]
        ain = [sb(f"ain{b}", [P, W]) for b in range(2)]
        yout = [sb(f"yout{b}", [P, W]) for b in range(2)]
        vv = sb("vv", [P, W])
        xm = sb("xm", [P, W])
        st = sb("st", [P, 6, SLOTS])

        wbk = [sb(f"wb{k}", [P, 4 * F * F]) for k in range(2)]
        bd = [sb(f"bd{k}", [P, P]) for k in range(4)]
        bdg = [sb(f"bdg{k}", [P, 4 * P]) for k in range(2)]
        bgate = sb("bgate", [P, 4, F])
        flat = lambda t: t.rearrange("p a b -> p (a b)")
        e2f = flat(e2)
        tile_of = lambda k: spare[k][:, 0:W]

        io_f = sb("io_f", [P, BLOCK], FP16)
        dgidx = [sb(f"dgidx{b}", [P, SG], I32) for b in range(2)]
        dy = [sb(f"dy{b}", [P, SG, F]) for b in range(2)]
        dp = [sb(f"dp{b}", [P, PARTS, SG * F], BF16) for b in range(2)]
        dr = [sb(f"dr{k}", [P, SG * F]) for k in range(2)]
        oneh = [[extra[:, (b * SG + j) * UNIT // 2:(b * SG + j + 1) * UNIT // 2].bitcast(BF16) for j in range(SG)]
                for b in range(2)]
        zt, ztT = spare[0:2], spare[2]

        sq = tile_of(0)
        rin = [edge_in[:, b * 2 * ET:b * 2 * ET + W] for b in range(2)]
        zz, yy, yT, hT, ex, zc = (tile_of(k) for k in range(3, 9))
        gates = [[tile_of(k) for k in ks] for ks in ((3, 7, 8, 9), (1, 2, 4, 14))]
        rh, nn, zx, mT = (tile_of(k) for k in range(10, 14))
        sT = [spare[4][:, 0:P], spare[4][:, P:2 * P]]
        prod = [spare[5][:, 0:512], spare[5][:, 512:1024]]
        raw, pool_prod = ([spare[a][:, 0:512], spare[a][:, 512:1024], spare[8][:, 512 * k:512 * (k + 1)]]
                          for k, a in enumerate((6, 7)))

        ps = [ctx.enter_context(nc.psum_tensor(f"ps{k}", [P, 1024], FP32)) for k in range(4)]

        block = ctx.enter_context(nc.Block())

        cst_in, keys_in, zero_made, first_made, spare_made = (
            sem(n) for n in ("cst_in", "keys_in", "zero_made", "first_made", "spare_made"))
        ft_zero, sums_zero = sem("ft_zero"), sem("sums_zero")
        k_same, k_far, k_d, k_m, k_idx = (sem(n) for n in ("k_same", "k_far", "k_d", "k_m", "k_idx"))
        far_out, ftidx_out, next_in = sem("far_out"), sem("ftidx_out"), sem("next_in")
        w_tp, w_made, w_bias = sem("w_tp"), sem("w_made"), sem("w_bias")

        main_in, xidx_in, fidx_in, x_gathered = pair("main_in"), pair("xidx_in"), pair("fidx_in"), pair("x_gathered")
        xT_ps, xT_sb, h_ps, h_sb, wa_ps, wm_ps = (sem(n) for n in ("xT_ps", "xT_sb", "h_ps", "h_sb", "wa_ps", "wm_ps"))
        e2_done, m_first, m_done, e1_done, u_done, mfar_done, d_done = (
            sem(n) for n in ("e2_done", "m_first", "m_done", "e1_done", "u_done", "mfar_done", "d_done"))
        p_done, c_done, q_done, den_done, num_done, ln_done, inv_done, rat_done = (
            sem(n) for n in ("p_done", "c_done", "q_done", "den_done", "num_done", "ln_done", "inv_done", "rat_done"))
        split_done, casts = sem("split_done"), sem("casts")
        ft_ps, ft_sb = sem("ft_ps"), sem("ft_sb")
        ft_scattered = pair("ft_scattered")

        sum_in, y_gathered = pair("sum_in"), pair("y_gathered")
        first_in, row_made, counted, v_shift, v_sum, v_ones, v_s, v_n, v_t, v_b, v_idx = (
            sem(n) for n in ("first_in", "row_made", "counted", "v_shift", "v_sum", "v_ones", "v_s", "v_n", "v_t", "v_b", "v_idx"))
        v_rows, v_cast, v_turned, v_off, slots_done, blk_out, offs_in, src_out = (
            sem(n) for n in ("v_rows", "v_cast", "v_turned", "v_off", "slots_done", "blk_out", "offs_in", "src_out"))
        didx_in, d_gathered = pair("didx_in"), pair("d_gathered")
        dsplit, oneh_done, slot_ps, acc_done = (sem(n) for n in ("dsplit", "oneh_done", "slot_ps", "acc_done"))
        kcf_done, eq_done, kdf_done, kmd_done, sidx_done, comb_ps, comb_sb, added = (
            sem(n) for n in ("kcf_done", "eq_done", "kdf_done", "kmd_done", "sidx_done", "comb_ps", "comb_sb", "added"))
        zt_done, ztT_ps, ztT_sb, ym_ps = (sem(n) for n in ("zt_done", "ztT_ps", "ztT_sb", "ym_ps"))
        ACC_ZEROS = 1

        node_in, late_in, stored = pair("node_in"), pair("late_in"), pair("stored")
        v_done, s_sum, s_xm, s_sq, s_vs, s_ve, s_sd, s_rs, y_done = (
            sem(n) for n in ("v_done", "s_sum", "s_xm", "s_sq", "s_vs", "s_ve", "s_sd", "s_rs", "y_done"))
        b_tps, b_tsb, b_ps, b_pool, b_z, b_zb = (
            sem(n) for n in ("b_tps", "b_tsb", "b_ps", "b_pool", "b_z", "b_zb"))
        b_read = [sem(f"b_read{k}") for k in range(4)]
        g_y, g_tps, g_tsb, g_hps, g_hsb, g_ops, g_o = (
            sem(n) for n in ("g_y", "g_tps", "g_tsb", "g_hps", "g_hsb", "g_ops", "g_o"))
        l_max, l_zc, l_ex, l_se, l_ln, l_t = (sem(n) for n in ("l_max", "l_zc", "l_ex", "l_se", "l_ln", "l_t"))
        u_tps, u_tsb, u_ps, u_g, u_sig, u_rh, u_in, u_n, u_zx, u_zd = (
            sem(n) for n in ("u_tps", "u_tsb", "u_ps", "u_g", "u_sig", "u_rh", "u_in", "u_n", "u_zx", "u_zd"))

        def static(i):
            return isinstance(i, int)

        def inside(i, c, n):
            return not static(i) or 0 <= 2 * i + c < n

        def later(i, c, least=0):
            return not static(i) or 2 * i + c >= least

        def nth(i, c):
            return i + c // 2

        def steps(eng, step, first, loop_from, loop_to, last):
            for t in range(first, loop_from):
                step(0, t)
            with eng.Fori(loop_from // 2, loop_to // 2) as i:
                step(i, 0)
                step(i, 1)
            for t in range(loop_to, last):
                step(0, t)

        NODE_HALF = NODE_TILES // 2

        def node_steps(eng, step, peeled=1):
            step(0, 0)
            step(0, 1)
            with eng.Fori(1, NODE_HALF - peeled) as i:
                step(i, 0)
                step(i, 1)
            for k in range(NODE_HALF - peeled, NODE_HALF):
                step(k, 0)
                step(k, 1)

        def softmax_steps(eng, step):
            steps(eng, step, 0, LOOP_FROM, LOOP_TO, TILES + DEPTH)

        def group_steps(eng, step):
            steps(eng, step, 0, 2, GROUPS - 2, GROUPS)

        def ntile(t):
            return bass.ds(t * NODE_TILE, NODE_TILE)

        def rows(table, i, c):
            return table[ntile(2 * i + c), :].rearrange("(g p j) f -> p g (j f)", g=PACKS, p=P)

        def tiled(buf):
            return buf.rearrange("p (g q) -> p g q", g=PACKS)

        def n_par(c, g):
            return (c * PACKS + g) % 2

        def bank_of(k):
            return ps[1 + k // 2][:, 512 * (k % 2):512 * (k % 2 + 1)]

        def pack_count(i, c, g):
            return (2 * i + c) * PACKS + g

        def has_packs_before(i, c, g, least=1):
            return not static(i) or pack_count(i, c, g) >= least

        def multiply(eng, o, products, x_tile, g, k):
            s0 = g * PACK + 2 * k
            return eng.tensor_tensor(o.rearrange("p (s u w) -> p s u w", s=2, u=F),
                                     products.rearrange("p (s u w) -> p s u w", s=2, u=F),
                                     x_tile.rearrange("p (k f) -> p k f", f=F)[:, s0:s0 + 2, :].unsqueeze(3)
                                     .broadcast_to((P, 2, F, F)), ALU.mult)

        NODE_PHASES = 5
        node_loads = [[(xin, x), (ain, ft_t)], [(xin, x1_t), (ain, sums_all)], [(xin, x2_t), (ain, None)],
                      [(xin, h_t), (ain, None)], [(rin, x3_t), (ain, None)]]
        late_loads = {3: (rin, x2_t), 4: (xin, x3_t)}
        node_store = [x1_t, x2_t, h_t, x3_t, out]
        loads_before = [sum(len(n) for n in node_loads[:k]) * NODE_HALF for k in range(NODE_PHASES + 1)]

        def node_count(ph, i, c):
            return NODE_TILES * ph + 2 * i + c

        def wait_late(eng, ph, i, c):
            eng.wait_ge(late_in[c], 16 * i + 16 * (NODE_HALF * (ph - 3) + 1))

        def wait_loaded(eng, ph, i, c):
            eng.wait_ge(node_in[c % 2], 16 * loads_before[ph] + 16 * len(node_loads[ph]) * (nth(i, c) + 1))

        @block.sync
        def _(sp):
            def wait(sem_, value):
                sp.wait_ge(sem_, value)
                if not static(value):
                    sp.nop(nofuse=True)

            sp.dma_start(cst[:, :], const).then_inc(cst_in, 16)
            sp.dma_start(prm[:, :], par).then_inc(cst_in, 16)
            sp.dma_start(prm16, par16).then_inc(cst_in, 16)
            sp.dma_start(wl[:, :], wlog).then_inc(cst_in, 16)
            sp.dma_start(repf, repcon).then_inc(cst_in, 16)
            sp.dma_start(node_of, block_node).then_inc(cst_in, 16)
            sp.dma_start(ka, dst_row.rearrange("(p c) -> p c", p=P)).then_inc(keys_in, 16)
            sp.dma_start(kb, prev_row.rearrange("(p c) -> p c", p=P)).then_inc(keys_in, 16)
            sp.dma_start(vrow, first_row.rearrange("(a n) -> a n", a=1).broadcast_to((P, COLS))).then_inc(first_in, 16)
            wait(zero_made, 1)
            for t in range(NODE_TILES):
                sp.dma_start(rows(ft_t, 0, t), tiled(zero[:, :])).then_inc(ft_zero, 16)
            wait(k_far, 1)
            sp.dma_start(far_row.rearrange("(p c) -> p c", p=P), kt).then_inc(far_out, 16)
            wait(far_out, 16)
            sp.dma_start(ka, dst_t).then_inc(next_in, 16)
            sp.dma_start(kb, next_t).then_inc(next_in, 16)
            wait(k_idx, 1)
            sp.dma_start(ftidx_t, ko).then_inc(ftidx_out, 16)
            wait(ftidx_out, 16)

            wait(row_made, 1)
            sp.dma_start(block_row, sl_row[:, :]).then_inc(blk_out, 16)
            wait(blk_out, 16)
            sp.dma_start(offs[:, :], block_row.rearrange("(a q) p -> a (q p)", a=1)).then_inc(offs_in, 16)
            wait(slots_done, 3)
            sp.dma_start(slot_src, srci).then_inc(src_out, 16)
            wait(src_out, 16)

            def load_xidx(i, c):
                if not inside(i, c, TILES):
                    return
                b = c % 2
                if later(i, c, 2):
                    wait(x_gathered[b], 16 * SUB * nth(i, c))
                sp.dma_start(xidx[b][:, :], src_t[:, bass.ds((2 * i + c) * SUB, SUB)]).then_inc(xidx_in[b], 16)

            def load_step(i, c):
                if inside(i, c, TILES):
                    b = c % 2
                    if later(i, c, 2):
                        wait(wm_ps, 2 * i + c - 1)
                        wait(mfar_done, 2 * i + c - 1)
                        wait(m_done, 2 * i + c - 1)
                    sp.dma_start(eft[b][:, :], ef[:, bass.ds((2 * i + c) * ET, ET)]).then_inc(main_in[b], 16)
                    sp.dma_start(far[b][:, :], far_row[bass.ds((2 * i + c) * ET, ET)].rearrange("(a n) -> a n", a=1)
                                 .broadcast_to((P, ET))).then_inc(main_in[b], 16)
                load_xidx(i, c + 2)
                if inside(i, c - 4, TILES):
                    b = c % 2
                    if later(i, c - 4, 2):
                        wait(ft_scattered[b], 16 * SUB * nth(i, c - 4))
                    sp.dma_start(fidx[b][:, :], ftidx_t[:, bass.ds((2 * i + c - 4) * SUB, SUB)]).then_inc(fidx_in[b], 16)
                if not static(i) and c == 0:
                    sp.dma_start(sums_all[bass.ds((i - LOOP_FROM // 2) * CLEAR_ROWS, CLEAR_ROWS), :]
                                 .rearrange("(p k) f -> p (k f)", p=P), zero[:, 0:CLEAR_SLOTS * F]).then_inc(sums_zero, 16)

            load_xidx(0, 0)
            load_xidx(0, 1)
            softmax_steps(sp, load_step)

            def node_stage(ph):
                def load_one(i, c, buf, table, done):
                    if table is None:
                        sp.dma_start(buf[c][:, :], acc[:, bass.ds((2 * i + c) * W, W)]).then_inc(done[c], 16)
                    else:
                        sp.dma_start(tiled(buf[c][:, :]), rows(table, i, c)).then_inc(done[c], 16)

                def load(i, c):
                    for buf, table in node_loads[ph]:
                        load_one(i, c, buf, table, node_in)

                def load_late(i, c):
                    if ph in late_loads:
                        load_one(i, c, *late_loads[ph], late_in)

                def free(i, c):
                    if ph == 4:
                        wait(u_tps, 2 * i + c + 1)
                    else:
                        wait(g_y, NODE_TILES * (ph - 2) + 2 * i + c + 1)

                def step(i, c):
                    d = (c + 1) % 2
                    i1 = i + (c + 1) // 2
                    if ph >= 2 and inside(i, c + 3, NODE_TILES):
                        free(i1, d)
                        load(i1 + 1, d)
                    wait(y_done, node_count(ph, i, c) + 1)
                    sp.dma_start(rows(node_store[ph], i, c), tiled(yout[c][:, :])).then_inc(stored[c], 16)
                    if inside(i, c + 2, NODE_TILES):
                        if ph < 2:
                            load(i + 1, c)
                        load_late(i + 1, c)

                for c in range(2):
                    load(0, c)
                    load_late(0, c)
                if ph >= 2:
                    free(0, 0)
                    load(1, 0)
                node_steps(sp, step, peeled=2)
                for c in range(2):
                    wait(stored[c], 16 * NODE_HALF * (ph + 1))

            def sum_by_source(gather_row, key_t, key_row):
                def step(i, c):
                    b = c % 2
                    if later(i, c, 2):
                        wait(y_gathered[b], 16 * GJ * nth(i, c))
                        wait(sidx_done, 2 * i + c - 1)
                    cols = bass.ds((2 * i + c) * GJ, GJ)
                    sp.dma_start(gidx[b][:, :], gather_row[:, cols]).then_inc(sum_in[b], 16)
                    sp.dma_start(kcol[b][:, :], key_t[:, cols]).then_inc(sum_in[b], 16)
                    sp.dma_start(krow[b], key_row[bass.ds((2 * i + c) * G, G)].rearrange("(a n) -> a n", a=1)
                                 .broadcast_to((P, G))).then_inc(sum_in[b], 16)
                group_steps(sp, step)

            def sum_by_destination(k):
                base = SLOT_GROUPS * k

                def step(i, c):
                    b = c % 2
                    if later(i, c, 2) or k:
                        wait(d_gathered[b], 16 * SG * i + 16 * SG * (base // 2 + c // 2))
                    sp.dma_start(dgidx[b][:, :], slot_src[:, bass.ds((2 * i + c) * SG, SG)]).then_inc(didx_in[b], 16)
                steps(sp, step, 0, 2, SLOT_GROUPS, SLOT_GROUPS)
                wait(acc_done, ACC_ZEROS * (k + 1) + SG * SLOT_GROUPS * (k + 1))

            for b in range(2):
                wait(ft_scattered[b], 16 * SUB * TILES // 2)
            node_stage(0)
            sum_by_source(dst_t, src_t, src_row)
            wait(added, 16 * GJ * GROUPS)
            node_stage(1)
            for k in range(DST_PASSES):
                sum_by_destination(k)
                node_stage(k + 2)

        @block.gpsimd
        def _(pool):
            pool.iota(kspare, pattern=[[P, COLS]], base=NP, channel_multiplier=1).then_inc(spare_made, 1)
            pool.iota(vcnt, pattern=[[1, COLS]], base=0, channel_multiplier=0).then_inc(counted, 1)
            pool.iota(sl_i[:, :], pattern=[[P, SQ]], base=0, channel_multiplier=1).then_inc(counted, 1)
            pool.wait_ge(v_idx, 1)
            for a, table in enumerate((src_row, dst_row, type_row)):
                for q in range(SQ):
                    pool.indirect_dma_start(grow[a][q].bitcast(I32), None, table.rearrange("(t e) -> t e", e=P),
                                            bass.IndirectOffsetOnAxis(ap=sl_ti[:, q:q + 1], axis=0)
                                            ).then_inc(v_rows, 16)

            def step(i, c):
                if inside(i, c, TILES):
                    pool.wait_ge(m_done, 2 * i + c + 1)
                    pool.wait_ge(main_in[c % 2], 32 * (nth(i, c) + 1))
                    if later(i, c, 1):
                        pool.wait_ge(d_done, 2 * i + c)
                    pool.tensor_tensor(mfar[:, :, :], mx[c % 2][:, :, 0:ET],
                                       far[c % 2][:, :].unsqueeze(1).broadcast_to((P, CH, ET)),
                                       ALU.add).then_inc(mfar_done, 1)
                gather(i, c + 2)
                if inside(i, c - 5, TILES):
                    b = (c - 5) % 2
                    pool.wait_ge(ft_sb, 2 * i + c - 5 + 1)
                    pool.wait_ge(fidx_in[b], 16 * (nth(i, c - 5) + 1))
                    pool.nop(nofuse=True)
                    for k in range(SUB):
                        pool.indirect_dma_start(ft_t, bass.IndirectOffsetOnAxis(ap=fidx[b][:, k:k + 1], axis=0),
                                                fts[b][:, k * F:(k + 1) * F], None).then_inc(ft_scattered[b], 16)

            def gather(i, c):
                if not inside(i, c, TILES):
                    return
                b = c % 2
                pool.wait_ge(xidx_in[b], 16 * (nth(i, c) + 1))
                if later(i, c, 2):
                    pool.wait_ge(split_done, 5 * (2 * i + c - 1))
                pool.nop(nofuse=True)
                for k in range(SUB):
                    pool.indirect_dma_start(xg[b][:, k, :], None, x,
                                            bass.IndirectOffsetOnAxis(ap=xidx[b][:, k:k + 1], axis=0)
                                            ).then_inc(x_gathered[b], 16)

            gather(0, 0)
            gather(0, 1)
            pool.wait_ge(ft_zero, 16 * NODE_TILES)
            softmax_steps(pool, step)

            def sum_by_source(table):
                for b in range(2):
                    pool.wait_ge(stored[b], 16 * NODE_HALF)

                def gather(i, c):
                    if not inside(i, c, GROUPS):
                        return
                    b = c % 2
                    pool.wait_ge(sum_in[b], 48 * (nth(i, c) + 1))
                    if later(i, c, 2):
                        pool.wait_ge(comb_ps, 2 * i + c - 1)
                    pool.nop(nofuse=True)
                    for j in range(GJ):
                        pool.indirect_dma_start(yg[b][:, j, :], None, table,
                                                bass.IndirectOffsetOnAxis(ap=gidx[b][:, j:j + 1], axis=0)
                                                ).then_inc(y_gathered[b], 16)

                def step(i, c):
                    gather(i, c + 2)
                    b = c % 2
                    pool.wait_ge(comb_sb, 2 * i + c + 1)
                    pool.wait_ge(sidx_done, 2 * i + c + 1)
                    if later(i, c, 1):
                        pool.wait_ge(added, 16 * GJ * (2 * i + c))
                    pool.nop(nofuse=True)
                    for j in range(GJ):
                        pool.indirect_dma_start(sums_all, bass.IndirectOffsetOnAxis(ap=sidx[b][:, j:j + 1], axis=0),
                                                cmb[b][:, j, :], None, compute_op=ALU.add).then_inc(added, 16)

                gather(0, 0)
                gather(0, 1)
                pool.wait_ge(sums_zero, 16 * CLEARS)
                group_steps(pool, step)

            def sum_by_destination(k, table):
                base = SLOT_GROUPS * k
                for b in range(2):
                    pool.wait_ge(stored[b], 16 * NODE_HALF * (k + 2))

                def step(i, c):
                    b = c % 2
                    pool.wait_ge(didx_in[b], 16 * i + 16 * (base // 2 + c // 2 + 1))
                    if later(i, c, 2) or k:
                        if k == DST_PASSES - 1 and later(i, c, 2):
                            pool.wait_ge(zt_done, 2 * i + c - 1)
                        else:
                            pool.wait_ge(dsplit, 10 * i + 5 * (base + c - 1))
                    pool.nop(nofuse=True)
                    for j in range(SG):
                        pool.indirect_dma_start(dy[b][:, j, :], None, table,
                                                bass.IndirectOffsetOnAxis(ap=dgidx[b][:, j:j + 1], axis=0)
                                                ).then_inc(d_gathered[b], 16)
                steps(pool, step, 0, 2, SLOT_GROUPS, SLOT_GROUPS)

            def bilinear(i, c):
                wait_loaded(pool, 1, i, c)
                for g in range(PACKS):
                    n = pack_count(i, c, g)
                    for k in range(1, 4):
                        pool.wait_ge(b_read[k], n + 1)
                        if has_packs_before(i, c, g):
                            pool.wait_ge(b_z, 4 * (n - 1) + k + 1)
                        multiply(pool, pool_prod[k - 1], raw[k - 1], xin[c][:, :], g, k).then_inc(b_pool, 1)

            sum_by_source(x1_t)
            node_steps(pool, bilinear)
            for k, table in enumerate((x2_t, h_t, x3_t)):
                sum_by_destination(k, table)

        @block.scalar
        def _(act):
            def step(i, c):
                b = c % 2
                if inside(i, c, TILES):
                    act.wait_ge(h_ps, 2 * i + c + 1)
                    if later(i, c, 1):
                        act.wait_ge(e1_done, 2 * i + c)
                    act.activation(flat(hS), ps[2][:, :], ACT.Copy).then_inc(h_sb, 1)
                if inside(i, c - 4, TILES):
                    act.wait_ge(ft_ps, 2 * i + c - 4 + 1)
                    if later(i, c - 4, 2):
                        act.wait_ge(ft_scattered[b], 16 * SUB * nth(i, c - 4))
                    act.activation(fts[b][:, :], ps[3][:, 512:512 + SUB * F], ACT.Copy).then_inc(ft_sb, 1)
                if inside(i, c - 2, TILES):
                    act.wait_ge(den_done, 2 * i + c - 2 + 1)
                    if later(i, c - 2, 1):
                        act.wait_ge(inv_done, 2 * i + c - 2)
                    act.activation(lnd[:, :, :], den[b][:, :, :], ACT.Ln).then_inc(ln_done, 1)
                    act.wait_ge(ln_done, 2 * i + c - 2 + 1)
                    if later(i, c - 2, 1):
                        act.wait_ge(rat_done, 2 * i + c - 2)
                    act.activation(inv[:, :, :], lnd[:, :, :], ACT.Exp, scale=-1.0).then_inc(inv_done, 1)
                copy_xT(i, c + 1)
                if inside(i, c, TILES):
                    act.wait_ge(u_done, 2 * i + c + 1)
                    act.activation(uu[b][:, :, :], uu[b][:, :, :], ACT.Exp).then_inc(p_done, 1)
                    act.wait_ge(d_done, 2 * i + c + 1)
                    act.activation(dd[b][:, :, :], dd[b][:, :, :], ACT.Exp).then_inc(c_done, 1)

            def copy_xT(i, c):
                if not inside(i, c, TILES):
                    return
                act.wait_ge(xT_ps, 2 * i + c + 1)
                if later(i, c, 1):
                    act.wait_ge(h_ps, 2 * i + c)
                act.activation(xT[:, :], ps[3][0:PARTS * F, 0:ET], ACT.Copy).then_inc(xT_sb, 1)

            copy_xT(0, 0)
            softmax_steps(act, step)

            def norm(ph, i, c, between=None):
                n = node_count(ph, i, c)
                act.wait_ge(s_xm, n + 1)
                act.activation(sq[:, :], xm[:, :], ACT.Square).then_inc(s_sq, 1)
                if between:
                    between()
                act.wait_ge(s_ve, n + 1)
                act.activation(st[:, 3, :], st[:, 2, :], ACT.Sqrt).then_inc(s_sd, 1)

            def both(eng, body):
                with eng.Fori(0, NODE_HALF) as i:
                    body(i, 0)
                    body(i, 1)

            def sum_by_source():
                def step(i, c):
                    b = c % 2
                    n = 2 * i + c
                    act.wait_ge(comb_ps, n + 1)
                    if later(i, c, 2):
                        act.wait_ge(added, 16 * GJ * (n - 1))
                    act.activation(cmb[b][:, :, :].rearrange("p a b -> p (a b)"),
                                   ps[3][:, 512 * b:512 * b + GJ * F], ACT.Copy).then_inc(comb_sb, 1)
                group_steps(act, step)

            def turn_by_type():
                def step(i, c):
                    n = 2 * i + c
                    act.wait_ge(ztT_ps, n + 1)
                    if later(i, c, 1):
                        act.wait_ge(ym_ps, n)
                    act.activation(ztT, ps[0][:, :], ACT.Copy).then_inc(ztT_sb, 1)
                steps(act, step, 0, 2, SLOT_GROUPS, SLOT_GROUPS)

            both(act, lambda i, c: norm(0, i, c))
            sum_by_source()

            def copy_turned(i, c, g):
                if not inside(i, c, NODE_TILES):
                    return
                n = pack_count(i, c, g)
                par_ = n_par(c, g)
                act.wait_ge(b_tps, n + 1)
                if has_packs_before(i, c, g, 2):
                    act.wait_ge(b_ps, 4 * (n - 1))
                act.activation(sT[par_], ps[0][:, 512 * par_:512 * par_ + P], ACT.Copy).then_inc(b_tsb, 1)

            def bilinear_pack(i, c, g):
                if not inside(i, c, NODE_TILES):
                    return
                n = pack_count(i, c, g)
                copy_turned(i, c + (g + 1) // PACKS, (g + 1) % PACKS)
                for k in range(1, 4):
                    act.wait_ge(b_ps, 4 * n + k + 1)
                    if has_packs_before(i, c, g):
                        act.wait_ge(b_pool, 3 * (n - 1) + k)
                    act.activation(raw[k - 1], bank_of(k), ACT.Copy).then_inc(b_read[k], 1)

            def bilinear(i, c):
                for g in range(2, PACKS):
                    bilinear_pack(i, c, g)
                bilinear_pack(i, c + 1, 0)
                norm(1, i, c, lambda: bilinear_pack(i, c + 1, 1))

            copy_turned(0, 0, 0)
            bilinear_pack(0, 0, 0)
            bilinear_pack(0, 0, 1)
            node_steps(act, bilinear)

            def gin_turned(q, i, c):
                if not inside(i, c, NODE_TILES):
                    return
                act.wait_ge(g_tps, NODE_TILES * q + 2 * i + c + 1)
                act.activation(yT, ps[0][:, 0:W], ACT.Copy).then_inc(g_tsb, 1)

            def gin_hidden(q, i, c):
                if not inside(i, c, NODE_TILES):
                    return
                n = NODE_TILES * q + 2 * i + c
                act.wait_ge(g_hps, n + 1)
                if q or later(i, c, 1):
                    act.wait_ge(g_ops, n)
                act.activation(hT, ps[1][:, 0:W], ACT.Relu, bias=prm[:, A_B1A + q:A_B1A + q + 1]).then_inc(g_hsb, 1)

            def gin(i, c):
                gin_turned(0, i, c)
                gin_hidden(0, i, c)

            node_steps(act, gin)

            def gin_out(i, c):
                n = 2 * i + c
                act.wait_ge(l_zc, n + 1)
                act.activation(ex, zc, ACT.Exp).then_inc(l_ex, 1)
                gin_turned(1, i, c + 1)
                act.wait_ge(l_se, n + 1)
                act.activation(st[:, 5, :], st[:, 4, :], ACT.Ln).then_inc(l_ln, 1)
                gin_hidden(1, i, c + 1)
                norm(3 - 1, i, c)

            gin_turned(1, 0, 0)
            gin_hidden(1, 0, 0)
            node_steps(act, gin_out)
            turn_by_type()

            def gru(i, c):
                n = 2 * i + c
                act.wait_ge(u_g, PACKS * (n + 1))
                act.activation(gates[c][0], gates[c][0], ACT.Sigmoid).then_inc(u_sig, 1)
                act.activation(gates[c][1], gates[c][1], ACT.Sigmoid).then_inc(u_sig, 1)
                act.wait_ge(u_in, n + 1)
                act.activation(nn, gates[c][2], ACT.Tanh).then_inc(u_n, 1)
                gru_turned(i, c + 2)
                norm(4 - 1, i, c)

            def gru_turned(i, c):
                if not inside(i, c, NODE_TILES):
                    return
                n = 2 * i + c
                act.wait_ge(u_tps, n + 1)
                if later(i, c, 1):
                    act.wait_ge(u_ps, PACKS * n)
                act.activation(mT, ps[0][:, 0:W], ACT.Copy).then_inc(u_tsb, 1)
                act.activation(yT, ps[1][:, 0:W], ACT.Copy).then_inc(u_tsb, 1)

            gru_turned(0, 0)
            gru_turned(0, 1)
            node_steps(act, gru)

        @block.tensor
        def _(pe):
            pe.wait_ge(cst_in, 96)
            pe.wait_ge(casts, 3)
            pe.wait_ge(v_off, 1)
            pe.transpose(ps[3][0:SQ, 0:P], sl_off[:, :], ident).then_inc(v_turned, 1)
            pe.wait_ge(v_cast, 3 * SQ)
            for a, bank in enumerate((ps[1][:, 0:SN], ps[1][:, 512:512 + SN], ps[2][:, 0:SN])):
                for q in range(SQ):
                    last = pe.transpose(bank[:, q * P:(q + 1) * P], growf[a][q], ident)
                last.then_inc(v_turned, 1)
            for u in range(F):
                last = pe.matmul(ps[0][:, u * F:(u + 1) * F], prm16[:, F + u * P:F + (u + 1) * P], prm16[:, 0:F],
                                 start=True, stop=True)
            last.then_inc(w_tp, 1)

            def step(i, c):
                b = c % 2
                n = 2 * i + c
                if inside(i, c - 4, TILES):
                    pe.wait_ge(rat_done, n - 3)
                    if later(i, c - 4, 1):
                        pe.wait_ge(ft_sb, n - 4)
                    for k in range(SUB):
                        for h in range(CH):
                            last = pe.matmul(ps[3][:, 512 + k * F:512 + (k + 1) * F],
                                             rat[b][:, h, k * P:(k + 1) * P], selo, start=h == 0, stop=h == CH - 1)
                    last.then_inc(ft_ps, 1)
                if inside(i, c, TILES):
                    pe.wait_ge(xT_sb, n + 1)
                    if later(i, c, 1):
                        pe.wait_ge(h_sb, n)
                    for h in range(CH):
                        last = pe.matmul(ps[2][:, h * ET:(h + 1) * ET], repsel[:, h * P:(h + 1) * P], xT[:, :],
                                         start=True, stop=True)
                    last.then_inc(h_ps, 1)
                    pe.wait_ge(main_in[b], 32 * (nth(i, c) + 1))
                    for k, used, made in ((0, e2_done, wa_ps), (1, e1_done, wm_ps)):
                        if later(i, c, 1):
                            pe.wait_ge(used, n)
                        elif k == 0:
                            pe.wait_ge(w_made, TYPES)
                        for h in range(CH):
                            last = pe.matmul(ps[k][:, h * ET:(h + 1) * ET],
                                             wl[:, (k * CH + h) * P:(k * CH + h + 1) * P], eft[b][:, :],
                                             start=True, stop=True)
                        last.then_inc(made, 1)
                transpose(i, c + 1)

            def transpose(i, c):
                if not inside(i, c, TILES):
                    return
                n = 2 * i + c
                pe.wait_ge(split_done, 5 * (n + 1))
                if later(i, c, 1):
                    pe.wait_ge(xT_sb, n)
                for k in range(SUB):
                    last = pe.matmul(ps[3][0:PARTS * F, k * P:(k + 1) * P],
                                     xp[:, k, :, :].rearrange("p a f -> p (a f)"), identb[:, :],
                                     start=True, stop=True)
                last.then_inc(xT_ps, 1)

            transpose(0, 0)
            softmax_steps(pe, step)

            def both(body):
                with pe.Fori(0, NODE_HALF) as i:
                    body(i, 0)
                    body(i, 1)

            def sum_by_source():
                def step(i, c):
                    b = c % 2
                    n = 2 * i + c
                    pe.wait_ge(y_gathered[b], 16 * GJ * (nth(i, c) + 1))
                    pe.wait_ge(eq_done, n + 1)
                    if later(i, c, 2):
                        pe.wait_ge(comb_sb, n - 1)
                    for t in range(GJ):
                        for j in range(t, GJ):
                            last = pe.matmul(ps[3][:, 512 * b + t * F:512 * b + (t + 1) * F],
                                             eqm[b][:, EQ0[j] + t * P:EQ0[j] + (t + 1) * P], yg[b][:, j, :],
                                             start=j == t, stop=j == GJ - 1)
                    last.then_inc(comb_ps, 1)
                group_steps(pe, step)

            def sum_by_destination(k):
                base = SLOT_GROUPS * k
                typed = k == DST_PASSES - 1

                def turn(i, c):
                    if not inside(i, c, SLOT_GROUPS):
                        return
                    n = 2 * i + c
                    pe.wait_ge(zt_done, n + 1)
                    if later(i, c, 1):
                        pe.wait_ge(ztT_sb, n)
                    for j in range(SG):
                        last = pe.transpose(ps[0][:, j * P:(j + 1) * P], zt[c % 2][:, j * P:(j + 1) * P], ident)
                    last.then_inc(ztT_ps, 1)

                def messages(i, c):
                    if not inside(i, c, SLOT_GROUPS):
                        return
                    n = 2 * i + c
                    pe.wait_ge(ztT_sb, n + 1)
                    if later(i, c, 1):
                        pe.wait_ge(dsplit, 10 * i + 5 * (base + c))
                    for j in range(SG):
                        last = pe.matmul(ps[1][:, j * F:(j + 1) * F], ztT[:, j * P:(j + 1) * P],
                                         prm[:, A_EMB:A_EMB + F], start=True, stop=True)
                    last.then_inc(ym_ps, 1)

                def step(i, c):
                    b = c % 2
                    n = 2 * i + c
                    if typed:
                        turn(i, c + 2)
                        messages(i, c + 1)
                    pe.wait_ge(dsplit, 10 * i + 5 * (base + c + 1))
                    if later(i, c, 2) or k:
                        pe.wait_ge(acc_done, 2 * SG * i + SG * (base + c - 1) + ACC_ZEROS * (k + later(i, c, 2)))
                    for j in range(SG):
                        pe.wait_ge(oneh_done, 2 * SG * i + SG * (base + c) + j + 1)
                        for u in range(PACK):
                            for a in range(PARTS):
                                last = pe.matmul(ps[2 + b][:, j * P + u * F:j * P + (u + 1) * F],
                                                 oneh[b][j][:, u * P:(u + 1) * P], dp[b][:, a, j * F:(j + 1) * F],
                                                 start=a == 0, stop=a == PARTS - 1)
                        last.then_inc(slot_ps, 1)
                if typed:
                    turn(0, 0)
                    turn(0, 1)
                    messages(0, 0)
                steps(pe, step, 0, 2, SLOT_GROUPS - 2, SLOT_GROUPS)

            sum_by_source()

            def turn(i, c, g):
                if not inside(i, c, NODE_TILES):
                    return
                n = pack_count(i, c, g)
                par_ = n_par(c, g)
                if g == 0:
                    wait_loaded(pe, 1, i, c)
                if has_packs_before(i, c, g, 2):
                    pe.wait_ge(b_tsb, n - 1)
                pe.transpose(ps[0][:, 512 * par_:512 * par_ + P], ain[c % 2][:, g * P:(g + 1) * P],
                             ident).then_inc(b_tps, 1)

            def bilinear(i, c):
                for g in range(PACKS):
                    n = pack_count(i, c, g)
                    par_ = n_par(c, g)
                    turn(i, c + (g + 1) // PACKS, (g + 1) % PACKS)
                    pe.wait_ge(b_tsb, n + 1)
                    for k in range(PACK // 2):
                        if has_packs_before(i, c, g):
                            pe.wait_ge(b_read[k], n)
                        for s in range(2):
                            j = 2 * k + s
                            last = pe.matmul(bank_of(k)[:, 256 * s:256 * (s + 1)], sT[par_],
                                             wbk[j // 4][:, (j % 4) * 256:(j % 4 + 1) * 256], start=True, stop=True)
                        last.then_inc(b_ps, 1)

            turn(0, 0, 0)
            node_steps(pe, bilinear)
            sum_by_destination(0)

            def gin(q, i, c):
                n = NODE_TILES * q + 2 * i + c
                pe.wait_ge(g_y, n + 1)
                for g in range(PACKS):
                    last = pe.transpose(ps[0][:, g * P:(g + 1) * P], yy[:, g * P:(g + 1) * P], ident)
                last.then_inc(g_tps, 1)
                pe.wait_ge(g_tsb, n + 1)
                pe.matmul(ps[1][:, 0:512], bd[2 * q][:, :], yT[:, 0:512], start=True, stop=True)
                pe.matmul(ps[1][:, 512:W], bd[2 * q][:, :], yT[:, 512:W], start=True, stop=True).then_inc(g_hps, 1)
                pe.wait_ge(g_hsb, n + 1)
                if q or later(i, c, 1):
                    pe.wait_ge(g_o, n)
                for g in range(PACKS):
                    last = pe.matmul(ps[2][:, g * P:(g + 1) * P], hT[:, g * P:(g + 1) * P], bd[2 * q + 1][:, :],
                                     start=True, stop=True)
                last.then_inc(g_ops, 1)

            node_steps(pe, lambda i, c: gin(0, i, c))
            sum_by_destination(1)
            node_steps(pe, lambda i, c: gin(1, i, c))
            sum_by_destination(2)

            def gru(i, c):
                n = 2 * i + c
                wait_loaded(pe, 4, i, c)
                for k, t in ((0, ain), (1, rin)):
                    for g in range(PACKS):
                        last = pe.transpose(ps[k][:, g * P:(g + 1) * P], t[c][:, g * P:(g + 1) * P], ident)
                last.then_inc(u_tps, 1)
                pe.wait_ge(u_tsb, 2 * (n + 1))
                for g in range(PACKS):
                    bank = ps[2 + g // 2 % 2][:, 512 * (g % 2):512 * (g % 2 + 1)]
                    if g >= 4:
                        pe.wait_ge(u_g, PACKS * n + g - 3)
                    elif later(i, c, 1):
                        pe.wait_ge(u_g, PACKS * n + min(g - 2, 0))
                    pe.matmul(bank, mT[:, g * P:(g + 1) * P], bdg[0][:, :], start=True, stop=False)
                    pe.matmul(bank, yT[:, g * P:(g + 1) * P], bdg[1][:, :], start=False, stop=True).then_inc(u_ps, 1)

            node_steps(pe, gru)

        @block.vector
        def _(dve):
            dve.memset(zero[:, :], 0.0).then_inc(zero_made, 1)
            for b in range(2):
                dve.memset(mx[b][:, :, :], FAR).then_inc(first_made, 1)
            dve.memset(den[1][:, :, :], 0.0).then_inc(first_made, 1)
            dve.memset(num[1][:, :, :], 0.0).then_inc(first_made, 1)
            dve.wait_ge(first_made, 4)
            dve.wait_ge(cst_in, 96)
            dve.tensor_copy(io_f[:, :], node_of).then_inc(casts, 1)
            dve.tensor_copy(repsel[:, :], repf).then_inc(casts, 1)
            dve.tensor_copy(identb[:, :], ident).then_inc(casts, 1)
            dve.wait_ge(keys_in, 32)
            dve.tensor_tensor(kd, ka, kb, ALU.is_equal).then_inc(k_same, 1)
            dve.wait_ge(k_same, 1)
            dve.tensor_scalar(kt, kd, -1.0, -FAR, ALU.add, ALU.mult).then_inc(k_far, 1)
            dve.wait_ge(next_in, 32)
            dve.wait_ge(spare_made, 1)
            dve.tensor_tensor(kd, ka, kb, ALU.is_equal).then_inc(k_same, 1)
            dve.tensor_tensor(kt2, kspare, ka, ALU.subtract).then_inc(k_d, 1)
            dve.wait_ge(k_same, 2)
            dve.wait_ge(k_d, 1)
            dve.tensor_tensor(kt2, kt2, kd, ALU.mult).then_inc(k_m, 1)
            dve.wait_ge(k_m, 1)
            dve.tensor_tensor(ko, kt2, ka, ALU.add).then_inc(k_idx, 1)
            dve.wait_ge(first_in, 16)
            dve.wait_ge(counted, 2)
            dve.memset(ones, 1.0).then_inc(v_ones, 1)
            dve.tensor_copy(sl_s[:, :], sl_i[:, :]).then_inc(v_s, 1)
            dve.tensor_scalar(vrow, vrow, BLOCK.bit_length() - 1, None, ALU.logical_shift_right).then_inc(v_shift, 1)
            dve.wait_ge(v_shift, 1)
            dve.tensor_tensor(vsum, vrow, vcnt, ALU.add).then_inc(v_sum, 1)
            dve.wait_ge(v_sum, 1)
            dve.wait_ge(v_ones, 1)
            dve.wait_ge(v_s, 1)
            for q in range(SQ):
                dve.scalar_tensor_tensor(kjunk[q], vsum, sl_s[:, q:q + 1], ones, ALU.is_le, ALU.mult,
                                         accum_out=sl_n[:, q:q + 1]).then_inc(v_n, 1)
            dve.wait_ge(v_n, SQ)
            dve.tensor_scalar(sl_t[:, :], sl_n[:, :], -1.0, 0.0, ALU.add, ALU.max).then_inc(v_t, 1)
            dve.wait_ge(v_t, 1)
            dve.tensor_copy(sl_ti[:, :], sl_t[:, :]).then_inc(v_idx, 1)
            dve.tensor_tensor(sl_b[:, :], sl_s[:, :], sl_t[:, :], ALU.subtract).then_inc(v_b, 1)
            dve.wait_ge(v_b, 1)
            dve.tensor_scalar(sl_base[:, :], sl_b[:, :], float(BLOCKS), float(BLOCK), ALU.min, ALU.mult).then_inc(v_b, 1)
            dve.tensor_scalar(sl_off[:, :], sl_b[:, :], float(BLOCKS), float(P), ALU.min, ALU.mult).then_inc(v_off, 1)
            dve.wait_ge(v_turned, 1)
            dve.tensor_copy(sl_row[:, :], ps[3][0:SQ, 0:P]).then_inc(row_made, 1)
            dve.wait_ge(v_b, 2)
            dve.wait_ge(v_rows, 16 * 3 * SQ)
            for q in range(SQ):
                dve.tensor_copy(growf[0][q], grow[0][q].bitcast(I32)).then_inc(v_cast, 1)
                dve.tensor_scalar(growf[1][q], grow[1][q].bitcast(I32), sl_base[:, q:q + 1], None,
                                  ALU.subtract).then_inc(v_cast, 1)
                dve.tensor_copy(growf[2][q], grow[2][q].bitcast(I32)).then_inc(v_cast, 1)
            dve.wait_ge(v_turned, 4)
            dve.tensor_copy(srci, ps[1][:, 0:SN]).then_inc(slots_done, 1)
            dve.tensor_copy(rel[:, :], ps[1][:, 512:512 + SN]).then_inc(slots_done, 1)
            dve.tensor_copy(typ[:, :], ps[2][:, 0:SN]).then_inc(slots_done, 1)
            blk = cst[:, C_BLK:C_BLK + PACK]
            bmask = blk.unsqueeze(2).broadcast_to((P, PACK, F))
            for k, a in enumerate((A_W1A, A_W1B, A_W2A, A_W2B)):
                dve.tensor_tensor(bd[k][:, :].rearrange("p (j f) -> p j f", f=F),
                                  prm[:, a:a + F].unsqueeze(1).broadcast_to((P, PACK, F)), bmask,
                                  ALU.mult).then_inc(w_bias, 1)
            for k, a, cols in ((0, A_WIH, (0, 1, 2, None)), (1, A_WHH, (0, 1, None, 2))):
                for q, g in enumerate(cols):
                    o = bdg[k][:, q * P:(q + 1) * P]
                    if g is None:
                        dve.memset(o, 0.0).then_inc(w_bias, 1)
                    else:
                        dve.tensor_tensor(o.rearrange("p (j f) -> p j f", f=F),
                                          prm[:, a + g * F:a + (g + 1) * F].unsqueeze(1).broadcast_to((P, PACK, F)),
                                          bmask, ALU.mult).then_inc(w_bias, 1)
            WEIGHTS_MADE = 16
            flatg = bgate[:, :, :].rearrange("p a b -> p (a b)")
            dve.tensor_tensor(flatg[:, 0:32], prm[:, A_BIH:A_BIH + 32], prm[:, A_BHH:A_BHH + 32],
                              ALU.add).then_inc(w_bias, 1)
            dve.tensor_copy(flatg[:, 32:48], prm[:, A_BIH + 32:A_BIH + 48]).then_inc(w_bias, 1)
            dve.tensor_copy(flatg[:, 48:64], prm[:, A_BHH + 32:A_BHH + 48]).then_inc(w_bias, 1)
            dve.tensor_scalar(prm[:, A_EPS1:A_EPS1 + 2], prm[:, A_EPS1:A_EPS1 + 2], 1.0, None,
                              ALU.add).then_inc(w_bias, 1)
            dve.wait_ge(w_tp, 1)
            for j in range(PACK):
                o = wbk[j // 4][:, (j % 4) * 256:(j % 4 + 1) * 256]
                dve.tensor_scalar(o, ps[0][:, 0:256], blk[:, j:j + 1], None, ALU.mult).then_inc(w_made, 1)
            dve.wait_ge(w_bias, WEIGHTS_MADE)

            def split(i, c):
                if not inside(i, c, TILES):
                    return
                n = 2 * i + c
                rows_, part = xg[c % 2], lambda a: xp[:, :, a, :]
                dve.wait_ge(x_gathered[c % 2], 16 * SUB * (nth(i, c) + 1))
                if later(i, c, 1):
                    dve.wait_ge(xT_ps, n)
                dve.tensor_copy(part(0), rows_[:, :, :]).then_inc(split_done, 1)
                dve.wait_ge(split_done, 5 * n + 1)
                dve.tensor_tensor(xr[0][:, :, :], rows_[:, :, :], part(0), ALU.subtract).then_inc(split_done, 1)
                dve.wait_ge(split_done, 5 * n + 2)
                dve.tensor_copy(part(1), xr[0][:, :, :]).then_inc(split_done, 1)
                dve.wait_ge(split_done, 5 * n + 3)
                dve.tensor_tensor(xr[1][:, :, :], xr[0][:, :, :], part(1), ALU.subtract).then_inc(split_done, 1)
                dve.wait_ge(split_done, 5 * n + 4)
                dve.tensor_copy(part(2), xr[1][:, :, :]).then_inc(split_done, 1)

            def step(i, c):
                n = 2 * i + c
                b = c % 2
                split(i, c + 1)
                if inside(i, c, TILES):
                    dve.wait_ge(h_sb, n + 1)
                    dve.wait_ge(wa_ps, n + 1)
                    dve.tensor_tensor(e2f, ps[0][:, :], flat(hS), ALU.mult).then_inc(e2_done, 1)
                    dve.wait_ge(main_in[b], 32 * (nth(i, c) + 1))
                    if later(i, c, 1):
                        dve.tensor_copy(mx[b][:, :, 0:1], mx[1 - b][:, :, ET:ET + 1]).then_inc(m_first, 1)
                        dve.wait_ge(m_first, n)
                    dve.wait_ge(e2_done, n + 1)
                    for h in range(CH):
                        last = dve.tensor_tensor_scan(mx[b][:, h, 1:ET + 1], far[b][:, :], e2f[:, h * ET:(h + 1) * ET],
                                                      mx[b][:, h, 0:1], ALU.add, ALU.max)
                    last.then_inc(m_done, 1)
                    dve.wait_ge(m_done, n + 1)
                    dve.tensor_tensor(uu[b][:, :, :], e2f.rearrange("p (h e) -> p h e", h=CH),
                                      mx[b][:, :, 1:ET + 1], ALU.subtract).then_inc(u_done, 1)
                    dve.wait_ge(wm_ps, n + 1)
                    dve.tensor_tensor(flat(e1[b]), ps[1][:, :], flat(hS), ALU.mult).then_inc(e1_done, 1)
                    dve.wait_ge(mfar_done, n + 1)
                    dve.tensor_tensor(dd[b][:, :, :], mfar[:, :, :], mx[b][:, :, 1:ET + 1],
                                      ALU.subtract).then_inc(d_done, 1)
                if inside(i, c - 1, TILES):
                    m = n - 1
                    o = 1 - b
                    dve.wait_ge(p_done, m + 1)
                    if later(i, c - 1, 1):
                        dve.wait_ge(num_done, m)
                    dve.tensor_tensor(qq[:, :, :], uu[o][:, :, :], e1[o][:, :, :], ALU.mult).then_inc(q_done, 1)
                    dve.wait_ge(c_done, m + 1)
                    for h in range(CH):
                        last = dve.tensor_tensor_scan(den[o][:, h, :], dd[o][:, h, :], uu[o][:, h, :],
                                                      den[1 - o][:, h, ET - 1:ET], ALU.mult, ALU.add)
                    last.then_inc(den_done, 1)
                    dve.wait_ge(q_done, m + 1)
                    for h in range(CH):
                        last = dve.tensor_tensor_scan(num[o][:, h, :], dd[o][:, h, :], qq[:, h, :],
                                                      num[1 - o][:, h, ET - 1:ET], ALU.mult, ALU.add)
                    last.then_inc(num_done, 1)
                if inside(i, c - 2, TILES):
                    m = n - 2
                    dve.wait_ge(inv_done, m + 1)
                    if later(i, c - 2, 2):
                        dve.wait_ge(ft_ps, m - 1)
                    dve.wait_ge(num_done, m + 1)
                    dve.tensor_tensor(rat[b][:, :, :], num[b][:, :, :], inv[:, :, :], ALU.mult).then_inc(rat_done, 1)

            split(0, 0)
            softmax_steps(dve, step)

            def both(body):
                with dve.Fori(0, NODE_HALF) as i:
                    body(i, 0)
                    body(i, 1)

            slots = lambda t: t.rearrange("p (k f) -> p k f", f=F)
            over = lambda t: t.unsqueeze(2).broadcast_to((P, SLOTS, F))

            def wait_yout(ph, i, c):
                if ph or later(i, c, 2):
                    dve.wait_ge(stored[c], i * 16 + 16 * NODE_HALF * ph)

            def norm(ph, n_norm, i, c, v, between=()):
                n = NODE_TILES * n_norm + 2 * i + c
                dve.wait_ge(v_done, n + 1)
                dve.tensor_reduce(st[:, 0, :], slots(v), AX, ALU.add).then_inc(s_sum, 1)
                dve.wait_ge(s_sum, n + 1)
                dve.scalar_tensor_tensor(slots(xm[:, :]), over(st[:, 0, :]), -1.0 / F, slots(v),
                                         ALU.mult, ALU.add).then_inc(s_xm, 1)
                if between:
                    between[0]()
                dve.wait_ge(s_sq, n + 1)
                dve.tensor_reduce(st[:, 1, :], slots(sq[:, :]), AX, ALU.add).then_inc(s_vs, 1)
                dve.wait_ge(s_vs, n + 1)
                dve.tensor_scalar(st[:, 2, :], st[:, 1, :], 1.0 / F, EPS, ALU.mult, ALU.add).then_inc(s_ve, 1)
                if between:
                    between[1]()
                dve.wait_ge(s_sd, n + 1)
                dve.reciprocal(st[:, 3, :], st[:, 3, :]).then_inc(s_rs, 1)
                dve.wait_ge(s_rs, n + 1)
                wait_yout(ph, i, c)
                dve.tensor_tensor(slots(yout[c][:, :]), slots(xm[:, :]), over(st[:, 3, :]),
                                  ALU.mult).then_inc(y_done, 1)

            def sum_by_source():
                tri = cst[:, C_TRI:C_TRI + G]

                def step(i, c):
                    b = c % 2
                    n = 2 * i + c
                    dve.wait_ge(sum_in[b], 48 * (nth(i, c) + 1))
                    dve.tensor_copy(kcf[b][:, :], kcol[b][:, :]).then_inc(kcf_done, 1)
                    dve.wait_ge(kcf_done, n + 1)
                    if later(i, c, 2):
                        dve.wait_ge(comb_ps, n - 1)
                    for j in range(GJ):
                        w = P * (j + 1)
                        last = dve.scalar_tensor_tensor(eqm[b][:, EQ0[j]:EQ0[j] + w], krow[b][:, 0:w],
                                                        kcf[b][:, j:j + 1], tri[:, G - w:G], ALU.is_equal, ALU.mult,
                                                        accum_out=cnt[b][:, j:j + 1])
                    last.then_inc(eq_done, 1)
                    dve.tensor_tensor(kdf[:, :], cst[:, C_TRASH:C_TRASH + GJ], kcf[b][:, :],
                                      ALU.subtract).then_inc(kdf_done, 1)
                    dve.wait_ge(eq_done, n + 1)
                    dve.wait_ge(kdf_done, n + 1)
                    dve.scalar_tensor_tensor(kmd[:, :], cnt[b][:, :], 1.5, kdf[:, :], ALU.is_gt,
                                             ALU.mult).then_inc(kmd_done, 1)
                    dve.wait_ge(kmd_done, n + 1)
                    if later(i, c, 2):
                        dve.wait_ge(added, 16 * GJ * (n - 1))
                    dve.tensor_tensor(sidx[b][:, :], kmd[:, :], kcf[b][:, :], ALU.add).then_inc(sidx_done, 1)
                group_steps(dve, step)

            def sum_by_destination(k):
                base = SLOT_GROUPS * k
                typed = k == DST_PASSES - 1
                iota = cst[:, C_IOTA:C_IOTA + TYPES].unsqueeze(2).broadcast_to((P, TYPES, F))
                dve.memset(acc, 0.0).then_inc(acc_done, ACC_ZEROS)

                def place(i, c):
                    if not inside(i, c, SLOT_GROUPS):
                        return
                    b = c % 2
                    n = 2 * i + c
                    dve.wait_ge(d_gathered[b], 16 * SG * i + 16 * SG * (base // 2 + c // 2 + 1))
                    if later(i, c, 2):
                        dve.wait_ge(ztT_ps, n - 1)
                    for j in range(SG):
                        last = dve.scalar_tensor_tensor(
                            zt[b][:, j * P:(j + 1) * P].rearrange("p (k f) -> p k f", f=F), iota,
                            typ[:, bass.ds(n * SG + j, 1)], dy[b][:, j, :].unsqueeze(1).broadcast_to((P, TYPES, F)),
                            ALU.is_equal, ALU.mult)
                    last.then_inc(zt_done, 1)

                def split(i, c):
                    b = c % 2
                    at = lambda d: 10 * i + 5 * (base + c) + d
                    if typed:
                        dve.wait_ge(ym_ps, 2 * i + c + 1)
                        rows_ = ps[1][:, 0:SG * F]
                    else:
                        dve.wait_ge(d_gathered[b], 16 * SG * i + 16 * SG * (base // 2 + c // 2 + 1))
                        rows_ = dy[b][:, :, :].rearrange("p j f -> p (j f)")
                    if later(i, c, 2) or k:
                        dve.wait_ge(slot_ps, 2 * SG * i + SG * (base + c - 1))
                    dve.tensor_copy(dp[b][:, 0, :], rows_).then_inc(dsplit, 1)
                    dve.wait_ge(dsplit, at(1))
                    dve.tensor_tensor(dr[0][:, :], rows_, dp[b][:, 0, :], ALU.subtract).then_inc(dsplit, 1)
                    dve.wait_ge(dsplit, at(2))
                    dve.tensor_copy(dp[b][:, 1, :], dr[0][:, :]).then_inc(dsplit, 1)
                    dve.wait_ge(dsplit, at(3))
                    dve.tensor_tensor(dr[1][:, :], dr[0][:, :], dp[b][:, 1, :], ALU.subtract).then_inc(dsplit, 1)
                    dve.wait_ge(dsplit, at(4))
                    dve.tensor_copy(dp[b][:, 2, :], dr[1][:, :]).then_inc(dsplit, 1)

                def load_offsets(i, c):
                    _, at = nc.values_load_multi_w_load_instructions(
                        offs[0:1, bass.ds((2 * i + c) * SG, SG)], engines=[mybir.EngineType.DVE], min_val=0,
                        max_val=BLOCKS * P,
                        skip_runtime_bounds_check_because="the offsets are clipped where they are made")
                    return at

                def collect(i, c, j, at):
                    s_ = 2 * SG * i + SG * (base + c) + j
                    if j % 4 == 0:
                        dve.wait_ge(slot_ps, s_ + 4)
                    dve.wait_ge(acc_done, s_ + ACC_ZEROS * (k + 1))
                    o = acc[:, bass.ds(at, P)]
                    dve.tensor_tensor(o, o, ps[2 + c % 2][:, j * P:(j + 1) * P], ALU.add).then_inc(acc_done, 1)

                def step(i, c):
                    b = c % 2
                    n = 2 * i + c
                    if typed:
                        place(i, c + 2)
                    split(i, c)
                    before = inside(i, c - 1, SLOT_GROUPS)
                    if before:
                        at = load_offsets(i, c - 1)
                    for j in range(SG):
                        dve.tensor_scalar(oneh[b][j], io_f[:, :], rel[:, bass.ds(n * SG + j, 1)], None,
                                          ALU.is_equal).then_inc(oneh_done, 1)
                        if before:
                            collect(i, c - 1, j, at[j])

                if typed:
                    place(0, 0)
                    place(0, 1)
                if k == 0:
                    dve.wait_ge(offs_in, 16)
                steps(dve, step, 0, 2, SLOT_GROUPS - 2, SLOT_GROUPS)
                at = load_offsets(0, SLOT_GROUPS - 1)
                for j in range(SG):
                    collect(0, SLOT_GROUPS - 1, j, at[j])

            def first(i, c):
                wait_loaded(dve, 0, i, c)
                dve.tensor_tensor(vv[:, :], xin[c][:, :], ain[c][:, :], ALU.add).then_inc(v_done, 1)
                norm(0, 0, i, c, vv[:, :])
            node_steps(dve, first)
            sum_by_source()

            def first_pair(i, c, g):
                if not inside(i, c, NODE_TILES):
                    return
                n = pack_count(i, c, g)
                if g == 0:
                    wait_loaded(dve, 1, i, c)
                dve.wait_ge(b_ps, 4 * n + 1)
                if has_packs_before(i, c, g, 2):
                    dve.wait_ge(b_z, 4 * (n - 2) + 1)
                multiply(dve, prod[n_par(c, g)], bank_of(0), xin[c % 2][:, :], g, 0).then_inc(b_read[0], 1)

            def bilinear_pack(i, c, g):
                if not inside(i, c, NODE_TILES):
                    return
                n = pack_count(i, c, g)
                first_pair(i, c + (g + 1) // PACKS, (g + 1) % PACKS)
                for k in range(PACK // 2):
                    if k == 0:
                        dve.wait_ge(b_read[0], n + 1)
                    else:
                        dve.wait_ge(b_pool, 3 * n + k)
                    s0 = g * PACK + 2 * k
                    dve.tensor_reduce(slots(zz)[:, s0:s0 + 2, :],
                                      ([prod[n_par(c, g)]] + pool_prod)[k].rearrange("p (s u w) -> p s w u", s=2, u=F),
                                      AX, ALU.add).then_inc(b_z, 1)

            def bilinear(i, c):
                for g in range(2, PACKS):
                    bilinear_pack(i, c, g)
                m = 2 * i + c
                dve.wait_ge(b_z, 4 * PACKS * (m + 1))
                dve.tensor_tensor(slots(zz), slots(zz),
                                  prm[:, A_BTP:A_BTP + F].unsqueeze(1).broadcast_to((P, SLOTS, F)),
                                  ALU.add).then_inc(b_zb, 1)
                dve.wait_ge(b_zb, m + 1)
                dve.tensor_tensor(vv[:, :], zz, xin[c][:, :], ALU.add).then_inc(v_done, 1)
                norm(1, 1, i, c, vv[:, :], [lambda g=g: bilinear_pack(i, c + 1, g) for g in range(2)])
            first_pair(0, 0, 0)
            bilinear_pack(0, 0, 0)
            bilinear_pack(0, 0, 1)
            node_steps(dve, bilinear)
            sum_by_destination(0)

            def gin_ahead(q, ph, i, c):
                if not inside(i, c, NODE_TILES):
                    return
                n = NODE_TILES * q + 2 * i + c
                wait_loaded(dve, ph, i, c)
                if q or later(i, c, 1):
                    dve.wait_ge(g_tps, n)
                dve.scalar_tensor_tensor(yy, xin[c % 2][:, :], prm[:, A_EPS1 + q:A_EPS1 + q + 1], ain[c % 2][:, :],
                                         ALU.mult, ALU.add).then_inc(g_y, 1)

            def gin(q, ph, i, c, dst):
                n = NODE_TILES * q + 2 * i + c
                dve.wait_ge(g_ops, n + 1)
                dve.wait_ge(y_done, node_count(ph, i, c))
                a = A_B1B + F * q
                dve.tensor_tensor(slots(dst), slots(ps[2][:, 0:W]),
                                  prm[:, a:a + F].unsqueeze(1).broadcast_to((P, SLOTS, F)),
                                  ALU.add).then_inc(g_o, 1)
                dve.wait_ge(g_o, n + 1)

            def gin_first(i, c):
                gin_ahead(0, 2, i, c + 1)
                gin(0, 2, i, c, zz)
                wait_yout(2, i, c)
                dve.tensor_scalar(yout[c][:, :], zz, 0.0, None, ALU.max).then_inc(y_done, 1)
            gin_ahead(0, 2, 0, 0)
            node_steps(dve, gin_first)
            sum_by_destination(1)

            def gin_second(i, c):
                gin(1, 3, i, c, zz)
                n = 2 * i + c
                dve.tensor_reduce(st[:, 4, :], slots(zz), AX, ALU.max).then_inc(l_max, 1)
                dve.wait_ge(l_max, n + 1)
                dve.tensor_tensor(slots(zc), slots(zz), over(st[:, 4, :]), ALU.subtract).then_inc(l_zc, 1)
                gin_ahead(1, 3, i, c + 1)
                dve.wait_ge(l_ex, n + 1)
                dve.tensor_reduce(st[:, 4, :], slots(ex), AX, ALU.add).then_inc(l_se, 1)
                dve.wait_ge(l_zc, n + 1)
                wait_late(dve, 3, i, c)
                dve.tensor_tensor(vv[:, :], zc, rin[c][:, :], ALU.add).then_inc(l_t, 1)
                dve.wait_ge(l_ln, n + 1)
                dve.wait_ge(l_t, n + 1)
                dve.tensor_tensor(slots(vv[:, :]), slots(vv[:, :]), over(st[:, 5, :]),
                                  ALU.subtract).then_inc(v_done, 1)
                norm(3, 2, i, c, vv[:, :])
            gin_ahead(1, 3, 0, 0)
            node_steps(dve, gin_second)
            sum_by_destination(2)

            def gru(i, c):
                n = 2 * i + c
                gates_ahead(i, c + 1, range(PACKS // 2 + 1))
                dve.wait_ge(u_sig, 2 * (n + 1))
                dve.wait_ge(u_g, PACKS * (n + 1))
                dve.tensor_tensor(rh, gates[c][0], gates[c][3], ALU.mult).then_inc(u_rh, 1)
                dve.wait_ge(u_rh, n + 1)
                dve.tensor_tensor(gates[c][2], rh, gates[c][2], ALU.add).then_inc(u_in, 1)
                gates_ahead(i, c + 1, range(PACKS // 2 + 1, PACKS))
                dve.wait_ge(u_n, n + 1)
                wait_late(dve, 4, i, c)
                dve.tensor_tensor(zx, xin[c][:, :], nn, ALU.subtract).then_inc(u_zx, 1)
                dve.wait_ge(u_zx, n + 1)
                dve.tensor_tensor(rh, zx, gates[c][1], ALU.mult).then_inc(u_zd, 1)
                dve.tensor_tensor(vv[:, :], nn, xin[c][:, :], ALU.add).then_inc(l_t, 1)
                dve.wait_ge(u_zd, n + 1)
                dve.wait_ge(l_t, NODE_TILES + n + 1)
                dve.tensor_tensor(vv[:, :], vv[:, :], rh, ALU.add).then_inc(v_done, 1)
                norm(4, 3, i, c, vv[:, :])

            def gates_ahead(i, c, packs):
                if not inside(i, c, NODE_TILES):
                    return
                n = 2 * i + c
                wait_loaded(dve, 4, i, c)
                for g in packs:
                    bank = ps[2 + g // 2 % 2][:, 512 * (g % 2):512 * (g % 2 + 1)].rearrange("p (a j f) -> p a j f", a=4, f=F)
                    dve.wait_ge(u_ps, PACKS * n + g + 1)
                    for a in range(4):
                        last = dve.tensor_tensor(gates[c % 2][a][:, g * P:(g + 1) * P].rearrange("p (j f) -> p j f", f=F),
                                                 bank[:, a], bgate[:, a, :].unsqueeze(1).broadcast_to((P, PACK, F)),
                                                 ALU.add)
                    last.then_inc(u_g, 1)

            gates_ahead(0, 0, range(PACKS))
            node_steps(dve, gru)


def kernel(**inputs):
    import numpy as np
    import concourse.bacc as bacc
    from concourse.bass_utils import run_bass_kernel_spmd

    a = {k: np.asarray(v) for k, v in inputs.items()}

    def padded(v, n, fill):
        return np.concatenate([v, np.full((n - len(v),) + v.shape[1:], fill, v.dtype)])

    def edge_tiles(v):
        return np.ascontiguousarray(v.reshape(COLS, P).T)

    tiled = lambda w: np.tile(w, (PACK, 1))
    on_all = lambda v: np.tile(v.reshape(1, -1), (P, 1))
    src, dst = padded(a["src"], EP, N_NODES), padded(a["dst"], EP, N_NODES)
    none = np.full((1,), NP, dst.dtype)
    p = np.arange(P)
    const = np.zeros((P, C_N), np.float32)
    const[:, C_ID:C_ID + P] = np.eye(P)
    const[:, C_TRI:C_TRI + G] = np.arange(G)[None] - (G - P) <= p[:, None]
    const[:, C_BLK:C_BLK + PACK] = p[:, None] // F == np.arange(PACK)[None]
    const[:, C_TRASH:C_TRASH + GJ] = NP + np.arange(GJ)[None] * P + p[:, None]
    const[:, C_IOTA:C_IOTA + TYPES] = np.arange(TYPES)[None]
    const[:, C_SELO:C_SELO + F] = p[:, None] % F == np.arange(F)[None]
    block_node = np.tile((PACK * p[None, :] + np.arange(PACK, dtype=np.float32)[:, None]).reshape(1, -1), (P, 1))
    rep = np.zeros((F, CH, P), np.float32)
    for h in range(CH):
        rep[PACK * h + p // F, h, p] = 1.0
    par = np.concatenate([
        on_all(a["L1_gnn_bias"]), on_all(a["L2_gnn_b1b"]), on_all(a["L2_gnn_b2b"]),
        on_all(a["L3_gnn_b_ih"]), on_all(a["L3_gnn_b_hh"]),
        np.tile(a["L2_gnn_b1a"], PACK)[:, None], np.tile(a["L2_gnn_b2a"], PACK)[:, None],
        on_all(a["L2_gnn_eps1"]), on_all(a["L2_gnn_eps2"]),
        tiled(a["L2_gnn_w1a"]), tiled(a["L2_gnn_w1b"]), tiled(a["L2_gnn_w2a"]), tiled(a["L2_gnn_w2b"]),
        tiled(a["L3_gnn_w_ih"].T), tiled(a["L3_gnn_w_hh"].T),
        a["L3_gnn_edge_emb"].reshape(TYPES, F, F).transpose(0, 2, 1).reshape(P, F),
    ], axis=1)
    wtp = np.tile(a["L1_gnn_W_tp"].transpose(2, 0, 1)[:, :, None, :], (1, 1, PACK, 1)).reshape(F, F * P)
    par16 = np.concatenate([a["L1_gnn_weight"].T, wtp], axis=1)
    arrays = {
        "x": padded(a["x"], NP, 0),
        "ef": np.concatenate([padded(a["edge_attr_16"], EP, 0).T, np.ones((1, EP), np.float32)]),
        "wlog": np.concatenate([np.concatenate([a["L0_gnn_W_attn"], a["L0_gnn_W_msg"]], axis=1),
                                np.concatenate([a["L0_gnn_b_attn"], a["L0_gnn_b_msg"]])[None]]),
        "repcon": np.tile(rep.reshape(F, CH * P), (PARTS, 1)),
        "src_t": edge_tiles(src), "dst_t": edge_tiles(dst),
        "next_t": edge_tiles(np.concatenate([dst[1:], none])),
        "src_row": src, "dst_row": dst, "prev_row": np.concatenate([none, dst[:-1]]),
        "type_row": padded(a["edge_type_8"], EP, 0), "first_row": dst[::P],
        "const": const, "par": par, "par16": par16, "block_node": block_node.astype(np.float32),
    }
    arrays = {k: np.ascontiguousarray(v) for k, v in arrays.items()}
    nc = bacc.Bacc("TRN2", target_bir_lowering=False, num_devices=1)
    args = [nc.dram_tensor(f"in_{k}", v.shape, mybir.dt.from_np(v.dtype), kind="ExternalInput").ap()
            for k, v in arrays.items()]
    out = nc.dram_tensor("out_x", (NP, F), FP32, kind="ExternalOutput").ap()
    build_program(nc, *args, out)
    r = run_bass_kernel_spmd(nc, [{f"in_{k}": v for k, v in arrays.items()}], core_ids=[0])
    return r.results[0]["out_x"][:N_NODES]
```
